# Optimizing a Trainium2 kernel written in Bass

```python
import numpy as np
import jax
import jax.numpy as jnp

def _softmax(x, axis=-1):
    return jax.nn.softmax(x, axis=axis)

def _gelu(x):
    return jax.nn.gelu(x, approximate=True)

def _silu(x):
    return jax.nn.silu(x)

def _sigmoid(x):
    return jax.nn.sigmoid(x)

def _layernorm(x, axis=-1, eps=1e-05):
    m = jnp.mean(x, axis=axis, keepdims=True)
    v = jnp.var(x, axis=axis, keepdims=True)
    return (x - m) / jnp.sqrt(v + eps)

def _scatter_add(tgt, idx, src, axis=0):
    return tgt.at[idx].add(src)

def _segment_sum(src, seg, n):
    return jax.ops.segment_sum(src, seg, n)
kernel_name = 'mk_gnn_resnorm_d4_gnn_r8_2e389d'

def setup_inputs(seed: int=0):
    np.random.seed(seed)
    _w = jnp.asarray

    def _rec_inputs():
        import jax
        import jax.numpy as jnp
        _gk = jax.random.key(seed)
        x = -0.0005121 + 1.001 * jax.random.normal(jax.random.fold_in(_gk, 1), (12500, 32), jnp.float32)
        src = jax.random.randint(jax.random.fold_in(_gk, 2), (200000,), 0, 12500, jnp.int32)
        dst = jnp.minimum((12500 * jax.random.uniform(jax.random.fold_in(_gk, 3), (200000,)) ** 2.0).astype(jnp.int32), 99999)
        _o = jnp.argsort(dst, stable=True)
        src = src[_o]
        dst = dst[_o]
        edge_attr_10 = jax.random.uniform(jax.random.fold_in(_gk, 12), (200000, 10), jnp.float32, 0.0, 1)
        edge_attr_3 = 0.000549083 + 1.00031 * jax.random.normal(jax.random.fold_in(_gk, 13), (200000, 3), jnp.float32)
        edge_attr_5 = -0.000325185 + 1.00005 * jax.random.normal(jax.random.fold_in(_gk, 14), (200000, 5), jnp.float32)
        edge_weight = jax.random.uniform(jax.random.fold_in(_gk, 16), (200000,), jnp.float32, 0.0, 0.999997)
        edge_weight1 = 0.000452788 + 0.999756 * jax.random.normal(jax.random.fold_in(_gk, 17), (200000, 1), jnp.float32)
        return (x, src, dst, edge_attr_10, edge_attr_3, edge_attr_5, edge_weight, edge_weight1)
    x, src, dst, edge_attr_10, edge_attr_3, edge_attr_5, edge_weight, edge_weight1 = _rec_inputs()

    def _L0_gnn_setup():
        import jax, jax.numpy as jnp
        import numpy as np
        import math
        M = 8
        COMBOS = [(0, 0, 0), (0, 1, 1), (1, 0, 1), (1, 1, 0), (1, 1, 1), (2, 1, 1)]

        def _cg_coeff(j1, m1, j2, m2, j3, m3):
            if m3 != m1 + m2:
                return 0.0
            f = math.factorial
            vmin = max(0, j2 - j3 - m1, j1 + m2 - j3)
            vmax = min(j1 + j2 - j3, j1 - m1, j2 + m2)
            pref = (2 * j3 + 1) * f(j3 + j1 - j2) * f(j3 - j1 + j2) * f(j1 + j2 - j3) / f(j1 + j2 + j3 + 1)
            pref *= f(j3 + m3) * f(j3 - m3) * f(j1 - m1) * f(j1 + m1) * f(j2 - m2) * f(j2 + m2)
            s = 0.0
            for v in range(vmin, vmax + 1):
                s += (-1) ** v / (f(v) * f(j1 + j2 - j3 - v) * f(j1 - m1 - v) * f(j2 + m2 - v) * f(j3 - j2 + m1 + v) * f(j3 - j1 - m2 + v))
            return math.sqrt(pref) * s

        def _su2_cg(l1, l2, l3):
            C = np.zeros((2 * l1 + 1, 2 * l2 + 1, 2 * l3 + 1), dtype=np.complex128)
            for m1 in range(-l1, l1 + 1):
                for m2 in range(-l2, l2 + 1):
                    m3 = m1 + m2
                    if -l3 <= m3 <= l3:
                        C[m1 + l1, m2 + l2, m3 + l3] = _cg_coeff(l1, m1, l2, m2, l3, m3)
            return C

        def _qmat(l):
            q = np.zeros((2 * l + 1, 2 * l + 1), dtype=np.complex128)
            for m in range(-l, 0):
                q[l + m, l + abs(m)] = 1 / np.sqrt(2)
                q[l + m, l - abs(m)] = -1j / np.sqrt(2)
            q[l, l] = 1.0
            for m in range(1, l + 1):
                q[l + m, l + abs(m)] = (-1) ** m / np.sqrt(2)
                q[l + m, l - abs(m)] = 1j * (-1) ** m / np.sqrt(2)
            return (-1j) ** l * q

        def _so3_cg(l1, l2, l3):
            C = np.einsum('ij,kl,mn,ikn->jlm', _qmat(l1), _qmat(l2), np.conj(_qmat(l3)).T, _su2_cg(l1, l2, l3))
            assert np.abs(C.imag).max() < 1e-06
            C = C.real
            return C / np.linalg.norm(C)
        CG = {c: jnp.asarray(_so3_cg(*c), dtype=jnp.float32) for c in COMBOS}
        N, E = (12500, 200000)
        ks = jax.random.split(jax.random.key(seed), 6)
        return {'node_irreps': jax.random.normal(ks[0], (N, 4 * M), jnp.float32), 'edge_index': jax.random.randint(ks[1], (2, E), 0, N, dtype=jnp.int32), 'sh0': jax.random.normal(ks[2], (E, 1), jnp.float32), 'sh1': jax.random.normal(ks[3], (E, 3), jnp.float32), 'sh2': jax.random.normal(ks[4], (E, 5), jnp.float32), 'W': jax.random.normal(ks[5], (len(COMBOS), M, M), jnp.float32)}
    _L0_gnn_all = _L0_gnn_setup()
    _L0_gnn_in = {k: v for k, v in _L0_gnn_all.items() if k in ('W',)}
    del _L0_gnn_all

    def _L1_gnn_setup():
        import jax, jax.numpy as jnp
        import numpy as np
        N, E, D, K, H = (12500, 200000, 32, 3, 1)

        def _cheb(src, dst, feat, lam, W, b, n):
            deg = jnp.clip(jax.ops.segment_sum(jnp.ones(src.shape[0], feat.dtype), dst, num_segments=n), 1.0)
            dinv = deg[:, None] ** (-0.5)
            re_norm = 2.0 / lam[0]

            def unnL(f):
                return jax.ops.segment_sum((f * dinv)[src], dst, num_segments=n) * dinv
            X0 = feat
            X1 = -re_norm * unnL(X0) + X0 * (re_norm - 1.0)
            Xs = [X0, X1]
            for _ in range(2, K):
                Xi = -2.0 * re_norm * unnL(X1) + X1 * (2.0 * (re_norm - 1.0)) - X0
                Xs.append(Xi)
                X0, X1 = (X1, Xi)
            return jax.nn.leaky_relu(jnp.concatenate(Xs, axis=1) @ W + b, 0.01)

        def _gatv2(src, dst, h, Ws, bs, Wd, bd, attn, n):
            Hh, Dd = attn.shape
            fs = (h @ Ws + bs).reshape(n, Hh, Dd)
            fd = (h @ Wd + bd).reshape(n, Hh, Dd)
            e = jax.nn.leaky_relu(fs[src] + fd[dst], 0.2)
            logits = jnp.einsum('ehd,hd->eh', e, attn)
            m = jax.ops.segment_max(logits, dst, num_segments=n)
            ex = jnp.exp(logits - m[dst])
            a = ex / jax.ops.segment_sum(ex, dst, num_segments=n)[dst]
            ft = jax.ops.segment_sum(fs[src] * a[..., None], dst, num_segments=n)
            return jax.nn.leaky_relu(ft, 0.01)
        key = jax.random.key(seed)
        ks = jax.random.split(key, 7)
        return {'src': jax.random.randint(ks[0], (E,), 0, N), 'dst': jax.random.randint(ks[1], (E,), 0, N), 'embedding': jax.random.normal(ks[2], (N, D), jnp.float32), 'lambda_max': jnp.full((1,), 2.0, jnp.float32), 'cheb_W': jax.random.normal(ks[3], (K * D, D), jnp.float32) / np.sqrt(K * D), 'cheb_b': jnp.zeros((D,), jnp.float32), 'gat_W_src': jax.random.normal(ks[4], (D, H * D), jnp.float32) / np.sqrt(D), 'gat_b_src': jnp.zeros((H * D,), jnp.float32), 'gat_W_dst': jax.random.normal(ks[5], (D, H * D), jnp.float32) / np.sqrt(D), 'gat_b_dst': jnp.zeros((H * D,), jnp.float32), 'gat_attn': jax.random.normal(ks[6], (H, D), jnp.float32) / np.sqrt(D)}
    _L1_gnn_all = _L1_gnn_setup()
    _L1_gnn_in = {k: v for k, v in _L1_gnn_all.items() if k in ('lambda_max', 'cheb_W', 'cheb_b', 'gat_W_src', 'gat_b_src', 'gat_W_dst', 'gat_b_dst', 'gat_attn')}
    del _L1_gnn_all

    def _L2_gnn_setup():
        import jax, jax.numpy as jnp
        import numpy as np
        MUL = 16
        MOUT = 8
        TANH_GAIN = 1.593
        INV_SQRT3 = 0.5773502691896258
        PW_S = 0.17677669529663687
        PW_V = 0.25

        def _w3j_121():
            s2, s6 = (2 ** 0.5, 6 ** 0.5)
            M = np.zeros((5, 3, 3))
            M[0, 0, 1] = M[0, 1, 0] = 1 / s2
            M[1, 1, 2] = M[1, 2, 1] = 1 / s2
            M[2] = np.diag([-1.0, -1.0, 2.0]) / s6
            M[3, 0, 2] = M[3, 2, 0] = 1 / s2
            M[4] = np.diag([1.0, -1.0, 0.0]) / s2
            return jnp.asarray(np.transpose(M, (1, 0, 2)) / 5 ** 0.5, jnp.float32)
        W3J121 = _w3j_121()

        def _sph(edge_vec):
            n = edge_vec / jnp.linalg.norm(edge_vec, axis=1, keepdims=True)
            x, y, z = (n[:, 0], n[:, 1], n[:, 2])
            y1 = 3.0 ** 0.5 * n
            s15 = 15.0 ** 0.5
            y2 = jnp.stack([s15 * x * y, s15 * y * z, 5.0 ** 0.5 / 2 * (3 * z * z - 1), s15 * x * z, s15 / 2 * (x * x - y * y)], axis=1)
            return (y1, y2)

        def _forward(x, edge_src, edge_dst, edge_vec, emb, norm, W1, W2):
            N, E = (x.shape[0], edge_src.shape[0])
            xs = jnp.concatenate([x[edge_src, :8], x[edge_dst, :8]], axis=1)
            xv = jnp.concatenate([x[edge_src, 8:].reshape(E, 8, 3), x[edge_dst, 8:].reshape(E, 8, 3)], axis=1)
            y1, y2 = _sph(edge_vec)
            h = 2.0 ** 0.5 * jax.nn.relu(emb @ W1 / 10.0 ** 0.5)
            w = (h @ W2 / 16.0 ** 0.5).reshape(E, 7, MUL, MOUT)
            wa_s, wb_s, wa_g, wb_g, wc, wd, we = [w[:, i] for i in range(7)]
            s_out = PW_S * (jnp.einsum('eu,euw->ew', xs, wa_s) + INV_SQRT3 * jnp.einsum('eui,ei,euw->ew', xv, y1, wb_s))
            g_out = PW_S * (jnp.einsum('eu,euw->ew', xs, wa_g) + INV_SQRT3 * jnp.einsum('eui,ei,euw->ew', xv, y1, wb_g))
            v_out = PW_V * (INV_SQRT3 * jnp.einsum('eu,ek,euw->ewk', xs, y1, wc) + INV_SQRT3 * jnp.einsum('eui,euw->ewi', xv, wd) + jnp.einsum('eui,ea,iak,euw->ewk', xv, y2, W3J121, we))
            s_act = TANH_GAIN * jnp.tanh(s_out)
            gates = TANH_GAIN * jnp.tanh(g_out)
            edge_ftr = jnp.concatenate([s_act, (gates[:, :, None] * v_out).reshape(E, 24)], axis=1) * norm[:, None]
            return jax.ops.segment_sum(edge_ftr, edge_dst, num_segments=N)
        key = jax.random.key(seed)
        ks = jax.random.split(key, 8)
        N, E = (6250, 37500)
        return {'x': jax.random.normal(ks[0], (N, 32), jnp.float32), 'edge_src': jax.random.randint(ks[1], (E,), 0, N), 'edge_dst': jax.random.randint(ks[2], (E,), 0, N), 'edge_vec': jax.random.normal(ks[3], (E, 3), jnp.float32), 'emb': jax.random.uniform(ks[4], (E, 10), jnp.float32), 'norm': jax.random.uniform(ks[5], (E,), jnp.float32), 'W1': jax.random.normal(ks[6], (10, 16), jnp.float32), 'W2': jax.random.normal(ks[7], (16, 896), jnp.float32)}
    _L2_gnn_all = _L2_gnn_setup()
    _L2_gnn_in = {k: v for k, v in _L2_gnn_all.items() if k in ('W1', 'W2')}
    del _L2_gnn_all

    def _L3_gnn_setup():
        import jax, jax.numpy as jnp
        import numpy as np
        N_NODES = 12500
        key = jax.random.key(seed)
        k1, k2 = jax.random.split(key)
        x = jax.random.normal(k1, (N_NODES, 32), dtype=jnp.float32)
        edge_index = jax.random.randint(k2, (2, 200000), 0, N_NODES, dtype=jnp.int64)
        return {'x': x, 'edge_index': edge_index}
    _L3_gnn_all = _L3_gnn_setup()
    _L3_gnn_in = {k: v for k, v in _L3_gnn_all.items() if k in ()}
    del _L3_gnn_all
    return {'x': x, 'src': src, 'dst': dst, 'edge_attr_10': edge_attr_10, 'edge_attr_3': edge_attr_3, 'edge_attr_5': edge_attr_5, 'edge_weight': edge_weight, 'edge_weight1': edge_weight1, 'L0_gnn_W': _L0_gnn_in['W'], 'L1_gnn_lambda_max': _L1_gnn_in['lambda_max'], 'L1_gnn_cheb_W': _L1_gnn_in['cheb_W'], 'L1_gnn_cheb_b': _L1_gnn_in['cheb_b'], 'L1_gnn_gat_W_src': _L1_gnn_in['gat_W_src'], 'L1_gnn_gat_b_src': _L1_gnn_in['gat_b_src'], 'L1_gnn_gat_W_dst': _L1_gnn_in['gat_W_dst'], 'L1_gnn_gat_b_dst': _L1_gnn_in['gat_b_dst'], 'L1_gnn_gat_attn': _L1_gnn_in['gat_attn'], 'L2_gnn_W1': _L2_gnn_in['W1'], 'L2_gnn_W2': _L2_gnn_in['W2']}

def reference(x, src, dst, edge_attr_10, edge_attr_3, edge_attr_5, edge_weight, edge_weight1, L0_gnn_W, L1_gnn_lambda_max, L1_gnn_cheb_W, L1_gnn_cheb_b, L1_gnn_gat_W_src, L1_gnn_gat_b_src, L1_gnn_gat_W_dst, L1_gnn_gat_b_dst, L1_gnn_gat_attn, L2_gnn_W1, L2_gnn_W2):
    import jax
    import jax.numpy as jnp

    def _L0_gnn_ref(node_irreps, edge_index, sh0, sh1, sh2, W):
        import jax, jax.numpy as jnp
        import numpy as np
        import math
        M = 8
        COMBOS = [(0, 0, 0), (0, 1, 1), (1, 0, 1), (1, 1, 0), (1, 1, 1), (2, 1, 1)]

        def _cg_coeff(j1, m1, j2, m2, j3, m3):
            if m3 != m1 + m2:
                return 0.0
            f = math.factorial
            vmin = max(0, j2 - j3 - m1, j1 + m2 - j3)
            vmax = min(j1 + j2 - j3, j1 - m1, j2 + m2)
            pref = (2 * j3 + 1) * f(j3 + j1 - j2) * f(j3 - j1 + j2) * f(j1 + j2 - j3) / f(j1 + j2 + j3 + 1)
            pref *= f(j3 + m3) * f(j3 - m3) * f(j1 - m1) * f(j1 + m1) * f(j2 - m2) * f(j2 + m2)
            s = 0.0
            for v in range(vmin, vmax + 1):
                s += (-1) ** v / (f(v) * f(j1 + j2 - j3 - v) * f(j1 - m1 - v) * f(j2 + m2 - v) * f(j3 - j2 + m1 + v) * f(j3 - j1 - m2 + v))
            return math.sqrt(pref) * s

        def _su2_cg(l1, l2, l3):
            C = np.zeros((2 * l1 + 1, 2 * l2 + 1, 2 * l3 + 1), dtype=np.complex128)
            for m1 in range(-l1, l1 + 1):
                for m2 in range(-l2, l2 + 1):
                    m3 = m1 + m2
                    if -l3 <= m3 <= l3:
                        C[m1 + l1, m2 + l2, m3 + l3] = _cg_coeff(l1, m1, l2, m2, l3, m3)
            return C

        def _qmat(l):
            q = np.zeros((2 * l + 1, 2 * l + 1), dtype=np.complex128)
            for m in range(-l, 0):
                q[l + m, l + abs(m)] = 1 / np.sqrt(2)
                q[l + m, l - abs(m)] = -1j / np.sqrt(2)
            q[l, l] = 1.0
            for m in range(1, l + 1):
                q[l + m, l + abs(m)] = (-1) ** m / np.sqrt(2)
                q[l + m, l - abs(m)] = 1j * (-1) ** m / np.sqrt(2)
            return (-1j) ** l * q

        def _so3_cg(l1, l2, l3):
            C = np.einsum('ij,kl,mn,ikn->jlm', _qmat(l1), _qmat(l2), np.conj(_qmat(l3)).T, _su2_cg(l1, l2, l3))
            assert np.abs(C.imag).max() < 1e-06
            C = C.real
            return C / np.linalg.norm(C)
        CG = {c: jnp.asarray(_so3_cg(*c), dtype=jnp.float32) for c in COMBOS}
        N, E = (node_irreps.shape[0], edge_index.shape[1])
        src = node_irreps[edge_index[0]]
        feats = {0: src[:, :M][:, :, None], 1: src[:, M:].reshape(E, M, 3)}
        sh = {0: sh0, 1: sh1, 2: sh2}
        msg = {0: jnp.zeros((E, M, 1), node_irreps.dtype), 1: jnp.zeros((E, M, 3), node_irreps.dtype)}
        for idx, (le, ln, lo) in enumerate(COMBOS):
            base = jnp.einsum('ijk,ei,emj->emk', CG[le, ln, lo], sh[le], feats[ln])
            msg[lo] = msg[lo] + jnp.einsum('io,eik->eok', W[idx], base)
        tgt = edge_index[1]
        agg0 = jax.ops.segment_sum(msg[0].reshape(E, M), tgt, num_segments=N)
        agg1 = jax.ops.segment_sum(msg[1].reshape(E, 3 * M), tgt, num_segments=N)
        return jnp.concatenate([agg0, agg1], axis=1)

    def _L1_gnn_ref(src, dst, embedding, lambda_max, cheb_W, cheb_b, gat_W_src, gat_b_src, gat_W_dst, gat_b_dst, gat_attn):
        import jax, jax.numpy as jnp
        import numpy as np
        N, E, D, K, H = (12500, 200000, 32, 3, 1)

        def _cheb(src, dst, feat, lam, W, b, n):
            deg = jnp.clip(jax.ops.segment_sum(jnp.ones(src.shape[0], feat.dtype), dst, num_segments=n), 1.0)
            dinv = deg[:, None] ** (-0.5)
            re_norm = 2.0 / lam[0]

            def unnL(f):
                return jax.ops.segment_sum((f * dinv)[src], dst, num_segments=n) * dinv
            X0 = feat
            X1 = -re_norm * unnL(X0) + X0 * (re_norm - 1.0)
            Xs = [X0, X1]
            for _ in range(2, K):
                Xi = -2.0 * re_norm * unnL(X1) + X1 * (2.0 * (re_norm - 1.0)) - X0
                Xs.append(Xi)
                X0, X1 = (X1, Xi)
            return jax.nn.leaky_relu(jnp.concatenate(Xs, axis=1) @ W + b, 0.01)

        def _gatv2(src, dst, h, Ws, bs, Wd, bd, attn, n):
            Hh, Dd = attn.shape
            fs = (h @ Ws + bs).reshape(n, Hh, Dd)
            fd = (h @ Wd + bd).reshape(n, Hh, Dd)
            e = jax.nn.leaky_relu(fs[src] + fd[dst], 0.2)
            logits = jnp.einsum('ehd,hd->eh', e, attn)
            m = jax.ops.segment_max(logits, dst, num_segments=n)
            ex = jnp.exp(logits - m[dst])
            a = ex / jax.ops.segment_sum(ex, dst, num_segments=n)[dst]
            ft = jax.ops.segment_sum(fs[src] * a[..., None], dst, num_segments=n)
            return jax.nn.leaky_relu(ft, 0.01)
        n, d = embedding.shape
        h = _cheb(src, dst, embedding, lambda_max, cheb_W, cheb_b, n)
        h = _cheb(src, dst, h, lambda_max, cheb_W, cheb_b, n)
        out = _gatv2(src, dst, h, gat_W_src, gat_b_src, gat_W_dst, gat_b_dst, gat_attn, n)
        return out.reshape(-1, d)

    def _L2_gnn_ref(x, edge_src, edge_dst, edge_vec, emb, norm, W1, W2):
        import jax, jax.numpy as jnp
        import numpy as np
        MUL = 16
        MOUT = 8
        TANH_GAIN = 1.593
        INV_SQRT3 = 0.5773502691896258
        PW_S = 0.17677669529663687
        PW_V = 0.25

        def _w3j_121():
            s2, s6 = (2 ** 0.5, 6 ** 0.5)
            M = np.zeros((5, 3, 3))
            M[0, 0, 1] = M[0, 1, 0] = 1 / s2
            M[1, 1, 2] = M[1, 2, 1] = 1 / s2
            M[2] = np.diag([-1.0, -1.0, 2.0]) / s6
            M[3, 0, 2] = M[3, 2, 0] = 1 / s2
            M[4] = np.diag([1.0, -1.0, 0.0]) / s2
            return jnp.asarray(np.transpose(M, (1, 0, 2)) / 5 ** 0.5, jnp.float32)
        W3J121 = _w3j_121()

        def _sph(edge_vec):
            n = edge_vec / jnp.linalg.norm(edge_vec, axis=1, keepdims=True)
            x, y, z = (n[:, 0], n[:, 1], n[:, 2])
            y1 = 3.0 ** 0.5 * n
            s15 = 15.0 ** 0.5
            y2 = jnp.stack([s15 * x * y, s15 * y * z, 5.0 ** 0.5 / 2 * (3 * z * z - 1), s15 * x * z, s15 / 2 * (x * x - y * y)], axis=1)
            return (y1, y2)

        def _forward(x, edge_src, edge_dst, edge_vec, emb, norm, W1, W2):
            N, E = (x.shape[0], edge_src.shape[0])
            xs = jnp.concatenate([x[edge_src, :8], x[edge_dst, :8]], axis=1)
            xv = jnp.concatenate([x[edge_src, 8:].reshape(E, 8, 3), x[edge_dst, 8:].reshape(E, 8, 3)], axis=1)
            y1, y2 = _sph(edge_vec)
            h = 2.0 ** 0.5 * jax.nn.relu(emb @ W1 / 10.0 ** 0.5)
            w = (h @ W2 / 16.0 ** 0.5).reshape(E, 7, MUL, MOUT)
            wa_s, wb_s, wa_g, wb_g, wc, wd, we = [w[:, i] for i in range(7)]
            s_out = PW_S * (jnp.einsum('eu,euw->ew', xs, wa_s) + INV_SQRT3 * jnp.einsum('eui,ei,euw->ew', xv, y1, wb_s))
            g_out = PW_S * (jnp.einsum('eu,euw->ew', xs, wa_g) + INV_SQRT3 * jnp.einsum('eui,ei,euw->ew', xv, y1, wb_g))
            v_out = PW_V * (INV_SQRT3 * jnp.einsum('eu,ek,euw->ewk', xs, y1, wc) + INV_SQRT3 * jnp.einsum('eui,euw->ewi', xv, wd) + jnp.einsum('eui,ea,iak,euw->ewk', xv, y2, W3J121, we))
            s_act = TANH_GAIN * jnp.tanh(s_out)
            gates = TANH_GAIN * jnp.tanh(g_out)
            edge_ftr = jnp.concatenate([s_act, (gates[:, :, None] * v_out).reshape(E, 24)], axis=1) * norm[:, None]
            return jax.ops.segment_sum(edge_ftr, edge_dst, num_segments=N)
        return _forward(x, edge_src, edge_dst, edge_vec, emb, norm, W1, W2)

    def _L3_gnn_ref(x, edge_index):
        import jax, jax.numpy as jnp
        import numpy as np
        N_NODES = 12500
        src = edge_index[0]
        dst = edge_index[1]
        x_j = x[src]
        out = jax.ops.segment_sum(x_j, dst, num_segments=x.shape[0])
        return out
    edge_index = jnp.stack([src, dst])
    x = _layernorm(x + _L0_gnn_ref(x, edge_index, edge_weight1, edge_attr_3, edge_attr_5, L0_gnn_W), axis=-1)
    x = _layernorm(x + _L1_gnn_ref(src, dst, x, L1_gnn_lambda_max, L1_gnn_cheb_W, L1_gnn_cheb_b, L1_gnn_gat_W_src, L1_gnn_gat_b_src, L1_gnn_gat_W_dst, L1_gnn_gat_b_dst, L1_gnn_gat_attn), axis=-1)
    x = _layernorm(x + _L2_gnn_ref(x, src, dst, edge_attr_3, edge_attr_10, edge_weight, L2_gnn_W1, L2_gnn_W2), axis=-1)
    x = _layernorm(x + _L3_gnn_ref(x, edge_index), axis=-1)
    return x

_drawn_inputs = setup_inputs


def setup_inputs(seed=0):
    import zlib

    import numpy as np

    out = dict(_drawn_inputs(seed))
    spreads = {'L1_gnn_cheb_b': (0.0, 0.1),
     'L1_gnn_gat_b_src': (0.0, 0.1),
     'L1_gnn_gat_b_dst': (0.0, 0.1)}
    factors = {}
    for name, (base, spread) in spreads.items():
        noise = np.random.default_rng([zlib.crc32(name.encode()), seed]).standard_normal(out[name].shape)
        drawn = base * np.exp(spread * noise) if base else spread * noise
        out[name] = jnp.asarray(drawn.astype(out[name].dtype))
    for name, factor in factors.items():
        out[name] = (out[name] * factor).astype(out[name].dtype)
    return out
```

```python
from contextlib import ExitStack
import math

import concourse.bass as bass
from concourse import mybir

F32 = mybir.dt.float32
BF16 = mybir.dt.bfloat16
I32 = mybir.dt.int32
ALU = mybir.AluOpType
ACT = mybir.ActivationFunctionType
AX = mybir.AxisListType

P = 128
D = 32
M = 8
LOG_P = 7
EPS = 1e-5
BIG = 1e30


def shapes(n_nodes, n_edges):
    nj = -(-n_nodes // P)
    t = -(-(-(-n_edges // P)) // 784) * 784
    return nj, t


def chain(engine, sem, start):
    count = [0]

    def link(instruction):
        count[0] += 1
        instruction.then_inc(sem, 1)
        engine.wait_ge(sem, start + count[0])

    return link, count


def gnn_kernel(nc, x, src, dst, emb_t, attr3, attr5, edge_w, edge_w1, l0_w, lam, cheb_w, cheb_b,
               gat_ws, gat_bs, gat_wd, gat_bd, gat_attn, w1, w2, out):
    NJ = x.shape[1]
    T = src.shape[1]
    ROWS = P * NJ
    EP = P * T
    C_SUM = 98
    C_MSG = 56
    assert T % (2 * C_SUM) == 0 and T % (2 * C_MSG) == 0
    JB = 14
    assert NJ % JB == 0 and JB * (D + 1) <= 512
    GROUPS = [(4 * g, min(4, NJ - 4 * g)) for g in range(-(-NJ // 4))]

    top = ExitStack()
    with top:
        def keep(name, shape, dt=F32):
            return top.enter_context(nc.sbuf_tensor(name, shape, dt))

        level = {}

        def signal(name):
            sem = top.enter_context(nc.semaphore(name))
            level[id(sem)] = 0
            return sem

        def at(sem, count):
            return level[id(sem)] + count

        def close(sem, count):
            level[id(sem)] += count

        src_rows = nc.dram_tensor("src_rows", [P, T], I32).ap()
        table_l0 = nc.dram_tensor("table_l0", [ROWS, 112], F32).ap()
        table = nc.dram_tensor("table", [ROWS, D], F32).ap()
        scanned_rows = nc.dram_tensor("scanned_rows", [EP, D], F32).ap()
        scanned_rows33 = nc.dram_tensor("scanned_rows33", [EP, D + 1], F32).ap()
        gathered_rows = nc.dram_tensor("gathered_rows", [EP, D], F32).ap()
        start_rows = nc.dram_tensor("start_rows", [EP, D], F32).ap()
        hidden = nc.dram_tensor("hidden", [P, T, 16], F32).ap()

        x_cur = keep("x_cur", [P, NJ, D])
        same = keep("same", [P, T])
        dst_f = keep("dst_f", [P, T])
        end_i = keep("end_i", [P, NJ], I32)
        start_i = keep("start_i", [P, NJ], I32)
        nonempty = keep("nonempty", [P, NJ])
        dinv = keep("dinv", [P, NJ])
        cross_lo = keep("cross_lo", [P, P])
        cross_hi = keep("cross_hi", [P, NJ])
        first_f = keep("first_f", [P, 1])
        last_f = keep("last_f", [P, 1])
        first_row = keep("first_row", [P, 1], I32)
        ident = keep("ident", [P, P])
        ones = keep("ones", [P, P])
        iota_f = keep("iota_f", [P, P])
        eps = keep("eps", [P, 1])
        tail = keep("tail", [P, D + 1])
        fill = keep("fill", [P, D])
        lam_c = keep("lam_c", [P, 6])
        agg = keep("agg", [P, NJ * (D + 1)])
        spread = keep("spread", [P, NJ * (D + 1)])
        stat = keep("stat", [P, NJ, 4])
        sq = keep("sq", [P, NJ, D])

        s_in = signal("s_in")
        s_v = signal("s_v")
        s_pool = signal("s_pool")
        s_pe = signal("s_pe")
        s_act = signal("s_act")
        s_vdone = signal("s_vdone")
        s_write = signal("s_write")
        s_agg = signal("s_agg")
        s_scatter = signal("s_scatter")
        chunks_begun = signal("chunks_begun")
        s_tp = signal("s_tp")
        s_xt = signal("s_xt")
        s_mm = signal("s_mm")
        s_ev = signal("s_ev")
        free = [signal(f"free{b}") for b in range(2)]
        loaded = [signal(f"loaded{b}") for b in range(2)]
        scanned = [signal(f"scanned{b}") for b in range(2)]
        stored = [signal(f"stored{b}") for b in range(2)]

        def gather_signals(tag):
            return [signal(f"gathered_{tag}{b}") for b in range(2)]

        def row_gather(pool, dest, table_ap, index):
            return pool.indirect_dma_start(out=dest, out_offset=None, in_=table_ap,
                                           in_offset=bass.IndirectOffsetOnAxis(ap=index, axis=0))

        def scans(v, buf, mask, carry, n):
            for f in range(n):
                last = v.tensor_tensor_scan(buf[:, :, f], mask, buf[:, :, f], carry[:, f:f + 1],
                                            ALU.mult, ALU.add)
            return last

        def prepare():
            CH = C_MSG // 2
            with ExitStack() as st:
                def sb(name, shape, dt=F32):
                    return st.enter_context(nc.sbuf_tensor(name, shape, dt))
                src_i = sb("src_i", [P, T], I32)
                dst_i = sb("dst_i", [P, T], I32)
                work_i = sb("work_i", [P, T], I32)
                lo_f = sb("lo_f", [P, T], BF16)
                hi_f = sb("hi_f", [P, T], BF16)
                iota_i = sb("iota_i", [P, P], I32)
                iota_b = sb("iota_b", [P, P], BF16)
                lower = sb("lower", [P, P])
                zeros = sb("zeros", [P, 2048])
                prev_i = sb("prev_i", [P, 1], I32)
                next_i = sb("next_i", [P, 1], I32)
                pn = sb("pn", [P, 4])
                part_i = sb("part_i", [P, 4], I32)
                cross_i = sb("cross_i", [P, 2], I32)
                lo1 = [sb(f"lo1_{b}", [P, CH, P], BF16) for b in range(2)]
                hi1 = [sb(f"hi1_{b}", [P, CH, NJ], BF16) for b in range(2)]
                zero_b = sb("zero_b", [P, P], BF16)
                cnt = sb("cnt", [P, NJ])
                cum = sb("cum", [P, 4, NJ])
                w1_s = sb("w1_s", [10, 16])
                emb_s = [sb(f"emb_s{b}", [10, CH * P]) for b in range(2)]
                hid = [sb(f"hid{b}", [P, CH, 16]) for b in range(2)]
                p_cnt = st.enter_context(nc.psum_tensor("p_cnt", [P, NJ], F32))
                p_cum = st.enter_context(nc.psum_tensor("p_cum", [P, 2, NJ], F32))
                p_h = [st.enter_context(nc.psum_tensor(f"p_h{b}", [P, 16 * CH], F32)) for b in range(2)]
                one_hot = signal("one_hot")
                counted = signal("counted")
                h_made = signal("h_made")
                h_out = [signal(f"h_out{b}") for b in range(2)]
                zero_out = signal("zero_out")
                h_free = signal("h_free")
                w1_in = signal("w1_in")
                h_in = [signal(f"h_in{b}") for b in range(2)]
                dst_flat = dst.rearrange("p t -> (p t)")

                with nc.Block() as block:
                    @block.gpsimd
                    def _(pool):
                        nc.gpsimd.iota(iota_i[:], [[1, P]], base=0, channel_multiplier=0).then_inc(s_pool, 1)
                        nc.gpsimd.memset(ones[:], 1.0).then_inc(s_pool, 1)
                        nc.gpsimd.memset(eps[:], EPS).then_inc(s_pool, 1)
                        nc.gpsimd.memset(zeros[:], 0.0).then_inc(s_pool, 1)
                        nc.gpsimd.memset(zero_b[:], 0.0).then_inc(s_pool, 1)
                        nc.gpsimd.memset(prev_i[:], -1).then_inc(s_pool, 1)
                        nc.gpsimd.memset(next_i[:], -1).then_inc(s_pool, 1)
                        pool.wait_ge(s_pool, 7)
                        nc.gpsimd.affine_select(out=ident[:], in_=ones[:], compare_op=ALU.is_equal, fill=0.0,
                                                base=0, pattern=[[-1, P]], channel_multiplier=1).then_inc(s_pool, 1)
                        nc.gpsimd.affine_select(out=lower[:], in_=ones[:], compare_op=ALU.is_ge, fill=0.0,
                                                base=0, pattern=[[1, P]], channel_multiplier=-1).then_inc(s_pool, 1)

                    @block.sync
                    def _(sp):
                        sp.dma_start(dst_i[:], dst).then_inc(s_in, 16)
                        sp.dma_start(src_i[:], src).then_inc(s_in, 16)
                        sp.dma_start(x_cur[:], x).then_inc(s_in, 16)
                        sp.dma_start(lam_c[:, 0:1], lam.rearrange("(a b) -> a b", a=1).to_broadcast([P, 1])).then_inc(s_in, 16)
                        sp.wait_ge(s_pool, 7)
                        with nc.allow_non_contiguous_dma(reason="one word of each partition"):
                            sp.dma_start(prev_i[1:P, :], dst[0:P - 1, T - 1:T]).then_inc(s_in, 16)
                            sp.dma_start(next_i[0:P - 1, :], dst[1:P, 0:1]).then_inc(s_in, 16)
                        zr = start_rows.rearrange("(p q) f -> p (q f)", p=P)
                        for c in range(0, T * D, 2048):
                            n = min(2048, T * D - c)
                            sp.dma_start(zr[:, c:c + n], zeros[:, 0:n]).then_inc(zero_out, 16)
                        sp.wait_ge(s_vdone, 1)
                        sp.dma_start(src_rows, work_i[:]).then_inc(s_write, 16)
                        sp.wait_ge(s_write, 16)
                        sp.wait_ge(zero_out, 16 * -(-T * D // 2048))

                    @block.vector
                    def _(v):
                        start = 0
                        link, count = chain(v, s_v, start)
                        v.wait_ge(s_in, 96)
                        v.wait_ge(s_pool, 9)
                        link(nc.vector.tensor_scalar(work_i[:], src_i[:], P - 1, None, ALU.bitwise_and))
                        link(nc.vector.tensor_scalar(src_i[:], src_i[:], LOG_P, None, ALU.logical_shift_right))
                        link(nc.vector.scalar_tensor_tensor(work_i[:], work_i[:], float(NJ), src_i[:], ALU.mult, ALU.add))
                        link(nc.vector.tensor_copy(dst_f[:], dst_i[:]))
                        link(nc.vector.tensor_tensor(same[:, 1:T], dst_f[:, 1:T], dst_f[:, 0:T - 1], ALU.is_equal))
                        link(nc.vector.tensor_copy(pn[:, 0:1], prev_i[:]))
                        link(nc.vector.tensor_copy(pn[:, 1:2], next_i[:]))
                        link(nc.vector.tensor_copy(first_f[:], dst_f[:, 0:1]))
                        link(nc.vector.tensor_copy(last_f[:], dst_f[:, T - 1:T]))
                        link(nc.vector.tensor_tensor(same[:, 0:1], pn[:, 0:1], first_f[:], ALU.is_equal))
                        link(nc.vector.tensor_tensor(pn[:, 2:3], pn[:, 1:2], last_f[:], ALU.is_equal))
                        link(nc.vector.tensor_scalar(part_i[:, 0:1], dst_i[:, 0:1], P - 1, None, ALU.bitwise_and))
                        link(nc.vector.tensor_scalar(part_i[:, 1:2], dst_i[:, 0:1], LOG_P, None, ALU.logical_shift_right))
                        link(nc.vector.scalar_tensor_tensor(first_row[:], part_i[:, 0:1], float(NJ), part_i[:, 1:2], ALU.mult, ALU.add))
                        link(nc.vector.tensor_scalar(cross_i[:, 0:1], dst_i[:, T - 1:T], P - 1, None, ALU.bitwise_and))
                        link(nc.vector.tensor_scalar(cross_i[:, 1:2], dst_i[:, T - 1:T], LOG_P, None, ALU.logical_shift_right))
                        link(nc.vector.tensor_copy(lam_c[:, 4:6], cross_i[:]))
                        link(nc.vector.tensor_copy(iota_f[:], iota_i[:]))
                        link(nc.vector.tensor_copy(iota_b[:], iota_i[:]))
                        link(nc.vector.tensor_scalar(cross_lo[:], iota_f[:], lam_c[:, 4:5], pn[:, 2:3], ALU.is_equal, ALU.mult))
                        link(nc.vector.tensor_scalar(cross_hi[:], iota_f[:, 0:NJ], lam_c[:, 5:6], None, ALU.is_equal))
                        link(nc.vector.tensor_scalar(src_i[:], dst_i[:], P - 1, None, ALU.bitwise_and))
                        link(nc.vector.tensor_copy(lo_f[:], src_i[:]))
                        link(nc.vector.tensor_scalar(src_i[:], dst_i[:], LOG_P, None, ALU.logical_shift_right))
                        ins = nc.vector.tensor_copy(hi_f[:], src_i[:])
                        link(ins)
                        nc.vector.memset(tail[:], 0.0).then_inc(s_vdone, 1)
                        link(nc.vector.reciprocal(lam_c[:, 1:2], lam_c[:, 0:1]))
                        link(nc.vector.tensor_scalar(lam_c[:, 0:1], lam_c[:, 1:2], -2.0, None, ALU.mult))
                        link(nc.vector.tensor_scalar(lam_c[:, 1:2], lam_c[:, 0:1], -1.0, -1.0, ALU.mult, ALU.add))
                        link(nc.vector.tensor_scalar(lam_c[:, 2:4], lam_c[:, 0:2], 2.0, None, ALU.mult))
                        v.sem_inc(one_hot, 1)
                        with v.Fori(0, T // CH // 2) as i:
                            for b in range(2):
                                v.wait_ge(counted, 1 + 2 * i + b)
                                t0 = (2 * i + b) * CH
                                for buf, half, n in ((lo1[b], lo_f, P), (hi1[b], hi_f, NJ)):
                                    last = nc.vector.tensor_tensor(
                                        buf[:], iota_b[:, 0:n].rearrange("p (a n) -> p a n", a=1).to_broadcast([P, CH, n]),
                                        half[:, bass.ds(t0, CH)].rearrange("p (t a) -> p t a", a=1).to_broadcast([P, CH, n]), ALU.is_equal)
                                last.then_inc(one_hot, 1)
                        v.wait_ge(s_pe, 1)
                        link(nc.vector.tensor_copy(cnt[:], p_cnt[:]))
                        link(nc.vector.tensor_scalar(nonempty[:], cnt[:], 1.0, None, ALU.min))
                        nc.vector.tensor_scalar(dinv[:], cnt[:], 1.0, None, ALU.max).then_inc(s_vdone, 1)
                        v.wait_ge(s_pe, 2)
                        link(nc.vector.tensor_copy(cum[:, 0:2, :], p_cum[:]))
                        link(nc.vector.tensor_tensor_scan(cum[:, 2, :], ones[:, 0:NJ], cum[:, 1, :], 0.0, ALU.mult, ALU.add))
                        link(nc.vector.tensor_tensor(cum[:, 2, :], cum[:, 2, :], cum[:, 1, :], ALU.subtract))
                        link(nc.vector.tensor_tensor(cum[:, 2, :], cum[:, 2, :], cum[:, 0, :], ALU.add))
                        link(nc.vector.tensor_scalar(cum[:, 3, :], cum[:, 2, :], -1.0, 0.0, ALU.add, ALU.max))
                        link(nc.vector.tensor_copy(end_i[:], cum[:, 3, :]))
                        link(nc.vector.tensor_tensor(cum[:, 2, :], cum[:, 2, :], cnt[:], ALU.subtract))
                        link(nc.vector.tensor_scalar(cum[:, 3, :], nonempty[:], -float(EP), float(EP), ALU.mult, ALU.add))
                        link(nc.vector.tensor_tensor(cum[:, 2, :], cum[:, 2, :], cum[:, 3, :], ALU.add))
                        link(nc.vector.tensor_copy(start_i[:], cum[:, 2, :]))
                        v.wait_ge(s_act, 1)
                        link(nc.vector.reciprocal(dinv[:], dinv[:]))
                        close(s_v, count[0])

                    @block.tensor
                    def _(pe):
                        pe.wait_ge(s_pool, 9)
                        nc.tensor.matmul(p_cnt[:], zero_b[:], zero_b[:, 0:NJ], start=True, stop=False).then_inc(counted, 2)
                        with pe.Fori(0, T // CH // 2) as i:
                            for b in range(2):
                                pe.wait_ge(one_hot, 2 + 2 * i + b)
                                for t in range(CH):
                                    last = nc.tensor.matmul(p_cnt[:], lo1[b][:, t, :], hi1[b][:, t, :], start=False, stop=False)
                                last.then_inc(counted, 1)
                        nc.tensor.matmul(p_cnt[:], zero_b[:], zero_b[:, 0:NJ], start=False, stop=True).then_inc(s_pe, 1)
                        pe.wait_ge(s_vdone, 2)
                        nc.tensor.matmul(p_cum[:, 0, :], lower[:], cnt[:], start=True, stop=True)
                        nc.tensor.matmul(p_cum[:, 1, :], ones[:], cnt[:], start=True, stop=True).then_inc(s_pe, 1)
                        pe.wait_ge(w1_in, 16)
                        with pe.Fori(0, T // CH // 2) as i:
                            for b in range(2):
                                pe.wait_ge(h_in[b], 16 * (i + 1))
                                pe.wait_ge(h_free, 1 + 2 * i + b)
                                for t in range(CH):
                                    last = nc.tensor.matmul(p_h[b][:, 16 * t:16 * t + 16],
                                                            emb_s[b][:, t * P:(t + 1) * P], w1_s[:], start=True, stop=True)
                                last.then_inc(h_made, 1)

                    @block.scalar
                    def _(act):
                        act.dma_start(w1_s[:], w1).then_inc(w1_in, 16)
                        act.wait_ge(s_vdone, 2)
                        nc.scalar.activation(dinv[:], dinv[:], ACT.Sqrt).then_inc(s_act, 1)
                        act.sem_inc(h_free, 2)
                        for b in range(2):
                            act.dma_start(emb_s[b][:], emb_t[:, b * CH * P:(b + 1) * CH * P]).then_inc(h_in[b], 16)
                        last_pair = T // CH // 2 - 1

                        def relu_out(i, b):
                            act.wait_ge(h_made, 1 + 2 * i + b)
                            nc.scalar.activation(hid[b][:], p_h[b][:].rearrange("p (t k) -> p t k", k=16),
                                                 ACT.Relu).then_inc(h_free, 1)
                            act.wait_ge(h_free, 3 + 2 * i + b)
                            act.dma_start(hidden[:, bass.ds((2 * i + b) * CH, CH), :], hid[b][:]).then_inc(h_out[b], 16)
                            act.wait_ge(h_out[b], 16 * (i + 1))
                        with act.Fori(0, last_pair) as i:
                            for b in range(2):
                                relu_out(i, b)
                                act.dma_start(emb_s[b][:], emb_t[:, bass.ds((2 * i + 2 + b) * CH * P, CH * P)]).then_inc(h_in[b], 16)
                        for b in range(2):
                            relu_out(last_pair, b)
                close(s_in, 96)
                close(s_pool, 9)
                close(s_vdone, 2)
                close(s_write, 16)
                close(s_pe, 2)
                close(s_act, 1)

        def fetch_sums(pool, rows, n):
            for j in range(NJ):
                row_gather(pool, agg[:, j * n:(j + 1) * n], rows, end_i[:, j:j + 1]).then_inc(s_agg, 16)

        def crossing_matmuls(pe, banks, n):
            pe.wait_ge(s_vdone, at(s_vdone, 1))
            for k in range(NJ // JB):
                if k >= 2:
                    pe.wait_ge(s_ev, at(s_ev, k - 1))
                nc.tensor.matmul(banks[k % 2][:, 0:JB * n], cross_lo[:], spread[:, k * JB * n:(k + 1) * JB * n],
                                 start=True, stop=True).then_inc(s_pe, 1)

        def finish_sums(v, link, banks, n):
            nc.vector.tensor_tensor(
                spread[:, 0:NJ * n].rearrange("p (j f) -> p j f", f=n),
                cross_hi[:].rearrange("p (j a) -> p j a", a=1).to_broadcast([P, NJ, n]),
                tail[:, 0:n].rearrange("p (a f) -> p a f", a=1).to_broadcast([P, NJ, n]),
                ALU.mult).then_inc(s_vdone, 1)
            v.wait_ge(s_agg, at(s_agg, 16 * NJ))
            a = agg[:, 0:NJ * n].rearrange("p (j f) -> p j f", f=n)
            link(nc.vector.tensor_tensor(a, a, nonempty[:].rearrange("p (j a) -> p j a", a=1).to_broadcast([P, NJ, n]), ALU.mult))
            for k in range(NJ // JB):
                v.wait_ge(s_pe, at(s_pe, k + 1))
                part = agg[:, k * JB * n:(k + 1) * JB * n]
                nc.vector.tensor_tensor(part, part, banks[k % 2][:, 0:JB * n], ALU.add).then_inc(s_ev, 1)
            v.wait_ge(s_ev, at(s_ev, NJ // JB))

        def sums_closed():
            close(s_agg, 16 * NJ)
            close(s_pe, NJ // JB)
            close(s_ev, NJ // JB)
            close(s_vdone, 1)

        def by_col(t):
            return t.rearrange("p (j a) -> p j a", a=1).to_broadcast([P, NJ, D])

        def layer_norm(v, link, t, act_done):
            link(nc.vector.tensor_reduce(stat[:, :, 0], t, AX.X, ALU.add))
            link(nc.vector.tensor_scalar(stat[:, :, 0], stat[:, :, 0], 1.0 / D, None, ALU.mult))
            link(nc.vector.tensor_tensor(t, t, stat[:, :, 0:1].to_broadcast([P, NJ, D]), ALU.subtract))
            link(nc.vector.tensor_tensor(sq[:], t, t, ALU.mult))
            nc.vector.tensor_reduce(stat[:, :, 1], sq[:], AX.X, ALU.add).then_inc(s_vdone, 1)
            v.wait_ge(s_act, act_done)
            link(nc.vector.reciprocal(stat[:, :, 3], stat[:, :, 2]))
            link(nc.vector.tensor_tensor(t, t, stat[:, :, 3:4].to_broadcast([P, NJ, D]), ALU.mult))

        def norm_root(act, ready):
            act.wait_ge(s_vdone, ready)
            nc.scalar.activation(stat[:, :, 2], stat[:, :, 1], ACT.Sqrt, bias=eps[:], scale=1.0 / D).then_inc(s_act, 1)

        def linear_pe(pe, srcs, w_list, n, pt, xt, po):
            for g, (j0, nj) in enumerate(GROUPS):
                if g >= 2:
                    pe.wait_ge(s_xt, at(s_xt, g - 1))
                for k, s in enumerate(srcs):
                    last = nc.tensor.transpose(pt[g % 2][0:nj * D, k * P:(k + 1) * P],
                                               s[:, j0:j0 + nj, :].rearrange("p j f -> p (j f)"), ident[:])
                last.then_inc(s_tp, 1)
                pe.wait_ge(s_xt, at(s_xt, g + 1))
                if g >= 2:
                    pe.wait_ge(s_ev, at(s_ev, g - 1))
                for k in range(len(srcs)):
                    last = nc.tensor.matmul(po[g % 2][:, 0:nj * n], xt[g % 2][0:nj * D, k * P:(k + 1) * P],
                                            w_list[k][0:nj * D, 0:nj * n],
                                            start=(k == 0), stop=(k == len(srcs) - 1))
                last.then_inc(s_mm, 1)

        def linear_act(act, n_srcs, pt, xt):
            for g, (j0, nj) in enumerate(GROUPS):
                act.wait_ge(s_tp, at(s_tp, g + 1))
                if g >= 2:
                    act.wait_ge(s_mm, at(s_mm, g - 1))
                nc.scalar.activation(xt[g % 2][0:nj * D, 0:n_srcs * P], pt[g % 2][0:nj * D, 0:n_srcs * P],
                                     ACT.Copy).then_inc(s_xt, 1)

        def linear_out(v, dest, n, po, bias=None):
            for g, (j0, nj) in enumerate(GROUPS):
                v.wait_ge(s_mm, at(s_mm, g + 1))
                got = po[g % 2][:, 0:nj * n].rearrange("p (j f) -> p j f", f=n)
                if bias is None:
                    nc.vector.tensor_copy(dest[:, j0:j0 + nj, :], got).then_inc(s_ev, 1)
                else:
                    nc.vector.tensor_tensor(dest[:, j0:j0 + nj, :], got,
                                            bias[:, 0:n].rearrange("p (a f) -> p a f", a=1).to_broadcast([P, nj, n]),
                                            ALU.add).then_inc(s_ev, 1)
            v.wait_ge(s_ev, at(s_ev, len(GROUPS)))

        def linear_closed():
            for s in (s_tp, s_xt, s_mm, s_ev):
                close(s, len(GROUPS))

        def replicate(sp, w, n):
            for k in range(1, 4):
                sp.dma_start(w[k * D:(k + 1) * D, k * n:(k + 1) * n], w[0:D, 0:n]).then_inc(s_write, 16)

        def sum_pass(tag):
            CH = C_SUM
            gathered = gather_signals(tag)
            with ExitStack() as st:
                idx = [st.enter_context(nc.sbuf_tensor(f"idx_{tag}{b}", [P, CH], I32)) for b in range(2)]
                rows = [st.enter_context(nc.sbuf_tensor(f"rows_{tag}{b}", [P, CH, D], F32)) for b in range(2)]
                z = scanned_rows.rearrange("(p t) f -> p t f", p=P)
                with nc.Block() as block:
                    @block.sync
                    def _(sp):
                        with sp.Fori(0, T // CH // 2) as i:
                            for b in range(2):
                                sp.wait_ge(free[b], at(free[b], 1 + i))
                                sp.dma_start(idx[b][:], src_rows[:, bass.ds((2 * i + b) * CH, CH)]).then_inc(loaded[b], 16)

                    @block.gpsimd
                    def _(pool):
                        with pool.Fori(0, T // CH // 2) as i:
                            for b in range(2):
                                pool.wait_ge(loaded[b], at(loaded[b], 16 * (i + 1)))
                                pool.sem_inc(chunks_begun, 1)
                                for t in range(CH):
                                    row_gather(pool, rows[b][:, t, :], table, idx[b][:, t:t + 1]).then_inc(gathered[b], 16)

                    @block.vector
                    def _(v):
                        nc.vector.memset(tail[:], 0.0).then_inc(s_v, 1)
                        with v.Fori(0, T // CH // 2) as i:
                            for b in range(2):
                                v.wait_ge(s_v, at(s_v, 1 + 4 * i + 2 * b))
                                v.wait_ge(gathered[b], 16 * CH * (i + 1))
                                scans(nc.vector, rows[b], same[:, bass.ds((2 * i + b) * CH, CH)], tail, D).then_inc(s_v, 1)
                                v.wait_ge(s_v, at(s_v, 2 + 4 * i + 2 * b))
                                nc.vector.tensor_copy(tail[:, 0:D], rows[b][:, CH - 1, :]).then_inc(s_v, 1)

                    @block.scalar
                    def _(act):
                        for b in range(2):
                            act.sem_inc(free[b], 1)
                        with act.Fori(0, T // CH // 2) as i:
                            for b in range(2):
                                act.wait_ge(s_v, at(s_v, 3 + 4 * i + 2 * b))
                                act.dma_start(z[:, bass.ds((2 * i + b) * CH, CH), :], rows[b][:]).then_inc(stored[b], 16)
                                act.wait_ge(stored[b], at(stored[b], 16 * (i + 1)))
                                act.sem_inc(free[b], 1)
            n = T // CH // 2
            close(s_v, 1 + 4 * n)
            for b in range(2):
                close(free[b], 1 + n)
                close(loaded[b], 16 * n)
                close(stored[b], 16 * n)

        def l0_table():
            R3 = 1.0 / math.sqrt(3.0)
            R6 = 1.0 / math.sqrt(6.0)
            with ExitStack() as st:
                wb = st.enter_context(nc.sbuf_tensor("wb_l0", [P, 4 * 112], F32))
                rows = st.enter_context(nc.sbuf_tensor("rows_l0", [P, NJ, 112], F32))
                pt = [st.enter_context(nc.psum_tensor(f"pt{b}", [P, 512], F32)) for b in range(2)]
                po = [st.enter_context(nc.psum_tensor(f"po{b}", [P, 512], F32)) for b in range(2)]
                xt = [st.enter_context(nc.sbuf_tensor(f"xt{b}", [P, P], F32)) for b in range(2)]
                with nc.Block() as block:
                    @block.sync
                    def _(sp):
                        sp.wait_ge(s_vdone, at(s_vdone, 1))
                        with nc.allow_non_contiguous_dma(reason="weights of a few hundred bytes"):
                            n = 0
                            for col, k in ((0, 0), (8, 2)):
                                sp.dma_start(wb[0:M, col:col + M], l0_w[k]).then_inc(s_in, 16)
                                n += 16
                            for col, k in ((16, 1), (40, 3), (64, 4), (88, 5)):
                                for c in range(3):
                                    sp.dma_start(wb[M + c:D:3, col + c:col + 24:3], l0_w[k]).then_inc(s_in, 16)
                                    n += 16
                        assert n == 14 * 16
                        sp.wait_ge(s_vdone, at(s_vdone, 2))
                        replicate(sp, wb, 112)
                        sp.wait_ge(s_vdone, at(s_vdone, 3))
                        sp.dma_start(table_l0.rearrange("(p j) f -> p j f", p=P), rows[:]).then_inc(s_write, 16)
                        sp.wait_ge(s_write, at(s_write, 64))

                    @block.vector
                    def _(v):
                        nc.vector.memset(wb[:], 0.0).then_inc(s_vdone, 1)
                        v.wait_ge(s_in, at(s_in, 14 * 16))
                        start = at(s_v, 0)
                        link, count = chain(v, s_v, start)
                        link(nc.vector.tensor_scalar(wb[0:D, 8:64], wb[0:D, 8:64], R3, None, ALU.mult))
                        nc.vector.tensor_scalar(wb[0:D, 64:88], wb[0:D, 64:88], R6, None, ALU.mult).then_inc(s_vdone, 1)
                        linear_out(v, rows, 112, po)
                        v.sem_inc(s_vdone, 1)
                        close(s_v, count[0])

                    @block.tensor
                    def _(pe):
                        pe.wait_ge(s_write, at(s_write, 48))
                        linear_pe(pe, [x_cur], [wb], 112, pt, xt, po)

                    @block.scalar
                    def _(act):
                        linear_act(act, 1, pt, xt)
            close(s_in, 14 * 16)
            close(s_vdone, 3)
            close(s_write, 64)
            linear_closed()

        def l0_pass():
            CH = C_MSG
            gathered = gather_signals("l0")
            A = 1.0 / math.sqrt(10.0)
            B = 1.0 / math.sqrt(30.0)
            with ExitStack() as st:
                def sb(name, shape, dt=F32):
                    return st.enter_context(nc.sbuf_tensor(name, shape, dt))
                idx = [sb(f"idx_l0{b}", [P, CH], I32) for b in range(2)]
                rows = [sb(f"g_l0{b}", [P, CH, 112]) for b in range(2)]
                msg = [sb(f"msg_l0{b}", [P, CH, D]) for b in range(2)]
                a3 = [sb(f"a3_{b}", [P, CH, 3]) for b in range(2)]
                a5 = [sb(f"a5_{b}", [P, CH, 5]) for b in range(2)]
                s0 = [sb(f"s0_{b}", [P, CH]) for b in range(2)]
                bm = sb("bm", [P, CH, 3, 3])
                tmp = sb("tmp", [P, CH, M, 3])
                z = scanned_rows.rearrange("(p t) f -> p t f", p=P)
                LINKS = 29
                with nc.Block() as block:
                    @block.sync
                    def _(sp):
                        with sp.Fori(0, T // CH // 2) as i:
                            for b in range(2):
                                ts = bass.ds((2 * i + b) * CH, CH)
                                sp.wait_ge(free[b], at(free[b], 1 + i))
                                sp.dma_start(idx[b][:], src_rows[:, ts]).then_inc(loaded[b], 16)
                                sp.dma_start(a3[b][:], attr3[:, ts, :]).then_inc(loaded[b], 16)
                                sp.dma_start(a5[b][:], attr5[:, ts, :]).then_inc(loaded[b], 16)
                                sp.dma_start(s0[b][:], edge_w1[:, ts]).then_inc(loaded[b], 16)

                    @block.gpsimd
                    def _(pool):
                        with pool.Fori(0, T // CH // 2) as i:
                            for b in range(2):
                                pool.wait_ge(loaded[b], at(loaded[b], 64 * (i + 1)))
                                pool.sem_inc(chunks_begun, 1)
                                for t in range(CH):
                                    row_gather(pool, rows[b][:, t, :], table_l0, idx[b][:, t:t + 1]).then_inc(gathered[b], 16)

                    @block.vector
                    def _(v):
                        nc.vector.memset(tail[:], 0.0).then_inc(s_v, 1)
                        with v.Fori(0, T // CH // 2) as i:
                            for b in range(2):
                                start = at(s_v, 1) + (2 * i + b) * LINKS
                                link, count = chain(v, s_v, start)
                                v.wait_ge(s_v, start)
                                v.wait_ge(loaded[b], at(loaded[b], 64 * (i + 1)))
                                V = nc.vector
                                g = rows[b]
                                a1, a3v, a4, a5v = (g[:, :, c:c + 24].rearrange("p t (o k) -> p t o k", k=3) for c in (16, 40, 64, 88))
                                o0 = msg[b][:, :, 0:M]
                                o1 = msg[b][:, :, M:D].rearrange("p t (o k) -> p t o k", k=3)
                                y = a5[b]
                                V.tensor_scalar(bm[:, :, 0, 2], y[:, :, 0], A, None, ALU.mult)
                                V.tensor_scalar(bm[:, :, 2, 0], y[:, :, 0], A, None, ALU.mult)
                                V.tensor_scalar(bm[:, :, 0, 1], y[:, :, 1], A, None, ALU.mult)
                                V.tensor_scalar(bm[:, :, 1, 0], y[:, :, 1], A, None, ALU.mult)
                                V.tensor_scalar(bm[:, :, 1, 2], y[:, :, 3], A, None, ALU.mult)
                                V.tensor_scalar(bm[:, :, 2, 1], y[:, :, 3], A, None, ALU.mult)
                                V.tensor_scalar(bm[:, :, 1, 1], y[:, :, 2], 2 * B, None, ALU.mult)
                                V.tensor_scalar(tmp[:, :, 0, 0], y[:, :, 4], -A, None, ALU.mult)
                                link(V.tensor_scalar(tmp[:, :, 1, 0], y[:, :, 4], A, None, ALU.mult))
                                V.scalar_tensor_tensor(bm[:, :, 0, 0], y[:, :, 2], -B, tmp[:, :, 0, 0], ALU.mult, ALU.add)
                                link(V.scalar_tensor_tensor(bm[:, :, 2, 2], y[:, :, 2], -B, tmp[:, :, 1, 0], ALU.mult, ALU.add))
                                v.wait_ge(gathered[b], 16 * CH * (i + 1))

                                s_e = s0[b][:].rearrange("p (t a) -> p t a", a=1)
                                v_k = a3[b][:].rearrange("p t (a k) -> p t a k", a=1).to_broadcast([P, CH, M, 3])
                                link(V.tensor_tensor(tmp[:], a3v, v_k, ALU.mult))
                                link(V.tensor_reduce(o0, tmp[:], AX.X, ALU.add))
                                t0 = tmp[:, :, 0:M, 0]
                                link(V.tensor_tensor(t0, g[:, :, 0:M], s_e.to_broadcast([P, CH, M]), ALU.mult))
                                link(V.tensor_tensor(o0, o0, t0, ALU.add))
                                link(V.tensor_tensor(msg[b][:, :, M:D], g[:, :, 16:40], s_e.to_broadcast([P, CH, 24]), ALU.mult))
                                link(V.tensor_tensor(tmp[:], g[:, :, 8:16].rearrange("p t (o a) -> p t o a", a=1).to_broadcast([P, CH, M, 3]), v_k, ALU.mult))
                                link(V.tensor_tensor(o1, o1, tmp[:], ALU.add))
                                for j in range(3):
                                    link(V.tensor_tensor(tmp[:], a5v[:, :, :, j:j + 1].to_broadcast([P, CH, M, 3]),
                                                         bm[:, :, j:j + 1, :].to_broadcast([P, CH, M, 3]), ALU.mult))
                                    link(V.tensor_tensor(o1, o1, tmp[:], ALU.add))
                                for k in range(3):
                                    p1, p2 = (k + 1) % 3, (k + 2) % 3
                                    for n, (iv, ja, op) in enumerate(((p1, p2, ALU.add), (p2, p1, ALU.subtract))):
                                        link(V.tensor_tensor(tmp[:, :, :, n], a4[:, :, :, ja],
                                                             a3[b][:, :, iv:iv + 1].to_broadcast([P, CH, M]), ALU.mult))
                                        link(V.tensor_tensor(o1[:, :, :, k], o1[:, :, :, k], tmp[:, :, :, n], op))
                                link(scans(V, msg[b], same[:, bass.ds((2 * i + b) * CH, CH)], tail, D))
                                ins = V.tensor_copy(tail[:, 0:D], msg[b][:, CH - 1, :])
                                count[0] += 1
                                ins.then_inc(s_v, 1)
                                links[0] = count[0]
                        assert links[0] == LINKS, links

                    @block.scalar
                    def _(act):
                        for b in range(2):
                            act.sem_inc(free[b], 1)
                        with act.Fori(0, T // CH // 2) as i:
                            for b in range(2):
                                act.wait_ge(s_v, at(s_v, 1) + (2 * i + b + 1) * LINKS)
                                act.dma_start(z[:, bass.ds((2 * i + b) * CH, CH), :], msg[b][:]).then_inc(stored[b], 16)
                                act.wait_ge(stored[b], at(stored[b], 16 * (i + 1)))
                                act.sem_inc(free[b], 1)
            n = T // CH // 2
            close(s_v, 1 + 2 * n * LINKS)
            for b in range(2):
                close(free[b], 1 + n)
                close(loaded[b], 64 * n)
                close(stored[b], 16 * n)

        links = [0]

        def residual_norm_stage(tag, rows, n, write_table, last=False, scale_table=False):
            with ExitStack() as st:
                banks = [st.enter_context(nc.psum_tensor(f"pc_{tag}{b}", [P, 512], F32)) for b in range(2)]
                with nc.Block() as block:
                    @block.gpsimd
                    def _(pool):
                        fetch_sums(pool, rows, n)
                        if write_table == "start":
                            scatter_starts(pool, x_cur, at(s_vdone, 3))

                    @block.tensor
                    def _(pe):
                        crossing_matmuls(pe, banks, n)

                    @block.vector
                    def _(v):
                        start = at(s_v, 0)
                        link, count = chain(v, s_v, start)
                        finish_sums(v, link, banks, n)
                        a = agg[:, 0:NJ * n].rearrange("p (j f) -> p j f", f=n)
                        if n == D:
                            link(nc.vector.tensor_tensor(x_cur[:], x_cur[:], a, ALU.add))
                        else:
                            link(nc.vector.tensor_scalar(stat[:, :, 0], nonempty[:], -1.0, 1.0, ALU.mult, ALU.add))
                            link(nc.vector.tensor_tensor(stat[:, :, 0], stat[:, :, 0], a[:, :, D], ALU.add))
                            link(nc.vector.reciprocal(stat[:, :, 1], stat[:, :, 0]))
                            link(nc.vector.tensor_tensor(sq[:], a[:, :, 0:D], stat[:, :, 1:2].to_broadcast([P, NJ, D]), ALU.mult))
                            link(nc.vector.scalar_tensor_tensor(sq[:], sq[:], 0.01, sq[:], ALU.mult, ALU.max))
                            link(nc.vector.tensor_tensor(x_cur[:], x_cur[:], sq[:], ALU.add))
                        layer_norm(v, link, x_cur[:], at(s_act, 1))
                        if scale_table:
                            link(nc.vector.tensor_tensor(sq[:], x_cur[:], by_col(dinv[:]), ALU.mult))
                        v.sem_inc(s_vdone, 1)
                        close(s_v, count[0])

                    @block.scalar
                    def _(act):
                        norm_root(act, at(s_vdone, 2))

                    @block.sync
                    def _(sp):
                        sp.wait_ge(s_vdone, at(s_vdone, 3))
                        dest = out if last else table.rearrange("(p j) f -> p j f", p=P)
                        sp.dma_start(dest, sq[:] if scale_table else x_cur[:]).then_inc(s_write, 16)
                        sp.wait_ge(s_write, at(s_write, 16))
            sums_closed()
            close(s_vdone, 2)
            close(s_act, 1)
            close(s_write, 16)
            if write_table == "start":
                close(s_scatter, 16 * NJ)

        def scatter_starts(pool, nodes, ready):
            pool.wait_ge(s_vdone, ready)
            for j in range(NJ):
                pool.indirect_dma_start(out=start_rows, out_offset=bass.IndirectOffsetOnAxis(ap=start_i[:, j:j + 1], axis=0),
                                        in_=nodes[:, j, :], in_offset=None, bounds_check=EP - 1,
                                        oob_is_err=False).then_inc(s_scatter, 16)
            pool.wait_ge(s_scatter, at(s_scatter, 16 * NJ))

        def cheb_step_stage(tag, x0, x1, x2, first):
            with ExitStack() as st:
                banks = [st.enter_context(nc.psum_tensor(f"pc_{tag}{b}", [P, 512], F32)) for b in range(2)]
                with nc.Block() as block:
                    @block.gpsimd
                    def _(pool):
                        fetch_sums(pool, scanned_rows, D)

                    @block.tensor
                    def _(pe):
                        crossing_matmuls(pe, banks, D)

                    @block.vector
                    def _(v):
                        start = at(s_v, 0)
                        link, count = chain(v, s_v, start)
                        finish_sums(v, link, banks, D)
                        a = agg[:, 0:NJ * D].rearrange("p (j f) -> p j f", f=D)
                        link(nc.vector.tensor_tensor(a, a, by_col(dinv[:]), ALU.mult))
                        if first:
                            link(nc.vector.tensor_scalar(a, a, lam_c[:, 0:1], None, ALU.mult))
                            link(nc.vector.scalar_tensor_tensor(x1[:], x0[:], lam_c[:, 1:2], a, ALU.mult, ALU.add))
                            link(nc.vector.tensor_tensor(sq[:], x1[:], by_col(dinv[:]), ALU.mult))
                        else:
                            link(nc.vector.tensor_scalar(a, a, lam_c[:, 2:3], None, ALU.mult))
                            link(nc.vector.scalar_tensor_tensor(x2[:], x1[:], lam_c[:, 3:4], a, ALU.mult, ALU.add))
                            link(nc.vector.tensor_tensor(x2[:], x2[:], x0[:], ALU.subtract))
                        v.sem_inc(s_vdone, 1)
                        close(s_v, count[0])

                    @block.sync
                    def _(sp):
                        if first:
                            sp.wait_ge(s_vdone, at(s_vdone, 2))
                            sp.dma_start(table.rearrange("(p j) f -> p j f", p=P), sq[:]).then_inc(s_write, 16)
                            sp.wait_ge(s_write, at(s_write, 16))
            sums_closed()
            close(s_vdone, 1)
            if first:
                close(s_write, 16)

        def cheb_mix_stage(tag, xs, dest, gat=None):
            with ExitStack() as st:
                def sb(name, shape, dt=F32):
                    return st.enter_context(nc.sbuf_tensor(f"{name}_{tag}", shape, dt))
                wc = [sb(f"wc{k}", [P, 4 * D]) for k in range(3)]
                bias = sb("bias", [P, D])
                wg = sb("wg", [P, 8 * D])
                gbias = sb("gbias", [P, 2 * D])
                both = sb("both", [P, NJ, 2 * D])
                pt = [st.enter_context(nc.psum_tensor(f"pt_{tag}{b}", [P, 512], F32)) for b in range(2)]
                po = [st.enter_context(nc.psum_tensor(f"po_{tag}{b}", [P, 512], F32)) for b in range(2)]
                xt = [sb(f"xt{b}", [P, 3 * P]) for b in range(2)]
                n_in = 4 + (4 if gat else 0)

                def row(a):
                    return a.rearrange("(a n) -> a n", a=1).to_broadcast([P, D])
                with nc.Block() as block:
                    @block.sync
                    def _(sp):
                        sp.wait_ge(s_vdone, at(s_vdone, 1))
                        for k in range(3):
                            sp.dma_start(wc[k][0:D, 0:D], cheb_w[k * D:(k + 1) * D, :]).then_inc(s_in, 16)
                        sp.dma_start(bias[:], row(cheb_b)).then_inc(s_in, 16)
                        if gat:
                            sp.dma_start(wg[0:D, 0:D], gat_ws).then_inc(s_in, 16)
                            sp.dma_start(wg[0:D, D:2 * D], gat_wd).then_inc(s_in, 16)
                            sp.dma_start(gbias[:, 0:D], row(gat_bs)).then_inc(s_in, 16)
                            sp.dma_start(gbias[:, D:2 * D], row(gat_bd)).then_inc(s_in, 16)
                        sp.wait_ge(s_in, at(s_in, 16 * n_in))
                        for k in range(3):
                            replicate(sp, wc[k], D)
                        replicate(sp, wg, 2 * D) if gat else None
                        sp.wait_ge(s_vdone, at(s_vdone, 2))
                        if not gat:
                            sp.dma_start(table.rearrange("(p j) f -> p j f", p=P), sq[:]).then_inc(s_write, 16)
                            sp.wait_ge(s_write, at(s_write, 16 * 10))

                    @block.tensor
                    def _(pe):
                        pe.wait_ge(s_write, at(s_write, 16 * (12 if gat else 9)))
                        linear_pe(pe, xs, wc, D, pt, xt, po)

                    @block.scalar
                    def _(act):
                        linear_act(act, 3, pt, xt)

                    @block.vector
                    def _(v):
                        start = at(s_v, 0)
                        link, count = chain(v, s_v, start)
                        for w in wc:
                            nc.vector.memset(w[:], 0.0)
                        nc.vector.memset(wg[:], 0.0).then_inc(s_vdone, 1)
                        v.wait_ge(s_in, at(s_in, 16 * n_in))
                        linear_out(v, dest, D, po, bias)
                        link(nc.vector.scalar_tensor_tensor(dest[:], dest[:], 0.01, dest[:], ALU.mult, ALU.max))
                        ins = nc.vector.tensor_tensor(sq[:], dest[:], by_col(dinv[:]), ALU.mult)
                        ins.then_inc(s_vdone, 1)
                        close(s_v, count[0])
                close(s_in, 16 * n_in)
                close(s_write, 16 * (12 if gat else 10))
                close(s_vdone, 2)
                linear_closed()
                if gat:
                    with nc.Block() as block:
                        @block.tensor
                        def _(pe):
                            linear_pe(pe, [dest], [wg], 2 * D, pt, xt, po)

                        @block.scalar
                        def _(act):
                            linear_act(act, 1, pt, xt)

                        @block.vector
                        def _(v):
                            linear_out(v, both, 2 * D, po, gbias)
                            start = at(s_v, 0)
                            link, count = chain(v, s_v, start)
                            link(nc.vector.tensor_copy(sq[:], both[:, :, D:2 * D]))
                            v.sem_inc(s_vdone, 1)
                            close(s_v, count[0])

                        @block.gpsimd
                        def _(pool):
                            scatter_starts(pool, sq, at(s_vdone, 1))
                            pool.wait_ge(s_write, at(s_write, 16))
                            row_gather(pool, fill[:], table, first_row[:]).then_inc(s_agg, 16)
                            pool.wait_ge(s_agg, at(s_agg, 16))

                        @block.sync
                        def _(sp):
                            sp.wait_ge(s_vdone, at(s_vdone, 1))
                            sp.dma_start(table.rearrange("(p j) f -> p j f", p=P), sq[:]).then_inc(s_write, 16)
                            sp.wait_ge(s_agg, at(s_agg, 16))
                            sp.dma_start(table.rearrange("(p j) f -> p j f", p=P), both[:, :, 0:D]).then_inc(s_write, 16)
                            sp.wait_ge(s_write, at(s_write, 32))
                    linear_closed()
                    close(s_vdone, 1)
                    close(s_agg, 16)
                    close(s_write, 32)
                    close(s_scatter, 16 * NJ)

        def gat_logit_pass(logit):
            CH = C_MSG
            gathered = gather_signals("gat")
            with ExitStack() as st:
                def sb(name, shape, dt=F32):
                    return st.enter_context(nc.sbuf_tensor(name, shape, dt))
                idx = [sb(f"idx_gat{b}", [P, CH], I32) for b in range(2)]
                rows = [sb(f"g_gat{b}", [P, CH, D]) for b in range(2)]
                fd = [sb(f"fd_gat{b}", [P, CH, D]) for b in range(2)]
                attn = sb("attn", [P, D])
                zg = gathered_rows.rearrange("(p t) f -> p t f", p=P)
                sr = start_rows.rearrange("(p t) f -> p t f", p=P)
                LINKS = 6
                with nc.Block() as block:
                    @block.sync
                    def _(sp):
                        sp.dma_start(attn[:], gat_attn.to_broadcast([P, D])).then_inc(s_in, 16)
                        with sp.Fori(0, T // CH // 2) as i:
                            for b in range(2):
                                ts = bass.ds((2 * i + b) * CH, CH)
                                sp.wait_ge(free[b], at(free[b], 1 + i))
                                sp.dma_start(idx[b][:], src_rows[:, ts]).then_inc(loaded[b], 16)
                                sp.dma_start(fd[b][:], sr[:, ts, :]).then_inc(loaded[b], 16)

                    @block.gpsimd
                    def _(pool):
                        with pool.Fori(0, T // CH // 2) as i:
                            for b in range(2):
                                pool.wait_ge(loaded[b], at(loaded[b], 32 * (i + 1)))
                                pool.sem_inc(chunks_begun, 1)
                                for t in range(CH):
                                    row_gather(pool, rows[b][:, t, :], table, idx[b][:, t:t + 1]).then_inc(gathered[b], 16)

                    @block.vector
                    def _(v):
                        V = nc.vector
                        v.wait_ge(s_in, at(s_in, 16))
                        V.memset(tail[:], 0.0).then_inc(s_v, 1)
                        with v.Fori(0, T // CH // 2) as i:
                            for b in range(2):
                                start = at(s_v, 1) + (2 * i + b) * LINKS
                                link, count = chain(v, s_v, start)
                                v.wait_ge(s_v, start)
                                v.wait_ge(loaded[b], at(loaded[b], 32 * (i + 1)))
                                ts = bass.ds((2 * i + b) * CH, CH)
                                link(scans(V, fd[b], same[:, ts], fill, D))
                                link(V.tensor_copy(fill[:], fd[b][:, CH - 1, :]))
                                v.wait_ge(gathered[b], 16 * CH * (i + 1))
                                link(V.tensor_tensor(fd[b][:], fd[b][:], rows[b][:], ALU.add))
                                link(V.scalar_tensor_tensor(fd[b][:], fd[b][:], 0.2, fd[b][:], ALU.mult, ALU.max))
                                link(V.tensor_tensor(fd[b][:], fd[b][:], attn[:].rearrange("p (a f) -> p a f", a=1).to_broadcast([P, CH, D]), ALU.mult))
                                V.tensor_reduce(logit[:, ts], fd[b][:], AX.X, ALU.add).then_inc(s_v, 1)
                                assert count[0] + 1 == LINKS

                    @block.scalar
                    def _(act):
                        for b in range(2):
                            act.sem_inc(free[b], 1)
                        with act.Fori(0, T // CH // 2) as i:
                            for b in range(2):
                                act.wait_ge(s_v, at(s_v, 1) + (2 * i + b + 1) * LINKS)
                                act.dma_start(zg[:, bass.ds((2 * i + b) * CH, CH), :], rows[b][:]).then_inc(stored[b], 16)
                                act.wait_ge(stored[b], at(stored[b], 16 * (i + 1)))
                                act.sem_inc(free[b], 1)
            n = T // CH // 2
            close(s_in, 16)
            close(s_v, 1 + 2 * n * LINKS)
            for b in range(2):
                close(free[b], 1 + n)
                close(loaded[b], 32 * n)
                close(stored[b], 16 * n)

        def gat_max_stage(logit, st):
            def sb(name, shape, dt=F32):
                return st.enter_context(nc.sbuf_tensor(name, shape, dt))
            pen = sb("pen", [P, T])
            top_f = sb("top_f", [P, T])
            work = sb("work_gat", [P, T])
            cols = sb("cols", [P, 4])
            diag = sb("diag", [P, 4, P])
            cand = sb("cand", [P, 4, P])
            mask = sb("mask", [P, 4, P])
            tops = sb("tops", [P, 2])
            with ExitStack() as pst:
                pr = pst.enter_context(nc.psum_tensor("pr", [P, 4, P], F32))
                with nc.Block() as block:
                    @block.vector
                    def _(v):
                        V = nc.vector
                        start = at(s_v, 0)
                        link, count = chain(v, s_v, start)
                        link(V.tensor_scalar(pen[:], same[:], BIG, -BIG, ALU.mult, ALU.add))
                        link(V.tensor_tensor_scan(top_f[:], pen[:], logit[:], -BIG, ALU.add, ALU.max))
                        link(V.memset(work[:, T - 1:T], -BIG))
                        link(V.tensor_copy(work[:, 0:T - 1], pen[:, 1:T]))
                        link(V.tensor_tensor_scan(top_f[:, ::-1], work[:, ::-1], top_f[:, ::-1], -BIG, ALU.add, ALU.max))
                        link(V.tensor_copy(cols[:, 0:1], first_f[:]))
                        link(V.tensor_copy(cols[:, 1:2], last_f[:]))
                        link(V.tensor_copy(cols[:, 2:3], top_f[:, 0:1]))
                        link(V.tensor_copy(cols[:, 3:4], top_f[:, T - 1:T]))
                        for k in range(4):
                            ins = V.tensor_scalar(diag[:, k, :], ident[:], cols[:, k:k + 1], None, ALU.mult)
                        ins.then_inc(s_vdone, 1)
                        v.wait_ge(s_pe, at(s_pe, 1))
                        for k in range(2):
                            for h in range(2):
                                link(V.tensor_scalar(mask[:, 2 * k + h, :], pr[:, h, :], cols[:, k:k + 1], None, ALU.is_equal))
                                link(V.tensor_tensor(cand[:, 2 * k + h, :], mask[:, 2 * k + h, :], pr[:, 2 + h, :], ALU.mult))
                                link(V.tensor_scalar(mask[:, 2 * k + h, :], mask[:, 2 * k + h, :], BIG, -BIG, ALU.mult, ALU.add))
                                link(V.tensor_tensor(cand[:, 2 * k + h, :], cand[:, 2 * k + h, :], mask[:, 2 * k + h, :], ALU.add))
                        for k in range(2):
                            link(V.tensor_reduce(tops[:, k:k + 1], cand[:, 2 * k:2 * k + 2, :].rearrange("p a q -> p (a q)"), AX.X, ALU.max))
                            link(V.tensor_scalar(work[:], dst_f[:], cols[:, k:k + 1], None, ALU.is_equal))
                            link(V.tensor_scalar(pen[:], work[:], BIG, -BIG, ALU.mult, ALU.add))
                            link(V.scalar_tensor_tensor(work[:], work[:], tops[:, k:k + 1], pen[:], ALU.mult, ALU.add))
                            link(V.tensor_tensor(top_f[:], top_f[:], work[:], ALU.max))
                        V.tensor_tensor(logit[:], logit[:], top_f[:], ALU.subtract).then_inc(s_vdone, 1)
                        close(s_v, count[0])

                    @block.tensor
                    def _(pe):
                        pe.wait_ge(s_vdone, at(s_vdone, 1))
                        nc.tensor.matmul(pr[:].rearrange("p a q -> p (a q)"), ones[:], diag[:].rearrange("p a q -> p (a q)"),
                                         start=True, stop=True).then_inc(s_pe, 1)

                    @block.scalar
                    def _(act):
                        act.wait_ge(s_vdone, at(s_vdone, 2))
                        nc.scalar.activation(logit[:], logit[:], ACT.Exp).then_inc(s_act, 1)
            close(s_vdone, 2)
            close(s_pe, 1)
            close(s_act, 1)

        def gat_sum_pass(weight):
            CH = C_MSG
            with ExitStack() as st:
                def sb(name, shape, dt=F32):
                    return st.enter_context(nc.sbuf_tensor(name, shape, dt))
                rows = [sb(f"g_gs{b}", [P, CH, D]) for b in range(2)]
                prod = [sb(f"prod_gs{b}", [P, CH, D + 1]) for b in range(2)]
                zg = gathered_rows.rearrange("(p t) f -> p t f", p=P)
                z = scanned_rows33.rearrange("(p t) f -> p t f", p=P)
                with nc.Block() as block:
                    @block.sync
                    def _(sp):
                        with sp.Fori(0, T // CH // 2) as i:
                            for b in range(2):
                                ts = bass.ds((2 * i + b) * CH, CH)
                                sp.wait_ge(free[b], at(free[b], 1 + i))
                                sp.dma_start(rows[b][:], zg[:, ts, :]).then_inc(loaded[b], 16)

                    @block.vector
                    def _(v):
                        V = nc.vector
                        V.memset(tail[:], 0.0).then_inc(s_v, 1)
                        with v.Fori(0, T // CH // 2) as i:
                            for b in range(2):
                                ts = bass.ds((2 * i + b) * CH, CH)
                                k = at(s_v, 1) + 6 * i + 3 * b
                                v.wait_ge(s_v, k)
                                v.wait_ge(loaded[b], at(loaded[b], 16 * (i + 1)))
                                w = weight[:, ts].rearrange("p (t a) -> p t a", a=1)
                                V.tensor_copy(prod[b][:, :, D:D + 1], w)
                                V.tensor_tensor(prod[b][:, :, 0:D], rows[b][:], w.to_broadcast([P, CH, D]), ALU.mult).then_inc(s_v, 1)
                                v.wait_ge(s_v, k + 1)
                                scans(V, prod[b], same[:, ts], tail, D + 1).then_inc(s_v, 1)
                                v.wait_ge(s_v, k + 2)
                                V.tensor_copy(tail[:], prod[b][:, CH - 1, :]).then_inc(s_v, 1)

                    @block.scalar
                    def _(act):
                        for b in range(2):
                            act.sem_inc(free[b], 1)
                        with act.Fori(0, T // CH // 2) as i:
                            for b in range(2):
                                act.wait_ge(s_v, at(s_v, 4) + 6 * i + 3 * b)
                                act.dma_start(z[:, bass.ds((2 * i + b) * CH, CH), :], prod[b][:]).then_inc(stored[b], 16)
                                act.wait_ge(stored[b], at(stored[b], 16 * (i + 1)))
                                act.sem_inc(free[b], 1)
            n = T // CH // 2
            close(s_v, 1 + 6 * n)
            for b in range(2):
                close(free[b], 1 + n)
                close(loaded[b], 16 * n)
                close(stored[b], 16 * n)

        def l2_pass():
            CH = C_MSG
            NZ = 80
            NG = 6
            NT = NG * 16 * M
            GAIN = 1.593
            PW_S, PW_V = 0.17677669529663687, 0.25
            KAP = math.sqrt(2.0) / math.sqrt(10.0) / 4.0
            gathered = gather_signals("l2")
            with ExitStack() as st:
                def sb(name, shape, dt=F32):
                    return st.enter_context(nc.sbuf_tensor(name, shape, dt))

                def ps(name, shape):
                    return st.enter_context(nc.psum_tensor(name, shape, F32))
                wz = sb("wz", [NZ, NG, 16 * M])
                we = sb("we", [NZ, 3, 16 * M])
                idx = [sb(f"idx_l2{b}", [P, CH], I32) for b in range(2)]
                z = [sb(f"z_l2{b}", [P, CH, NZ]) for b in range(2)]
                hid = [sb(f"h_l2{b}", [P, CH, 16]) for b in range(2)]
                vec = [sb(f"vec{b}", [P, CH, 3]) for b in range(2)]
                ew = [sb(f"ew{b}", [P, CH]) for b in range(2)]
                msg = [sb(f"msg_l2{b}", [P, CH, D]) for b in range(2)]
                nrm = sb("nrm", [P, CH, 4])
                pv = sb("pv", [P, CH, 2 * M, 3])
                res = sb("res", [P, CH, NG, M])
                th = sb("th", [P, CH, 2 * M])
                zt = [sb(f"zt{b}", [NZ, 4 * P]) for b in range(2)]
                prod = [sb(f"prod{b}", [P, 2 * NG, 16, M]) for b in range(2)]
                p_z = [ps(f"p_z{b}", [P, 512]) for b in range(2)]
                p_t = [ps(f"p_t{b}", [P, 3 * 512]) for b in range(2)]
                zt_ready = signal("zt_ready")
                z_done = signal("z_done")
                transposed = signal("transposed")
                t_made = signal("t_made")
                t_used = signal("t_used")
                zt_used = signal("zt_used")
                res_done = signal("res_done")
                th_done = signal("th_done")
                n_done = signal("n_done")
                zr = scanned_rows.rearrange("(p t) f -> p t f", p=P)
                sr = start_rows.rearrange("(p t) f -> p t f", p=P)
                w2v = w2.rearrange("k (i u w) -> i u k w", i=7, u=16)

                with nc.Block() as block:
                    plan = []
                    for g, iw in ((0, 0), (1, 2), (2, 4)):
                        plan += [(wz, g, 0, 1, iw, 0), (wz, g, 32, 1, iw, 8)]
                    for g, iw in ((0, 1), (1, 3), (2, 6)):
                        plan += [(wz, g, 64, 1, iw, 0), (wz, g, 72, 1, iw, 8)]
                    for c in range(3):
                        plan += [(wz, 3 + c, 8 + c, 3, 5, 0), (wz, 3 + c, 40 + c, 3, 5, 8)]
                        plan += [(we, c, 8 + c, 3, 6, 0), (we, c, 40 + c, 3, 6, 8)]

                    @block.sync
                    def _(sp):
                        sp.wait_ge(s_vdone, at(s_vdone, 2))
                        with nc.allow_non_contiguous_dma(reason="weights, in runs of 8"):
                            for t, g, r, step, iw, u in plan:
                                sp.dma_start(t[r:r + 7 * step + 1:step, g, :].rearrange("u (k w) -> u k w", w=M),
                                             w2v[iw, u:u + 8]).then_inc(s_in, 16)

                    @block.gpsimd
                    def _(pool):
                        row_gather(pool, fill[:], table, first_row[:]).then_inc(s_agg, 16)
                        pool.wait_ge(s_agg, at(s_agg, 16))

                    @block.vector
                    def _(v):
                        V = nc.vector
                        V.memset(wz[:], 0.0).then_inc(s_vdone, 1)
                        V.memset(we[:], 0.0).then_inc(s_vdone, 1)
                        v.wait_ge(s_in, at(s_in, 16 * len(plan)))
                        start = at(s_v, 0)
                        link, count = chain(v, s_v, start)
                        link(V.tensor_scalar(wz[:, 0:2, :], wz[:, 0:2, :], KAP * PW_S, None, ALU.mult))
                        link(V.tensor_scalar(wz[0:64, 2, :], wz[0:64, 2, :], KAP * PW_V, None, ALU.mult))
                        link(V.tensor_scalar(wz[64:80, 2, :], wz[64:80, 2, :], KAP * PW_V * math.sqrt(1.5), None, ALU.mult))
                        link(V.tensor_scalar(wz[:, 3:6, :], wz[:, 3:6, :], KAP * PW_V / math.sqrt(3.0), None, ALU.mult))
                        link(V.scalar_tensor_tensor(wz[:, 3:6, :], we[:], -KAP * PW_V * math.sqrt(1.5) / 3.0, wz[:, 3:6, :], ALU.mult, ALU.add))
                        close(s_v, count[0])
                close(s_in, 16 * len(plan))
                close(s_vdone, 2)
                close(s_agg, 16)

                LINKS = 14
                Q = CH // 4
                with nc.Block() as block:
                    @block.sync
                    def _(sp):
                        with sp.Fori(0, T // CH // 2) as i:
                            for b in range(2):
                                ts = bass.ds((2 * i + b) * CH, CH)
                                sp.wait_ge(free[b], at(free[b], 1 + i))
                                sp.dma_start(idx[b][:], src_rows[:, ts]).then_inc(loaded[b], 16)
                                sp.dma_start(z[b][:, :, D:2 * D], sr[:, ts, :]).then_inc(loaded[b], 16)
                                sp.dma_start(hid[b][:], hidden[:, ts, :]).then_inc(loaded[b], 16)
                                sp.dma_start(vec[b][:], attr3[:, ts, :]).then_inc(loaded[b], 16)
                                sp.dma_start(ew[b][:], edge_w[:, ts]).then_inc(loaded[b], 16)

                    @block.gpsimd
                    def _(pool):
                        with pool.Fori(0, T // CH // 2) as i:
                            for b in range(2):
                                pool.wait_ge(loaded[b], at(loaded[b], 80 * (i + 1)))
                                pool.sem_inc(chunks_begun, 1)
                                for t in range(CH):
                                    row_gather(pool, z[b][:, t, 0:D], table, idx[b][:, t:t + 1]).then_inc(gathered[b], 16)

                    @block.tensor
                    def _(pe):
                        with pe.Fori(0, T // CH // 2) as i:
                            for b in range(2):
                                c = 2 * i + b
                                pe.wait_ge(z_done, c + 1)

                                def transposes(q):
                                    pe.wait_ge(zt_ready, c * Q + q + 1)
                                    for t in range(4):
                                        last = nc.tensor.transpose(p_z[q % 2][0:NZ, t * P:(t + 1) * P],
                                                                   z[b][:, 4 * q + t, :], ident[:])
                                    last.then_inc(transposed, 1)

                                transposes(0)
                                for q in range(Q):
                                    if q + 1 < Q:
                                        transposes(q + 1)
                                    pe.wait_ge(zt_ready, c * Q + q + 3)
                                    for pair in range(2):
                                        pe.wait_ge(t_used, 2 * (c * Q + q) + pair + 1)
                                        for t in range(2):
                                            lhs = zt[q % 2][:, (2 * pair + t) * P:(2 * pair + t + 1) * P]
                                            cuts = ((0, 512), (512, NT)) if t == 0 else ((0, 256), (256, NT))
                                            for a, e in cuts:
                                                last = nc.tensor.matmul(p_t[pair][:, t * NT + a:t * NT + e], lhs,
                                                                        wz[:].rearrange("z g k -> z (g k)")[:, a:e],
                                                                        start=True, stop=True)
                                        last.then_inc(t_made, 1)

                    @block.scalar
                    def _(act):
                        for b in range(2):
                            act.sem_inc(free[b], 1)
                        act.sem_inc(zt_ready, 2)
                        with act.Fori(0, T // CH // 2) as i:
                            for b in range(2):
                                c = 2 * i + b
                                act.wait_ge(n_done, c + 1)
                                nc.scalar.activation(nrm[:, :, 3], nrm[:, :, 3], ACT.Sqrt).then_inc(s_act, 1)
                                for q in range(Q):
                                    act.wait_ge(transposed, c * Q + q + 1)
                                    if q >= 2:
                                        act.wait_ge(t_made, 2 * (c * Q + q - 1))
                                    nc.scalar.activation(zt[q % 2][:], p_z[q % 2][0:NZ, :], ACT.Copy).then_inc(zt_ready, 1)
                                act.wait_ge(res_done, c + 1)
                                nc.scalar.activation(th[:], res[:, :, 0:2, :].rearrange("p t g w -> p t (g w)"),
                                                     ACT.Tanh).then_inc(th_done, 1)
                                act.wait_ge(s_v, at(s_v, 1) + (c + 1) * LINKS)
                                act.dma_start(zr[:, bass.ds(c * CH, CH), :], msg[b][:]).then_inc(stored[b], 16)
                                act.wait_ge(stored[b], at(stored[b], 16 * (i + 1)))
                                act.sem_inc(free[b], 1)

                    @block.vector
                    def _(v):
                        V = nc.vector
                        V.memset(tail[:], 0.0).then_inc(s_v, 1)
                        V.memset(th[:], 0.0).then_inc(t_used, 2)
                        with v.Fori(0, T // CH // 2) as i:
                            for b in range(2):
                                c = 2 * i + b
                                ts = bass.ds(c * CH, CH)
                                start = at(s_v, 1) + c * LINKS
                                link, count = chain(v, s_v, start)
                                v.wait_ge(s_v, start)
                                v.wait_ge(loaded[b], at(loaded[b], 80 * (i + 1)))
                                link(V.tensor_tensor(pv[:, :, 0, :], vec[b][:], vec[b][:], ALU.mult))
                                V.tensor_reduce(nrm[:, :, 3], pv[:, :, 0, :], AX.X, ALU.add).then_inc(n_done, 1)
                                link(scans(V, z[b][:, :, D:2 * D], same[:, ts], fill, D))
                                link(V.tensor_copy(fill[:], z[b][:, CH - 1, D:2 * D]))
                                v.wait_ge(s_act, at(s_act, c + 1))
                                link(V.reciprocal(nrm[:, :, 0], nrm[:, :, 3]))
                                link(V.tensor_tensor(vec[b][:], vec[b][:], nrm[:, :, 0:1].to_broadcast([P, CH, 3]), ALU.mult))
                                n_i = vec[b][:].rearrange("p t (a i) -> p t a i", a=1).to_broadcast([P, CH, M, 3])
                                v.wait_ge(gathered[b], 16 * CH * (i + 1))
                                V.tensor_tensor(pv[:, :, 0:M, :], z[b][:, :, M:D].rearrange("p t (m i) -> p t m i", i=3), n_i, ALU.mult)
                                link(V.tensor_tensor(pv[:, :, M:2 * M, :], z[b][:, :, D + M:2 * D].rearrange("p t (m i) -> p t m i", i=3), n_i, ALU.mult))
                                V.tensor_reduce(z[b][:, :, 2 * D:NZ], pv[:], AX.X, ALU.add).then_inc(z_done, 1)
                                for u in range(CH // 2):
                                    v.wait_ge(t_made, c * (CH // 2) + u + 1)
                                    for t in range(2):
                                        h = hid[b][:, 2 * u + t, :].rearrange("p (a k e) -> p a k e", a=1, e=1).to_broadcast([P, NG, 16, M])
                                        ins = V.tensor_tensor(prod[u % 2][:, t * NG:(t + 1) * NG],
                                                              p_t[u % 2][:, t * NT:(t + 1) * NT].rearrange("p (g k w) -> p g k w", g=NG, k=16), h, ALU.mult)
                                    ins.then_inc(t_used, 1)
                                    v.wait_ge(t_used, c * (CH // 2) + u + 3)
                                    ins = V.tensor_reduce(res[:, 2 * u:2 * u + 2, :, :].rearrange("p t g w -> p (t g) w"),
                                                          prod[u % 2][:].rearrange("p g k w -> p g w k"), AX.X, ALU.add)
                                ins.then_inc(res_done, 1)
                                v.wait_ge(res_done, c + 1)
                                o1 = msg[b][:, :, M:D].rearrange("p t (w k) -> p t w k", k=3)
                                link(V.tensor_tensor(o1, res[:, :, 2, :].rearrange("p t (w a) -> p t w a", a=1).to_broadcast([P, CH, M, 3]), n_i, ALU.mult))
                                link(V.tensor_tensor(o1, o1, res[:, :, 3:6, :].rearrange("p t k w -> p t w k"), ALU.add))
                                link(V.tensor_scalar(ew[b][:], ew[b][:], GAIN, None, ALU.mult))
                                v.wait_ge(th_done, c + 1)
                                link(V.tensor_tensor(o1, o1, th[:, :, M:2 * M].rearrange("p t (w a) -> p t w a", a=1).to_broadcast([P, CH, M, 3]), ALU.mult))
                                link(V.tensor_copy(msg[b][:, :, 0:M], th[:, :, 0:M]))
                                link(V.tensor_tensor(msg[b][:], msg[b][:], ew[b][:].rearrange("p (t a) -> p t a", a=1).to_broadcast([P, CH, D]), ALU.mult))
                                link(scans(V, msg[b], same[:, ts], tail, D))
                                V.tensor_copy(tail[:, 0:D], msg[b][:, CH - 1, :]).then_inc(s_v, 1)
                                links[0] = count[0] + 1
                        assert links[0] == LINKS, links
            n = T // CH // 2
            close(s_v, 1 + 2 * n * LINKS)
            close(s_act, 2 * n)
            for b in range(2):
                close(free[b], 1 + n)
                close(loaded[b], 80 * n)
                close(stored[b], 16 * n)

        prepare()
        l0_table()
        l0_pass()
        residual_norm_stage("l0", scanned_rows, D, "plain", scale_table=True)
        with ExitStack() as st:
            x1 = st.enter_context(nc.sbuf_tensor("cheb_x1", [P, NJ, D], F32))
            x2 = st.enter_context(nc.sbuf_tensor("cheb_x2", [P, NJ, D], F32))
            h = st.enter_context(nc.sbuf_tensor("cheb_h", [P, NJ, D], F32))
            for r, x0 in enumerate((x_cur, h)):
                sum_pass(f"cheb{r}a")
                cheb_step_stage(f"cs{r}a", x0, x1, x2, True)
                sum_pass(f"cheb{r}b")
                cheb_step_stage(f"cs{r}b", x0, x1, x2, False)
                cheb_mix_stage(f"mix{r}", [x0, x1, x2], h, gat=(r == 1))
        with ExitStack() as st:
            logit = st.enter_context(nc.sbuf_tensor("logit", [P, T], F32))
            gat_logit_pass(logit)
            with ExitStack() as st2:
                gat_max_stage(logit, st2)
            gat_sum_pass(logit)
        residual_norm_stage("gat", scanned_rows33, D + 1, "start")
        l2_pass()
        residual_norm_stage("l2", scanned_rows, D, "plain")
        sum_pass("l3")
        residual_norm_stage("l3", scanned_rows, D, "plain", last=True)


def kernel(**inputs):
    import numpy as np
    import concourse.bacc as bacc
    from concourse.bass_utils import run_bass_kernel_spmd as run

    a = {k: np.asarray(v) for k, v in inputs.items()}
    n_nodes, n_edges = a["x"].shape[0], a["src"].shape[0]
    NJ, T = shapes(n_nodes, n_edges)

    def by_edge(v, pad):
        full = np.full((P * T,) + v.shape[1:], pad, v.dtype)
        full[:n_edges] = v
        return full.reshape((P, T) + v.shape[1:])

    x = np.zeros((NJ * P, D), a["x"].dtype)
    x[:n_nodes] = a["x"]
    emb = by_edge(a["edge_attr_10"], 0)
    arrays = {
        "x": np.ascontiguousarray(x.reshape(NJ, P, D).transpose(1, 0, 2)),
        "src": by_edge(a["src"], 0),
        "dst": by_edge(a["dst"], n_nodes),
        "emb_t": np.ascontiguousarray(emb.transpose(2, 1, 0)).reshape(10, T * P),
        "attr3": by_edge(a["edge_attr_3"], 1),
        "attr5": by_edge(a["edge_attr_5"], 0),
        "edge_w": by_edge(a["edge_weight"], 0),
        "edge_w1": by_edge(a["edge_weight1"].reshape(-1), 0),
        "l0_w": a["L0_gnn_W"], "lam": a["L1_gnn_lambda_max"], "cheb_w": a["L1_gnn_cheb_W"],
        "cheb_b": a["L1_gnn_cheb_b"], "gat_ws": a["L1_gnn_gat_W_src"], "gat_bs": a["L1_gnn_gat_b_src"],
        "gat_wd": a["L1_gnn_gat_W_dst"], "gat_bd": a["L1_gnn_gat_b_dst"], "gat_attn": a["L1_gnn_gat_attn"],
        "w1": a["L2_gnn_W1"], "w2": a["L2_gnn_W2"],
    }
    nc = bacc.Bacc("TRN2", target_bir_lowering=False, num_devices=1)
    args = [nc.dram_tensor(f"in_{k}", v.shape, mybir.dt.from_np(v.dtype), kind="ExternalInput").ap()
            for k, v in arrays.items()]
    out = nc.dram_tensor("out_x", (P, NJ, D), F32, kind="ExternalOutput").ap()
    gnn_kernel(nc, *args, out)
    r = run(nc, [{f"in_{k}": v for k, v in arrays.items()}], core_ids=[0])
    got = r.results[0]["out_x"]
    return np.ascontiguousarray(got.transpose(1, 0, 2)).reshape(NJ * P, D)[:n_nodes]
```

```python
from contextlib import ExitStack
import math

import concourse.bass as bass
from concourse import mybir

F32 = mybir.dt.float32
BF16 = mybir.dt.bfloat16
I32 = mybir.dt.int32
ALU = mybir.AluOpType
ACT = mybir.ActivationFunctionType
AX = mybir.AxisListType

P = 128
D = 32
M = 8
LOG_P = 7
EPS = 1e-5
BIG = 1e30


def shapes(n_nodes, n_edges):
    nj = -(-n_nodes // P)
    t = -(-(-(-n_edges // P)) // 784) * 784
    return nj, t


def chain(engine, sem, start):
    count = [0]

    def link(instruction):
        count[0] += 1
        instruction.then_inc(sem, 1)
        engine.wait_ge(sem, start + count[0])

    return link, count


def gnn_kernel(nc, x, src, dst, emb_t, attr3, attr5, edge_w, edge_w1, l0_w, lam, cheb_w, cheb_b,
               gat_ws, gat_bs, gat_wd, gat_bd, gat_attn, w1, w2, out):
    NJ = x.shape[1]
    T = src.shape[1]
    ROWS = P * NJ
    EP = P * T
    C_SUM = 98
    C_MSG = 56
    assert T % (2 * C_SUM) == 0 and T % (2 * C_MSG) == 0
    JB = 14
    assert NJ % JB == 0 and JB * (D + 1) <= 512
    GROUPS = [(4 * g, min(4, NJ - 4 * g)) for g in range(-(-NJ // 4))]

    top = ExitStack()
    with top:
        def keep(name, shape, dt=F32):
            return top.enter_context(nc.sbuf_tensor(name, shape, dt))

        level = {}

        def signal(name):
            sem = top.enter_context(nc.semaphore(name))
            level[id(sem)] = 0
            return sem

        def at(sem, count):
            return level[id(sem)] + count

        def close(sem, count):
            level[id(sem)] += count

        src_rows = nc.dram_tensor("src_rows", [P, T], I32).ap()
        table_l0 = nc.dram_tensor("table_l0", [ROWS, 112], F32).ap()
        table = nc.dram_tensor("table", [ROWS, D], F32).ap()
        scanned_rows = nc.dram_tensor("scanned_rows", [EP, D], F32).ap()
        scanned_rows33 = nc.dram_tensor("scanned_rows33", [EP, D + 1], F32).ap()
        gathered_rows = nc.dram_tensor("gathered_rows", [EP, D], F32).ap()
        start_rows = nc.dram_tensor("start_rows", [EP, D], F32).ap()
        hidden = nc.dram_tensor("hidden", [P, T, 16], F32).ap()
        unit = nc.dram_tensor("unit", [P, T, 3], F32).ap()

        x_cur = keep("x_cur", [P, NJ, D])
        same = keep("same", [P, T])
        dst_f = keep("dst_f", [P, T])
        end_i = keep("end_i", [P, NJ], I32)
        start_i = keep("start_i", [P, NJ], I32)
        nonempty = keep("nonempty", [P, NJ])
        dinv = keep("dinv", [P, NJ])
        cross_lo = keep("cross_lo", [P, P])
        cross_hi = keep("cross_hi", [P, NJ])
        first_f = keep("first_f", [P, 1])
        last_f = keep("last_f", [P, 1])
        first_row = keep("first_row", [P, 1], I32)
        ident = keep("ident", [P, P])
        ones = keep("ones", [P, P])
        iota_f = keep("iota_f", [P, P])
        eps = keep("eps", [P, 1])
        tail = keep("tail", [P, D + 1])
        fill = keep("fill", [P, D])
        lam_c = keep("lam_c", [P, 6])
        agg = keep("agg", [P, NJ * (D + 1)])
        spread = keep("spread", [P, NJ * (D + 1)])
        stat = keep("stat", [P, NJ, 4])
        sq = keep("sq", [P, NJ, D])

        s_in = signal("s_in")
        s_v = signal("s_v")
        s_pool = signal("s_pool")
        s_pe = signal("s_pe")
        s_act = signal("s_act")
        s_vdone = signal("s_vdone")
        s_write = signal("s_write")
        s_agg = signal("s_agg")
        s_scatter = signal("s_scatter")
        chunks_begun = signal("chunks_begun")
        s_tp = signal("s_tp")
        s_xt = signal("s_xt")
        s_mm = signal("s_mm")
        s_ev = signal("s_ev")
        free = [signal(f"free{b}") for b in range(2)]
        loaded = [signal(f"loaded{b}") for b in range(2)]
        scanned = [signal(f"scanned{b}") for b in range(2)]
        stored = [signal(f"stored{b}") for b in range(2)]

        def gather_signals(tag):
            return [signal(f"gathered_{tag}{b}") for b in range(2)]

        def row_gather(pool, dest, table_ap, index):
            return pool.indirect_dma_start(out=dest, out_offset=None, in_=table_ap,
                                           in_offset=bass.IndirectOffsetOnAxis(ap=index, axis=0))

        def scans(v, buf, mask, carry, n):
            for f in range(n):
                last = v.tensor_tensor_scan(buf[:, :, f], mask, buf[:, :, f], carry[:, f:f + 1],
                                            ALU.mult, ALU.add)
            return last

        def prepare(lo_f, hi_f, iota_b):
            with ExitStack() as st:
                def sb(name, shape, dt=F32):
                    return st.enter_context(nc.sbuf_tensor(name, shape, dt))
                src_i = sb("src_i", [P, T], I32)
                dst_i = sb("dst_i", [P, T], I32)
                work_i = sb("work_i", [P, T], I32)
                iota_i = sb("iota_i", [P, P], I32)
                prev_i = sb("prev_i", [P, 1], I32)
                next_i = sb("next_i", [P, 1], I32)
                pn = sb("pn", [P, 4])
                part_i = sb("part_i", [P, 4], I32)
                cross_i = sb("cross_i", [P, 2], I32)

                with nc.Block() as block:
                    @block.gpsimd
                    def _(pool):
                        nc.gpsimd.iota(iota_i[:], [[1, P]], base=0, channel_multiplier=0).then_inc(s_pool, 1)
                        nc.gpsimd.memset(ones[:], 1.0).then_inc(s_pool, 1)
                        nc.gpsimd.memset(eps[:], EPS).then_inc(s_pool, 1)
                        nc.gpsimd.memset(prev_i[:], -1).then_inc(s_pool, 1)
                        nc.gpsimd.memset(next_i[:], -1).then_inc(s_pool, 1)
                        pool.wait_ge(s_pool, 5)
                        nc.gpsimd.affine_select(out=ident[:], in_=ones[:], compare_op=ALU.is_equal, fill=0.0,
                                                base=0, pattern=[[-1, P]], channel_multiplier=1).then_inc(s_pool, 1)

                    @block.sync
                    def _(sp):
                        sp.dma_start(dst_i[:], dst).then_inc(s_in, 16)
                        sp.dma_start(src_i[:], src).then_inc(s_in, 16)
                        sp.dma_start(x_cur[:], x).then_inc(s_in, 16)
                        sp.dma_start(lam_c[:, 0:1], lam.rearrange("(a b) -> a b", a=1).to_broadcast([P, 1])).then_inc(s_in, 16)
                        sp.wait_ge(s_pool, 5)
                        with nc.allow_non_contiguous_dma(reason="one word of each partition"):
                            sp.dma_start(prev_i[1:P, :], dst[0:P - 1, T - 1:T]).then_inc(s_in, 16)
                            sp.dma_start(next_i[0:P - 1, :], dst[1:P, 0:1]).then_inc(s_in, 16)
                        sp.wait_ge(s_vdone, 1)
                        sp.dma_start(src_rows, work_i[:]).then_inc(s_write, 16)
                        sp.wait_ge(s_write, 16)

                    @block.vector
                    def _(v):
                        start = 0
                        link, count = chain(v, s_v, start)
                        v.wait_ge(s_in, 96)
                        v.wait_ge(s_pool, 6)
                        link(nc.vector.tensor_scalar(work_i[:], src_i[:], P - 1, None, ALU.bitwise_and))
                        link(nc.vector.tensor_scalar(src_i[:], src_i[:], LOG_P, None, ALU.logical_shift_right))
                        ins = nc.vector.scalar_tensor_tensor(work_i[:], work_i[:], float(NJ), src_i[:], ALU.mult, ALU.add)
                        ins.then_inc(s_vdone, 1)
                        v.wait_ge(s_vdone, 1)
                        link(nc.vector.tensor_copy(dst_f[:], dst_i[:]))
                        link(nc.vector.tensor_tensor(same[:, 1:T], dst_f[:, 1:T], dst_f[:, 0:T - 1], ALU.is_equal))
                        link(nc.vector.tensor_copy(pn[:, 0:1], prev_i[:]))
                        link(nc.vector.tensor_copy(pn[:, 1:2], next_i[:]))
                        link(nc.vector.tensor_copy(first_f[:], dst_f[:, 0:1]))
                        link(nc.vector.tensor_copy(last_f[:], dst_f[:, T - 1:T]))
                        link(nc.vector.tensor_tensor(same[:, 0:1], pn[:, 0:1], first_f[:], ALU.is_equal))
                        link(nc.vector.tensor_tensor(pn[:, 2:3], pn[:, 1:2], last_f[:], ALU.is_equal))
                        link(nc.vector.tensor_scalar(part_i[:, 0:1], dst_i[:, 0:1], P - 1, None, ALU.bitwise_and))
                        link(nc.vector.tensor_scalar(part_i[:, 1:2], dst_i[:, 0:1], LOG_P, None, ALU.logical_shift_right))
                        link(nc.vector.scalar_tensor_tensor(first_row[:], part_i[:, 0:1], float(NJ), part_i[:, 1:2], ALU.mult, ALU.add))
                        link(nc.vector.tensor_scalar(cross_i[:, 0:1], dst_i[:, T - 1:T], P - 1, None, ALU.bitwise_and))
                        link(nc.vector.tensor_scalar(cross_i[:, 1:2], dst_i[:, T - 1:T], LOG_P, None, ALU.logical_shift_right))
                        link(nc.vector.tensor_copy(lam_c[:, 4:6], cross_i[:]))
                        link(nc.vector.tensor_copy(iota_f[:], iota_i[:]))
                        link(nc.vector.tensor_copy(iota_b[:], iota_i[:]))
                        link(nc.vector.tensor_scalar(cross_lo[:], iota_f[:], lam_c[:, 4:5], pn[:, 2:3], ALU.is_equal, ALU.mult))
                        link(nc.vector.tensor_scalar(cross_hi[:], iota_f[:, 0:NJ], lam_c[:, 5:6], None, ALU.is_equal))
                        link(nc.vector.tensor_scalar(src_i[:], dst_i[:], P - 1, None, ALU.bitwise_and))
                        link(nc.vector.tensor_copy(lo_f[:], src_i[:]))
                        link(nc.vector.tensor_scalar(src_i[:], dst_i[:], LOG_P, None, ALU.logical_shift_right))
                        link(nc.vector.tensor_copy(hi_f[:], src_i[:]))
                        link(nc.vector.reciprocal(lam_c[:, 1:2], lam_c[:, 0:1]))
                        link(nc.vector.tensor_scalar(lam_c[:, 0:1], lam_c[:, 1:2], -2.0, None, ALU.mult))
                        link(nc.vector.tensor_scalar(lam_c[:, 1:2], lam_c[:, 0:1], -1.0, -1.0, ALU.mult, ALU.add))
                        link(nc.vector.tensor_scalar(lam_c[:, 2:4], lam_c[:, 0:2], 2.0, None, ALU.mult))
                        close(s_v, count[0])
                close(s_in, 96)
                close(s_pool, 6)
                close(s_vdone, 1)
                close(s_write, 16)

        def fetch_sums(pool, rows, n):
            for j in range(NJ):
                row_gather(pool, agg[:, j * n:(j + 1) * n], rows, end_i[:, j:j + 1]).then_inc(s_agg, 16)

        def crossing_matmuls(pe, banks, n):
            pe.wait_ge(s_vdone, at(s_vdone, 1))
            for k in range(NJ // JB):
                if k >= 2:
                    pe.wait_ge(s_ev, at(s_ev, k - 1))
                nc.tensor.matmul(banks[k % 2][:, 0:JB * n], cross_lo[:], spread[:, k * JB * n:(k + 1) * JB * n],
                                 start=True, stop=True).then_inc(s_pe, 1)

        def finish_sums(v, link, banks, n):
            nc.vector.tensor_tensor(
                spread[:, 0:NJ * n].rearrange("p (j f) -> p j f", f=n),
                cross_hi[:].rearrange("p (j a) -> p j a", a=1).to_broadcast([P, NJ, n]),
                tail[:, 0:n].rearrange("p (a f) -> p a f", a=1).to_broadcast([P, NJ, n]),
                ALU.mult).then_inc(s_vdone, 1)
            v.wait_ge(s_agg, at(s_agg, 16 * NJ))
            a = agg[:, 0:NJ * n].rearrange("p (j f) -> p j f", f=n)
            link(nc.vector.tensor_tensor(a, a, nonempty[:].rearrange("p (j a) -> p j a", a=1).to_broadcast([P, NJ, n]), ALU.mult))
            for k in range(NJ // JB):
                v.wait_ge(s_pe, at(s_pe, k + 1))
                part = agg[:, k * JB * n:(k + 1) * JB * n]
                nc.vector.tensor_tensor(part, part, banks[k % 2][:, 0:JB * n], ALU.add).then_inc(s_ev, 1)
            v.wait_ge(s_ev, at(s_ev, NJ // JB))

        def sums_closed():
            close(s_agg, 16 * NJ)
            close(s_pe, NJ // JB)
            close(s_ev, NJ // JB)
            close(s_vdone, 1)

        def by_col(t):
            return t.rearrange("p (j a) -> p j a", a=1).to_broadcast([P, NJ, D])

        def layer_norm(v, link, t, act_done):
            link(nc.vector.tensor_reduce(stat[:, :, 0], t, AX.X, ALU.add))
            link(nc.vector.tensor_scalar(stat[:, :, 0], stat[:, :, 0], 1.0 / D, None, ALU.mult))
            link(nc.vector.tensor_tensor(t, t, stat[:, :, 0:1].to_broadcast([P, NJ, D]), ALU.subtract))
            link(nc.vector.tensor_tensor(sq[:], t, t, ALU.mult))
            nc.vector.tensor_reduce(stat[:, :, 1], sq[:], AX.X, ALU.add).then_inc(s_vdone, 1)
            v.wait_ge(s_act, act_done)
            link(nc.vector.reciprocal(stat[:, :, 3], stat[:, :, 2]))
            link(nc.vector.tensor_tensor(t, t, stat[:, :, 3:4].to_broadcast([P, NJ, D]), ALU.mult))

        def norm_root(act, ready):
            act.wait_ge(s_vdone, ready)
            nc.scalar.activation(stat[:, :, 2], stat[:, :, 1], ACT.Sqrt, bias=eps[:], scale=1.0 / D).then_inc(s_act, 1)

        def linear_pe(pe, srcs, w_list, n, pt, xt, po):
            for g, (j0, nj) in enumerate(GROUPS):
                if g >= 2:
                    pe.wait_ge(s_xt, at(s_xt, g - 1))
                for k, s in enumerate(srcs):
                    last = nc.tensor.transpose(pt[g % 2][0:nj * D, k * P:(k + 1) * P],
                                               s[:, j0:j0 + nj, :].rearrange("p j f -> p (j f)"), ident[:])
                last.then_inc(s_tp, 1)
                pe.wait_ge(s_xt, at(s_xt, g + 1))
                if g >= 2:
                    pe.wait_ge(s_ev, at(s_ev, g - 1))
                for k in range(len(srcs)):
                    last = nc.tensor.matmul(po[g % 2][:, 0:nj * n], xt[g % 2][0:nj * D, k * P:(k + 1) * P],
                                            w_list[k][0:nj * D, 0:nj * n],
                                            start=(k == 0), stop=(k == len(srcs) - 1))
                last.then_inc(s_mm, 1)

        def linear_act(act, n_srcs, pt, xt):
            for g, (j0, nj) in enumerate(GROUPS):
                act.wait_ge(s_tp, at(s_tp, g + 1))
                if g >= 2:
                    act.wait_ge(s_mm, at(s_mm, g - 1))
                nc.scalar.activation(xt[g % 2][0:nj * D, 0:n_srcs * P], pt[g % 2][0:nj * D, 0:n_srcs * P],
                                     ACT.Copy).then_inc(s_xt, 1)

        def linear_out(v, dest, n, po, bias=None):
            for g, (j0, nj) in enumerate(GROUPS):
                v.wait_ge(s_mm, at(s_mm, g + 1))
                got = po[g % 2][:, 0:nj * n].rearrange("p (j f) -> p j f", f=n)
                if bias is None:
                    nc.vector.tensor_copy(dest[:, j0:j0 + nj, :], got).then_inc(s_ev, 1)
                else:
                    nc.vector.tensor_tensor(dest[:, j0:j0 + nj, :], got,
                                            bias[:, 0:n].rearrange("p (a f) -> p a f", a=1).to_broadcast([P, nj, n]),
                                            ALU.add).then_inc(s_ev, 1)
            v.wait_ge(s_ev, at(s_ev, len(GROUPS)))

        def linear_closed():
            for s in (s_tp, s_xt, s_mm, s_ev):
                close(s, len(GROUPS))

        def replicate(sp, w, n):
            for k in range(1, 4):
                sp.dma_start(w[k * D:(k + 1) * D, k * n:(k + 1) * n], w[0:D, 0:n]).then_inc(s_write, 16)

        def sum_pass(tag):
            CH = C_SUM
            gathered = gather_signals(tag)
            with ExitStack() as st:
                idx = [st.enter_context(nc.sbuf_tensor(f"idx_{tag}{b}", [P, CH], I32)) for b in range(2)]
                rows = [st.enter_context(nc.sbuf_tensor(f"rows_{tag}{b}", [P, CH, D], F32)) for b in range(2)]
                z = scanned_rows.rearrange("(p t) f -> p t f", p=P)
                with nc.Block() as block:
                    @block.sync
                    def _(sp):
                        with sp.Fori(0, T // CH // 2) as i:
                            for b in range(2):
                                sp.wait_ge(free[b], at(free[b], 1 + i))
                                sp.dma_start(idx[b][:], src_rows[:, bass.ds((2 * i + b) * CH, CH)]).then_inc(loaded[b], 16)

                    @block.gpsimd
                    def _(pool):
                        with pool.Fori(0, T // CH // 2) as i:
                            for b in range(2):
                                pool.wait_ge(loaded[b], at(loaded[b], 16 * (i + 1)))
                                pool.sem_inc(chunks_begun, 1)
                                for t in range(CH):
                                    row_gather(pool, rows[b][:, t, :], table, idx[b][:, t:t + 1]).then_inc(gathered[b], 16)

                    @block.vector
                    def _(v):
                        nc.vector.memset(tail[:], 0.0).then_inc(s_v, 1)
                        with v.Fori(0, T // CH // 2) as i:
                            for b in range(2):
                                v.wait_ge(s_v, at(s_v, 1 + 4 * i + 2 * b))
                                v.wait_ge(gathered[b], 16 * CH * (i + 1))
                                scans(nc.vector, rows[b], same[:, bass.ds((2 * i + b) * CH, CH)], tail, D).then_inc(s_v, 1)
                                v.wait_ge(s_v, at(s_v, 2 + 4 * i + 2 * b))
                                nc.vector.tensor_copy(tail[:, 0:D], rows[b][:, CH - 1, :]).then_inc(s_v, 1)

                    @block.scalar
                    def _(act):
                        for b in range(2):
                            act.sem_inc(free[b], 1)
                        with act.Fori(0, T // CH // 2) as i:
                            for b in range(2):
                                act.wait_ge(s_v, at(s_v, 3 + 4 * i + 2 * b))
                                act.dma_start(z[:, bass.ds((2 * i + b) * CH, CH), :], rows[b][:]).then_inc(stored[b], 16)
                                act.wait_ge(stored[b], at(stored[b], 16 * (i + 1)))
                                act.sem_inc(free[b], 1)
            n = T // CH // 2
            close(s_v, 1 + 4 * n)
            for b in range(2):
                close(free[b], 1 + n)
                close(loaded[b], 16 * n)
                close(stored[b], 16 * n)

        def l0_table():
            R3 = 1.0 / math.sqrt(3.0)
            R6 = 1.0 / math.sqrt(6.0)
            with ExitStack() as st:
                wb = st.enter_context(nc.sbuf_tensor("wb_l0", [P, 4 * 112], F32))
                rows = st.enter_context(nc.sbuf_tensor("rows_l0", [P, NJ, 112], F32))
                pt = [st.enter_context(nc.psum_tensor(f"pt{b}", [P, 512], F32)) for b in range(2)]
                po = [st.enter_context(nc.psum_tensor(f"po{b}", [P, 512], F32)) for b in range(2)]
                xt = [st.enter_context(nc.sbuf_tensor(f"xt{b}", [P, P], F32)) for b in range(2)]
                with nc.Block() as block:
                    @block.sync
                    def _(sp):
                        sp.wait_ge(s_vdone, at(s_vdone, 1))
                        with nc.allow_non_contiguous_dma(reason="weights of a few hundred bytes"):
                            n = 0
                            for col, k in ((0, 0), (8, 2)):
                                sp.dma_start(wb[0:M, col:col + M], l0_w[k]).then_inc(s_in, 16)
                                n += 16
                            for col, k in ((16, 1), (40, 3), (64, 4), (88, 5)):
                                for c in range(3):
                                    sp.dma_start(wb[M + c:D:3, col + c:col + 24:3], l0_w[k]).then_inc(s_in, 16)
                                    n += 16
                        assert n == 14 * 16
                        sp.wait_ge(s_vdone, at(s_vdone, 2))
                        replicate(sp, wb, 112)
                        sp.wait_ge(s_vdone, at(s_vdone, 3))
                        sp.dma_start(table_l0.rearrange("(p j) f -> p j f", p=P), rows[:]).then_inc(s_write, 16)
                        sp.wait_ge(s_write, at(s_write, 64))

                    @block.vector
                    def _(v):
                        nc.vector.memset(wb[:], 0.0).then_inc(s_vdone, 1)
                        v.wait_ge(s_in, at(s_in, 14 * 16))
                        start = at(s_v, 0)
                        link, count = chain(v, s_v, start)
                        link(nc.vector.tensor_scalar(wb[0:D, 8:64], wb[0:D, 8:64], R3, None, ALU.mult))
                        nc.vector.tensor_scalar(wb[0:D, 64:88], wb[0:D, 64:88], R6, None, ALU.mult).then_inc(s_vdone, 1)
                        linear_out(v, rows, 112, po)
                        v.sem_inc(s_vdone, 1)
                        close(s_v, count[0])

                    @block.tensor
                    def _(pe):
                        pe.wait_ge(s_write, at(s_write, 48))
                        linear_pe(pe, [x_cur], [wb], 112, pt, xt, po)

                    @block.scalar
                    def _(act):
                        linear_act(act, 1, pt, xt)
            close(s_in, 14 * 16)
            close(s_vdone, 3)
            close(s_write, 64)
            linear_closed()

        def l0_pass(lo_f, hi_f, iota_b):
            CH = C_MSG
            SUBS = 4
            CS = CH // SUBS
            assert CS * SUBS == CH
            gathered = gather_signals("l0")
            A = 1.0 / math.sqrt(10.0)
            B = 1.0 / math.sqrt(30.0)
            with ExitStack() as st:
                def sb(name, shape, dt=F32):
                    return st.enter_context(nc.sbuf_tensor(name, shape, dt))
                idx = [sb(f"idx_l0{b}", [P, CH], I32) for b in range(2)]
                rows = [sb(f"g_l0{b}", [P, CH, 112]) for b in range(2)]
                msg = [sb(f"msg_l0{b}", [P, CH, D]) for b in range(2)]
                a3 = [sb(f"a3_{b}", [P, CH, 3]) for b in range(2)]
                a5 = [sb(f"a5_{b}", [P, CH, 5]) for b in range(2)]
                s0 = [sb(f"s0_{b}", [P, CH]) for b in range(2)]
                bm = sb("bm", [P, CH, 3, 3])
                tmp = sb("tmp", [P, CH, M, 3])
                squares = sb("squares", [P, CH, 3])
                length = sb("length", [P, CH])
                direction = [sb(f"direction{b}", [P, CH, 3]) for b in range(2)]
                lower = sb("lower", [P, P])
                zeros = sb("zeros", [P, CH * D])
                zero_b = sb("zero_b", [P, P], BF16)
                lo1 = [sb(f"lo1_{b}", [P, CS, P], BF16) for b in range(2)]
                hi1 = [sb(f"hi1_{b}", [P, CS, NJ], BF16) for b in range(2)]
                cnt = sb("cnt", [P, NJ])
                cum = sb("cum", [P, 4, NJ])
                w1_s = sb("w1_s", [10, 16])
                emb_s = [sb(f"emb_s{b}", [10, CS * P]) for b in range(2)]
                hid = [sb(f"hid{b}", [P, CH, 16]) for b in range(2)]
                p_cnt = st.enter_context(nc.psum_tensor("p_cnt", [P, 512], F32))
                p_cum = st.enter_context(nc.psum_tensor("p_cum", [P, 2, NJ], F32))
                p_h = [st.enter_context(nc.psum_tensor(f"p_h{b}", [P, 512], F32)) for b in range(2)]
                one_hot = signal("one_hot")
                counted = signal("counted")
                h_in = [signal(f"h_in{b}") for b in range(2)]
                h_made = signal("h_made")
                h_free = signal("h_free")
                h_out = [signal(f"h_out{b}") for b in range(2)]
                zero_out = signal("zero_out")
                w1_in = signal("w1_in")
                len_made = signal("len_made")
                len_root = signal("len_root")
                unit_out = [signal(f"unit_out{b}") for b in range(2)]
                z = scanned_rows.rearrange("(p t) f -> p t f", p=P)
                zero_dest = start_rows.rearrange("(p t) f -> p (t f)", p=P)
                LINKS = 31
                with nc.Block() as block:
                    @block.sync
                    def _(sp):
                        sp.dma_start(w1_s[:], w1).then_inc(w1_in, 16)
                        for b in range(2):
                            sp.sem_inc(stored[b], 16)
                            sp.sem_inc(unit_out[b], 16)
                        sp.wait_ge(s_pool, at(s_pool, 1))
                        with sp.Fori(0, T // CH // 2) as i:
                            for b in range(2):
                                c = 2 * i + b
                                ts = bass.ds(c * CH, CH)
                                sp.wait_ge(stored[b], at(stored[b], 16 * (i + 1)))
                                sp.wait_ge(unit_out[b], 16 * (i + 1))
                                sp.dma_start(idx[b][:], src_rows[:, ts]).then_inc(loaded[b], 16)
                                sp.dma_start(a3[b][:], attr3[:, ts, :]).then_inc(loaded[b], 16)
                                sp.dma_start(a5[b][:], attr5[:, ts, :]).then_inc(loaded[b], 16)
                                sp.dma_start(s0[b][:], edge_w1[:, ts]).then_inc(loaded[b], 16)
                                sp.dma_start(zero_dest[:, bass.ds(c * CH * D, CH * D)], zeros[:]).then_inc(zero_out, 16)
                                for u in range(SUBS):
                                    sp.wait_ge(h_made, c * SUBS + u + 1)
                                    sp.dma_start(emb_s[u % 2][:], emb_t[:, bass.ds((c * CH + u * CS) * P, CS * P)]).then_inc(h_in[u % 2], 16)
                        sp.wait_ge(zero_out, 16 * (T // CH))

                    @block.gpsimd
                    def _(pool):
                        nc.gpsimd.memset(zeros[:], 0.0).then_inc(s_pool, 1)
                        nc.gpsimd.memset(zero_b[:], 0.0)
                        nc.gpsimd.affine_select(out=lower[:], in_=ones[:], compare_op=ALU.is_ge, fill=0.0,
                                                base=0, pattern=[[1, P]], channel_multiplier=-1).then_inc(s_pool, 1)
                        with pool.Fori(0, T // CH // 2) as i:
                            for b in range(2):
                                pool.wait_ge(loaded[b], at(loaded[b], 64 * (i + 1)))
                                pool.sem_inc(chunks_begun, 1)
                                for t in range(CH):
                                    row_gather(pool, rows[b][:, t, :], table_l0, idx[b][:, t:t + 1]).then_inc(gathered[b], 16)

                    @block.vector
                    def _(v):
                        nc.vector.memset(tail[:], 0.0).then_inc(s_v, 1)
                        v.sem_inc(one_hot, 1)
                        with v.Fori(0, T // CH // 2) as i:
                            for b in range(2):
                                c = 2 * i + b
                                for u in range(SUBS):
                                    v.wait_ge(counted, 1 + c * SUBS + u)
                                    for buf, half, n in ((lo1[u % 2], lo_f, P), (hi1[u % 2], hi_f, NJ)):
                                        last = nc.vector.tensor_tensor(
                                            buf[:], iota_b[:, 0:n].rearrange("p (a n) -> p a n", a=1).to_broadcast([P, CS, n]),
                                            half[:, bass.ds(c * CH + u * CS, CS)].rearrange("p (t a) -> p t a", a=1).to_broadcast([P, CS, n]), ALU.is_equal)
                                    last.then_inc(one_hot, 1)
                                start = at(s_v, 1) + (2 * i + b) * LINKS
                                link, count = chain(v, s_v, start)
                                v.wait_ge(s_v, start)
                                v.wait_ge(loaded[b], at(loaded[b], 64 * (i + 1)))
                                V = nc.vector
                                g = rows[b]
                                a1, a3v, a4, a5v = (g[:, :, c:c + 24].rearrange("p t (o k) -> p t o k", k=3) for c in (16, 40, 64, 88))
                                o0 = msg[b][:, :, 0:M]
                                o1 = msg[b][:, :, M:D].rearrange("p t (o k) -> p t o k", k=3)
                                y = a5[b]
                                link(V.tensor_tensor(squares[:], a3[b][:], a3[b][:], ALU.mult))
                                V.tensor_reduce(length[:], squares[:], AX.X, ALU.add).then_inc(len_made, 1)
                                V.tensor_scalar(bm[:, :, 0, 2], y[:, :, 0], A, None, ALU.mult)
                                V.tensor_scalar(bm[:, :, 2, 0], y[:, :, 0], A, None, ALU.mult)
                                V.tensor_scalar(bm[:, :, 0, 1], y[:, :, 1], A, None, ALU.mult)
                                V.tensor_scalar(bm[:, :, 1, 0], y[:, :, 1], A, None, ALU.mult)
                                V.tensor_scalar(bm[:, :, 1, 2], y[:, :, 3], A, None, ALU.mult)
                                V.tensor_scalar(bm[:, :, 2, 1], y[:, :, 3], A, None, ALU.mult)
                                V.tensor_scalar(bm[:, :, 1, 1], y[:, :, 2], 2 * B, None, ALU.mult)
                                V.tensor_scalar(tmp[:, :, 0, 0], y[:, :, 4], -A, None, ALU.mult)
                                link(V.tensor_scalar(tmp[:, :, 1, 0], y[:, :, 4], A, None, ALU.mult))
                                V.scalar_tensor_tensor(bm[:, :, 0, 0], y[:, :, 2], -B, tmp[:, :, 0, 0], ALU.mult, ALU.add)
                                link(V.scalar_tensor_tensor(bm[:, :, 2, 2], y[:, :, 2], -B, tmp[:, :, 1, 0], ALU.mult, ALU.add))
                                v.wait_ge(len_root, c + 1)
                                link(V.reciprocal(length[:], length[:]))
                                V.tensor_tensor(direction[b][:], a3[b][:], length[:].rearrange("p (t a) -> p t a", a=1).to_broadcast([P, CH, 3]), ALU.mult)
                                v.wait_ge(gathered[b], 16 * CH * (i + 1))

                                s_e = s0[b][:].rearrange("p (t a) -> p t a", a=1)
                                v_k = a3[b][:].rearrange("p t (a k) -> p t a k", a=1).to_broadcast([P, CH, M, 3])
                                link(V.tensor_tensor(tmp[:], a3v, v_k, ALU.mult))
                                link(V.tensor_reduce(o0, tmp[:], AX.X, ALU.add))
                                t0 = tmp[:, :, 0:M, 0]
                                link(V.tensor_tensor(t0, g[:, :, 0:M], s_e.to_broadcast([P, CH, M]), ALU.mult))
                                link(V.tensor_tensor(o0, o0, t0, ALU.add))
                                link(V.tensor_tensor(msg[b][:, :, M:D], g[:, :, 16:40], s_e.to_broadcast([P, CH, 24]), ALU.mult))
                                link(V.tensor_tensor(tmp[:], g[:, :, 8:16].rearrange("p t (o a) -> p t o a", a=1).to_broadcast([P, CH, M, 3]), v_k, ALU.mult))
                                link(V.tensor_tensor(o1, o1, tmp[:], ALU.add))
                                for j in range(3):
                                    link(V.tensor_tensor(tmp[:], a5v[:, :, :, j:j + 1].to_broadcast([P, CH, M, 3]),
                                                         bm[:, :, j:j + 1, :].to_broadcast([P, CH, M, 3]), ALU.mult))
                                    link(V.tensor_tensor(o1, o1, tmp[:], ALU.add))
                                for k in range(3):
                                    p1, p2 = (k + 1) % 3, (k + 2) % 3
                                    for n, (iv, ja, op) in enumerate(((p1, p2, ALU.add), (p2, p1, ALU.subtract))):
                                        link(V.tensor_tensor(tmp[:, :, :, n], a4[:, :, :, ja],
                                                             a3[b][:, :, iv:iv + 1].to_broadcast([P, CH, M]), ALU.mult))
                                        link(V.tensor_tensor(o1[:, :, :, k], o1[:, :, :, k], tmp[:, :, :, n], op))
                                link(scans(V, msg[b], same[:, bass.ds((2 * i + b) * CH, CH)], tail, D))
                                ins = V.tensor_copy(tail[:, 0:D], msg[b][:, CH - 1, :])
                                count[0] += 1
                                ins.then_inc(s_v, 1)
                                links[0] = count[0]
                        assert links[0] == LINKS, links
                        link, count = chain(v, s_v, at(s_v, 1) + T // CH * LINKS)
                        v.wait_ge(s_pe, at(s_pe, 1))
                        link(nc.vector.tensor_copy(cnt[:], p_cnt[:, 0:NJ]))
                        link(nc.vector.tensor_scalar(nonempty[:], cnt[:], 1.0, None, ALU.min))
                        nc.vector.tensor_scalar(dinv[:], cnt[:], 1.0, None, ALU.max).then_inc(s_vdone, 1)
                        v.wait_ge(s_pe, at(s_pe, 2))
                        link(nc.vector.tensor_copy(cum[:, 0:2, :], p_cum[:]))
                        link(nc.vector.tensor_tensor_scan(cum[:, 2, :], ones[:, 0:NJ], cum[:, 1, :], 0.0, ALU.mult, ALU.add))
                        link(nc.vector.tensor_tensor(cum[:, 2, :], cum[:, 2, :], cum[:, 1, :], ALU.subtract))
                        link(nc.vector.tensor_tensor(cum[:, 2, :], cum[:, 2, :], cum[:, 0, :], ALU.add))
                        link(nc.vector.tensor_scalar(cum[:, 3, :], cum[:, 2, :], -1.0, 0.0, ALU.add, ALU.max))
                        link(nc.vector.tensor_copy(end_i[:], cum[:, 3, :]))
                        link(nc.vector.tensor_tensor(cum[:, 2, :], cum[:, 2, :], cnt[:], ALU.subtract))
                        link(nc.vector.tensor_scalar(cum[:, 3, :], nonempty[:], -float(EP), float(EP), ALU.mult, ALU.add))
                        link(nc.vector.tensor_tensor(cum[:, 2, :], cum[:, 2, :], cum[:, 3, :], ALU.add))
                        link(nc.vector.tensor_copy(start_i[:], cum[:, 2, :]))
                        v.wait_ge(s_act, at(s_act, 1))
                        link(nc.vector.reciprocal(dinv[:], dinv[:]))
                        final[0] = count[0]

                    @block.tensor
                    def _(pe):
                        pe.wait_ge(s_pool, at(s_pool, 2))
                        pe.wait_ge(w1_in, 16)
                        nc.tensor.matmul(p_cnt[:, 0:NJ], zero_b[:], zero_b[:, 0:NJ], start=True, stop=False).then_inc(counted, 2)
                        pe.sem_inc(h_made, 2)
                        with pe.Fori(0, T // CH // 2) as i:
                            for b in range(2):
                                c = 2 * i + b
                                for u in range(SUBS):
                                    pe.wait_ge(h_in[u % 2], 16 * (c * (SUBS // 2) + u // 2 + 1))
                                    pe.wait_ge(h_free, c * SUBS + u + 1)
                                    for t in range(CS):
                                        last = nc.tensor.matmul(p_h[u % 2][:, 16 * t:16 * t + 16],
                                                                emb_s[u % 2][:, t * P:(t + 1) * P], w1_s[:], start=True, stop=True)
                                    last.then_inc(h_made, 1)
                                for u in range(SUBS):
                                    pe.wait_ge(one_hot, 2 + c * SUBS + u)
                                    for t in range(CS):
                                        last = nc.tensor.matmul(p_cnt[:, 0:NJ], lo1[u % 2][:, t, :], hi1[u % 2][:, t, :], start=False, stop=False)
                                    last.then_inc(counted, 1)
                        nc.tensor.matmul(p_cnt[:, 0:NJ], zero_b[:], zero_b[:, 0:NJ], start=False, stop=True).then_inc(s_pe, 1)
                        pe.wait_ge(s_vdone, at(s_vdone, 1))
                        nc.tensor.matmul(p_cum[:, 0, :], lower[:], cnt[:], start=True, stop=True)
                        nc.tensor.matmul(p_cum[:, 1, :], ones[:], cnt[:], start=True, stop=True).then_inc(s_pe, 1)

                    @block.scalar
                    def _(act):
                        act.sem_inc(h_free, 2)
                        for b in range(2):
                            act.sem_inc(h_out[b], 16)
                        with act.Fori(0, T // CH // 2) as i:
                            for b in range(2):
                                c = 2 * i + b
                                act.wait_ge(h_out[b], 16 * (i + 1))
                                for u in range(SUBS):
                                    act.wait_ge(h_made, c * SUBS + u + 3)
                                    nc.scalar.activation(hid[b][:, u * CS:(u + 1) * CS, :],
                                                         p_h[u % 2][:, 0:16 * CS].rearrange("p (t k) -> p t k", k=16),
                                                         ACT.Relu).then_inc(h_free, 1)
                                act.wait_ge(h_free, (c + 1) * SUBS + 2)
                                act.dma_start(hidden[:, bass.ds(c * CH, CH), :], hid[b][:]).then_inc(h_out[b], 16)
                                act.wait_ge(len_made, c + 1)
                                nc.scalar.activation(length[:], length[:], ACT.Sqrt).then_inc(len_root, 1)
                                act.wait_ge(s_v, at(s_v, 1) + (c + 1) * LINKS)
                                act.dma_start(z[:, bass.ds(c * CH, CH), :], msg[b][:]).then_inc(stored[b], 16)
                                act.dma_start(unit[:, bass.ds(c * CH, CH), :], direction[b][:]).then_inc(unit_out[b], 16)
                        act.wait_ge(s_vdone, at(s_vdone, 1))
                        nc.scalar.activation(dinv[:], dinv[:], ACT.Sqrt).then_inc(s_act, 1)
                        for b in range(2):
                            act.wait_ge(stored[b], at(stored[b], 16 + 16 * (T // CH // 2)))
                            act.wait_ge(unit_out[b], 16 + 16 * (T // CH // 2))
                            act.wait_ge(h_out[b], 16 + 16 * (T // CH // 2))
            n = T // CH // 2
            close(s_v, 1 + 2 * n * LINKS + final[0])
            close(s_pool, 2)
            close(s_pe, 2)
            close(s_act, 1)
            close(s_vdone, 1)
            for b in range(2):
                close(loaded[b], 64 * n)
                close(stored[b], 16 + 16 * n)

        links = [0]
        final = [0]

        def residual_norm_stage(tag, rows, n, write_table, last=False, scale_table=False):
            with ExitStack() as st:
                banks = [st.enter_context(nc.psum_tensor(f"pc_{tag}{b}", [P, 512], F32)) for b in range(2)]
                with nc.Block() as block:
                    @block.gpsimd
                    def _(pool):
                        fetch_sums(pool, rows, n)
                        if write_table == "start":
                            scatter_starts(pool, x_cur, at(s_vdone, 3))

                    @block.tensor
                    def _(pe):
                        crossing_matmuls(pe, banks, n)

                    @block.vector
                    def _(v):
                        start = at(s_v, 0)
                        link, count = chain(v, s_v, start)
                        finish_sums(v, link, banks, n)
                        a = agg[:, 0:NJ * n].rearrange("p (j f) -> p j f", f=n)
                        if n == D:
                            link(nc.vector.tensor_tensor(x_cur[:], x_cur[:], a, ALU.add))
                        else:
                            link(nc.vector.tensor_scalar(stat[:, :, 0], nonempty[:], -1.0, 1.0, ALU.mult, ALU.add))
                            link(nc.vector.tensor_tensor(stat[:, :, 0], stat[:, :, 0], a[:, :, D], ALU.add))
                            link(nc.vector.reciprocal(stat[:, :, 1], stat[:, :, 0]))
                            link(nc.vector.tensor_tensor(sq[:], a[:, :, 0:D], stat[:, :, 1:2].to_broadcast([P, NJ, D]), ALU.mult))
                            link(nc.vector.scalar_tensor_tensor(sq[:], sq[:], 0.01, sq[:], ALU.mult, ALU.max))
                            link(nc.vector.tensor_tensor(x_cur[:], x_cur[:], sq[:], ALU.add))
                        layer_norm(v, link, x_cur[:], at(s_act, 1))
                        if scale_table:
                            link(nc.vector.tensor_tensor(sq[:], x_cur[:], by_col(dinv[:]), ALU.mult))
                        v.sem_inc(s_vdone, 1)
                        close(s_v, count[0])

                    @block.scalar
                    def _(act):
                        norm_root(act, at(s_vdone, 2))

                    @block.sync
                    def _(sp):
                        sp.wait_ge(s_vdone, at(s_vdone, 3))
                        dest = out if last else table.rearrange("(p j) f -> p j f", p=P)
                        sp.dma_start(dest, sq[:] if scale_table else x_cur[:]).then_inc(s_write, 16)
                        sp.wait_ge(s_write, at(s_write, 16))
            sums_closed()
            close(s_vdone, 2)
            close(s_act, 1)
            close(s_write, 16)
            if write_table == "start":
                close(s_scatter, 16 * NJ)

        def scatter_starts(pool, nodes, ready):
            pool.wait_ge(s_vdone, ready)
            for j in range(NJ):
                pool.indirect_dma_start(out=start_rows, out_offset=bass.IndirectOffsetOnAxis(ap=start_i[:, j:j + 1], axis=0),
                                        in_=nodes[:, j, :], in_offset=None, bounds_check=EP - 1,
                                        oob_is_err=False).then_inc(s_scatter, 16)
            pool.wait_ge(s_scatter, at(s_scatter, 16 * NJ))

        def cheb_step_stage(tag, x0, x1, x2, first):
            with ExitStack() as st:
                banks = [st.enter_context(nc.psum_tensor(f"pc_{tag}{b}", [P, 512], F32)) for b in range(2)]
                with nc.Block() as block:
                    @block.gpsimd
                    def _(pool):
                        fetch_sums(pool, scanned_rows, D)

                    @block.tensor
                    def _(pe):
                        crossing_matmuls(pe, banks, D)

                    @block.vector
                    def _(v):
                        start = at(s_v, 0)
                        link, count = chain(v, s_v, start)
                        finish_sums(v, link, banks, D)
                        a = agg[:, 0:NJ * D].rearrange("p (j f) -> p j f", f=D)
                        link(nc.vector.tensor_tensor(a, a, by_col(dinv[:]), ALU.mult))
                        if first:
                            link(nc.vector.tensor_scalar(a, a, lam_c[:, 0:1], None, ALU.mult))
                            link(nc.vector.scalar_tensor_tensor(x1[:], x0[:], lam_c[:, 1:2], a, ALU.mult, ALU.add))
                            link(nc.vector.tensor_tensor(sq[:], x1[:], by_col(dinv[:]), ALU.mult))
                        else:
                            link(nc.vector.tensor_scalar(a, a, lam_c[:, 2:3], None, ALU.mult))
                            link(nc.vector.scalar_tensor_tensor(x2[:], x1[:], lam_c[:, 3:4], a, ALU.mult, ALU.add))
                            link(nc.vector.tensor_tensor(x2[:], x2[:], x0[:], ALU.subtract))
                        v.sem_inc(s_vdone, 1)
                        close(s_v, count[0])

                    @block.sync
                    def _(sp):
                        if first:
                            sp.wait_ge(s_vdone, at(s_vdone, 2))
                            sp.dma_start(table.rearrange("(p j) f -> p j f", p=P), sq[:]).then_inc(s_write, 16)
                            sp.wait_ge(s_write, at(s_write, 16))
            sums_closed()
            close(s_vdone, 1)
            if first:
                close(s_write, 16)

        def cheb_mix_stage(tag, xs, dest, gat=None):
            with ExitStack() as st:
                def sb(name, shape, dt=F32):
                    return st.enter_context(nc.sbuf_tensor(f"{name}_{tag}", shape, dt))
                wc = [sb(f"wc{k}", [P, 4 * D]) for k in range(3)]
                bias = sb("bias", [P, D])
                wg = sb("wg", [P, 8 * D])
                gbias = sb("gbias", [P, 2 * D])
                both = sb("both", [P, NJ, 2 * D])
                pt = [st.enter_context(nc.psum_tensor(f"pt_{tag}{b}", [P, 512], F32)) for b in range(2)]
                po = [st.enter_context(nc.psum_tensor(f"po_{tag}{b}", [P, 512], F32)) for b in range(2)]
                xt = [sb(f"xt{b}", [P, 3 * P]) for b in range(2)]
                n_in = 4 + (4 if gat else 0)

                def row(a):
                    return a.rearrange("(a n) -> a n", a=1).to_broadcast([P, D])
                with nc.Block() as block:
                    @block.sync
                    def _(sp):
                        sp.wait_ge(s_vdone, at(s_vdone, 1))
                        for k in range(3):
                            sp.dma_start(wc[k][0:D, 0:D], cheb_w[k * D:(k + 1) * D, :]).then_inc(s_in, 16)
                        sp.dma_start(bias[:], row(cheb_b)).then_inc(s_in, 16)
                        if gat:
                            sp.dma_start(wg[0:D, 0:D], gat_ws).then_inc(s_in, 16)
                            sp.dma_start(wg[0:D, D:2 * D], gat_wd).then_inc(s_in, 16)
                            sp.dma_start(gbias[:, 0:D], row(gat_bs)).then_inc(s_in, 16)
                            sp.dma_start(gbias[:, D:2 * D], row(gat_bd)).then_inc(s_in, 16)
                        sp.wait_ge(s_in, at(s_in, 16 * n_in))
                        for k in range(3):
                            replicate(sp, wc[k], D)
                        replicate(sp, wg, 2 * D) if gat else None
                        sp.wait_ge(s_vdone, at(s_vdone, 2))
                        if not gat:
                            sp.dma_start(table.rearrange("(p j) f -> p j f", p=P), sq[:]).then_inc(s_write, 16)
                            sp.wait_ge(s_write, at(s_write, 16 * 10))

                    @block.tensor
                    def _(pe):
                        pe.wait_ge(s_write, at(s_write, 16 * (12 if gat else 9)))
                        linear_pe(pe, xs, wc, D, pt, xt, po)

                    @block.scalar
                    def _(act):
                        linear_act(act, 3, pt, xt)

                    @block.vector
                    def _(v):
                        start = at(s_v, 0)
                        link, count = chain(v, s_v, start)
                        for w in wc:
                            nc.vector.memset(w[:], 0.0)
                        nc.vector.memset(wg[:], 0.0).then_inc(s_vdone, 1)
                        v.wait_ge(s_in, at(s_in, 16 * n_in))
                        linear_out(v, dest, D, po, bias)
                        link(nc.vector.scalar_tensor_tensor(dest[:], dest[:], 0.01, dest[:], ALU.mult, ALU.max))
                        ins = nc.vector.tensor_tensor(sq[:], dest[:], by_col(dinv[:]), ALU.mult)
                        ins.then_inc(s_vdone, 1)
                        close(s_v, count[0])
                close(s_in, 16 * n_in)
                close(s_write, 16 * (12 if gat else 10))
                close(s_vdone, 2)
                linear_closed()
                if gat:
                    with nc.Block() as block:
                        @block.tensor
                        def _(pe):
                            linear_pe(pe, [dest], [wg], 2 * D, pt, xt, po)

                        @block.scalar
                        def _(act):
                            linear_act(act, 1, pt, xt)

                        @block.vector
                        def _(v):
                            linear_out(v, both, 2 * D, po, gbias)
                            start = at(s_v, 0)
                            link, count = chain(v, s_v, start)
                            link(nc.vector.tensor_copy(sq[:], both[:, :, D:2 * D]))
                            v.sem_inc(s_vdone, 1)
                            close(s_v, count[0])

                        @block.gpsimd
                        def _(pool):
                            scatter_starts(pool, sq, at(s_vdone, 1))
                            pool.wait_ge(s_write, at(s_write, 16))
                            row_gather(pool, fill[:], table, first_row[:]).then_inc(s_agg, 16)
                            pool.wait_ge(s_agg, at(s_agg, 16))

                        @block.sync
                        def _(sp):
                            sp.wait_ge(s_vdone, at(s_vdone, 1))
                            sp.dma_start(table.rearrange("(p j) f -> p j f", p=P), sq[:]).then_inc(s_write, 16)
                            sp.wait_ge(s_agg, at(s_agg, 16))
                            sp.dma_start(table.rearrange("(p j) f -> p j f", p=P), both[:, :, 0:D]).then_inc(s_write, 16)
                            sp.wait_ge(s_write, at(s_write, 32))
                    linear_closed()
                    close(s_vdone, 1)
                    close(s_agg, 16)
                    close(s_write, 32)
                    close(s_scatter, 16 * NJ)

        def gat_logit_pass(logit):
            CH = C_MSG
            gathered = gather_signals("gat")
            with ExitStack() as st:
                def sb(name, shape, dt=F32):
                    return st.enter_context(nc.sbuf_tensor(name, shape, dt))
                idx = [sb(f"idx_gat{b}", [P, CH], I32) for b in range(2)]
                rows = [sb(f"g_gat{b}", [P, CH, D]) for b in range(2)]
                fd = [sb(f"fd_gat{b}", [P, CH, D]) for b in range(2)]
                attn = sb("attn", [P, D])
                zg = gathered_rows.rearrange("(p t) f -> p t f", p=P)
                sr = start_rows.rearrange("(p t) f -> p t f", p=P)
                LINKS = 6
                with nc.Block() as block:
                    @block.sync
                    def _(sp):
                        sp.dma_start(attn[:], gat_attn.to_broadcast([P, D])).then_inc(s_in, 16)
                        with sp.Fori(0, T // CH // 2) as i:
                            for b in range(2):
                                ts = bass.ds((2 * i + b) * CH, CH)
                                sp.wait_ge(free[b], at(free[b], 1 + i))
                                sp.dma_start(idx[b][:], src_rows[:, ts]).then_inc(loaded[b], 16)
                                sp.dma_start(fd[b][:], sr[:, ts, :]).then_inc(loaded[b], 16)

                    @block.gpsimd
                    def _(pool):
                        with pool.Fori(0, T // CH // 2) as i:
                            for b in range(2):
                                pool.wait_ge(loaded[b], at(loaded[b], 32 * (i + 1)))
                                pool.sem_inc(chunks_begun, 1)
                                for t in range(CH):
                                    row_gather(pool, rows[b][:, t, :], table, idx[b][:, t:t + 1]).then_inc(gathered[b], 16)

                    @block.vector
                    def _(v):
                        V = nc.vector
                        v.wait_ge(s_in, at(s_in, 16))
                        V.memset(tail[:], 0.0).then_inc(s_v, 1)
                        with v.Fori(0, T // CH // 2) as i:
                            for b in range(2):
                                start = at(s_v, 1) + (2 * i + b) * LINKS
                                link, count = chain(v, s_v, start)
                                v.wait_ge(s_v, start)
                                v.wait_ge(loaded[b], at(loaded[b], 32 * (i + 1)))
                                ts = bass.ds((2 * i + b) * CH, CH)
                                link(scans(V, fd[b], same[:, ts], fill, D))
                                link(V.tensor_copy(fill[:], fd[b][:, CH - 1, :]))
                                v.wait_ge(gathered[b], 16 * CH * (i + 1))
                                link(V.tensor_tensor(fd[b][:], fd[b][:], rows[b][:], ALU.add))
                                link(V.scalar_tensor_tensor(fd[b][:], fd[b][:], 0.2, fd[b][:], ALU.mult, ALU.max))
                                link(V.tensor_tensor(fd[b][:], fd[b][:], attn[:].rearrange("p (a f) -> p a f", a=1).to_broadcast([P, CH, D]), ALU.mult))
                                V.tensor_reduce(logit[:, ts], fd[b][:], AX.X, ALU.add).then_inc(s_v, 1)
                                assert count[0] + 1 == LINKS

                    @block.scalar
                    def _(act):
                        for b in range(2):
                            act.sem_inc(free[b], 1)
                        with act.Fori(0, T // CH // 2) as i:
                            for b in range(2):
                                act.wait_ge(s_v, at(s_v, 1) + (2 * i + b + 1) * LINKS)
                                act.dma_start(zg[:, bass.ds((2 * i + b) * CH, CH), :], rows[b][:]).then_inc(stored[b], 16)
                                act.wait_ge(stored[b], at(stored[b], 16 * (i + 1)))
                                act.sem_inc(free[b], 1)
            n = T // CH // 2
            close(s_in, 16)
            close(s_v, 1 + 2 * n * LINKS)
            for b in range(2):
                close(free[b], 1 + n)
                close(loaded[b], 32 * n)
                close(stored[b], 16 * n)

        def gat_max_stage(logit, st):
            def sb(name, shape, dt=F32):
                return st.enter_context(nc.sbuf_tensor(name, shape, dt))
            pen = sb("pen", [P, T])
            top_f = sb("top_f", [P, T])
            work = sb("work_gat", [P, T])
            cols = sb("cols", [P, 4])
            diag = sb("diag", [P, 4, P])
            cand = sb("cand", [P, 4, P])
            mask = sb("mask", [P, 4, P])
            tops = sb("tops", [P, 2])
            with ExitStack() as pst:
                pr = pst.enter_context(nc.psum_tensor("pr", [P, 4, P], F32))
                with nc.Block() as block:
                    @block.vector
                    def _(v):
                        V = nc.vector
                        start = at(s_v, 0)
                        link, count = chain(v, s_v, start)
                        link(V.tensor_scalar(pen[:], same[:], BIG, -BIG, ALU.mult, ALU.add))
                        link(V.tensor_tensor_scan(top_f[:], pen[:], logit[:], -BIG, ALU.add, ALU.max))
                        link(V.memset(work[:, T - 1:T], -BIG))
                        link(V.tensor_copy(work[:, 0:T - 1], pen[:, 1:T]))
                        link(V.tensor_tensor_scan(top_f[:, ::-1], work[:, ::-1], top_f[:, ::-1], -BIG, ALU.add, ALU.max))
                        link(V.tensor_copy(cols[:, 0:1], first_f[:]))
                        link(V.tensor_copy(cols[:, 1:2], last_f[:]))
                        link(V.tensor_copy(cols[:, 2:3], top_f[:, 0:1]))
                        link(V.tensor_copy(cols[:, 3:4], top_f[:, T - 1:T]))
                        for k in range(4):
                            ins = V.tensor_scalar(diag[:, k, :], ident[:], cols[:, k:k + 1], None, ALU.mult)
                        ins.then_inc(s_vdone, 1)
                        v.wait_ge(s_pe, at(s_pe, 1))
                        for k in range(2):
                            for h in range(2):
                                link(V.tensor_scalar(mask[:, 2 * k + h, :], pr[:, h, :], cols[:, k:k + 1], None, ALU.is_equal))
                                link(V.tensor_tensor(cand[:, 2 * k + h, :], mask[:, 2 * k + h, :], pr[:, 2 + h, :], ALU.mult))
                                link(V.tensor_scalar(mask[:, 2 * k + h, :], mask[:, 2 * k + h, :], BIG, -BIG, ALU.mult, ALU.add))
                                link(V.tensor_tensor(cand[:, 2 * k + h, :], cand[:, 2 * k + h, :], mask[:, 2 * k + h, :], ALU.add))
                        for k in range(2):
                            link(V.tensor_reduce(tops[:, k:k + 1], cand[:, 2 * k:2 * k + 2, :].rearrange("p a q -> p (a q)"), AX.X, ALU.max))
                            link(V.tensor_scalar(work[:], dst_f[:], cols[:, k:k + 1], None, ALU.is_equal))
                            link(V.tensor_scalar(pen[:], work[:], BIG, -BIG, ALU.mult, ALU.add))
                            link(V.scalar_tensor_tensor(work[:], work[:], tops[:, k:k + 1], pen[:], ALU.mult, ALU.add))
                            link(V.tensor_tensor(top_f[:], top_f[:], work[:], ALU.max))
                        V.tensor_tensor(logit[:], logit[:], top_f[:], ALU.subtract).then_inc(s_vdone, 1)
                        close(s_v, count[0])

                    @block.tensor
                    def _(pe):
                        pe.wait_ge(s_vdone, at(s_vdone, 1))
                        nc.tensor.matmul(pr[:].rearrange("p a q -> p (a q)"), ones[:], diag[:].rearrange("p a q -> p (a q)"),
                                         start=True, stop=True).then_inc(s_pe, 1)

                    @block.scalar
                    def _(act):
                        act.wait_ge(s_vdone, at(s_vdone, 2))
                        nc.scalar.activation(logit[:], logit[:], ACT.Exp).then_inc(s_act, 1)
            close(s_vdone, 2)
            close(s_pe, 1)
            close(s_act, 1)

        def gat_sum_pass(weight):
            CH = C_MSG
            with ExitStack() as st:
                def sb(name, shape, dt=F32):
                    return st.enter_context(nc.sbuf_tensor(name, shape, dt))
                rows = [sb(f"g_gs{b}", [P, CH, D]) for b in range(2)]
                prod = [sb(f"prod_gs{b}", [P, CH, D + 1]) for b in range(2)]
                zg = gathered_rows.rearrange("(p t) f -> p t f", p=P)
                z = scanned_rows33.rearrange("(p t) f -> p t f", p=P)
                with nc.Block() as block:
                    @block.sync
                    def _(sp):
                        with sp.Fori(0, T // CH // 2) as i:
                            for b in range(2):
                                ts = bass.ds((2 * i + b) * CH, CH)
                                sp.wait_ge(free[b], at(free[b], 1 + i))
                                sp.dma_start(rows[b][:], zg[:, ts, :]).then_inc(loaded[b], 16)

                    @block.vector
                    def _(v):
                        V = nc.vector
                        V.memset(tail[:], 0.0).then_inc(s_v, 1)
                        with v.Fori(0, T // CH // 2) as i:
                            for b in range(2):
                                ts = bass.ds((2 * i + b) * CH, CH)
                                k = at(s_v, 1) + 6 * i + 3 * b
                                v.wait_ge(s_v, k)
                                v.wait_ge(loaded[b], at(loaded[b], 16 * (i + 1)))
                                w = weight[:, ts].rearrange("p (t a) -> p t a", a=1)
                                V.tensor_copy(prod[b][:, :, D:D + 1], w)
                                V.tensor_tensor(prod[b][:, :, 0:D], rows[b][:], w.to_broadcast([P, CH, D]), ALU.mult).then_inc(s_v, 1)
                                v.wait_ge(s_v, k + 1)
                                scans(V, prod[b], same[:, ts], tail, D + 1).then_inc(s_v, 1)
                                v.wait_ge(s_v, k + 2)
                                V.tensor_copy(tail[:], prod[b][:, CH - 1, :]).then_inc(s_v, 1)

                    @block.scalar
                    def _(act):
                        for b in range(2):
                            act.sem_inc(free[b], 1)
                        with act.Fori(0, T // CH // 2) as i:
                            for b in range(2):
                                act.wait_ge(s_v, at(s_v, 4) + 6 * i + 3 * b)
                                act.dma_start(z[:, bass.ds((2 * i + b) * CH, CH), :], prod[b][:]).then_inc(stored[b], 16)
                                act.wait_ge(stored[b], at(stored[b], 16 * (i + 1)))
                                act.sem_inc(free[b], 1)
            n = T // CH // 2
            close(s_v, 1 + 6 * n)
            for b in range(2):
                close(free[b], 1 + n)
                close(loaded[b], 16 * n)
                close(stored[b], 16 * n)

        def l2_pass():
            CH = C_MSG
            Q = CH // 4
            NG, KM = 6, 16 * M
            NT = NG * KM
            NS, NV = P, 112
            LOW = 2.0 ** 11
            GAIN = 1.593
            PW_S, PW_V = 0.17677669529663687, 0.25
            KAP = math.sqrt(2.0) / math.sqrt(10.0) / 4.0
            n = T // CH // 2
            F16 = mybir.dt.float16
            gathered = gather_signals("l2")
            with ExitStack() as st:
                def sb(name, shape, dt=F32):
                    return st.enter_context(nc.sbuf_tensor(name, shape, dt))

                def ps(name, shape, dt=F32):
                    return st.enter_context(nc.psum_tensor(name, shape, dt))
                idx = [sb(f"idx_l2{b}", [P, CH], I32) for b in range(2)]
                z = [sb(f"z_l2{b}", [P, CH, 80]) for b in range(2)]
                zs = [sb(f"zs{b}", [P, CH, NS], F16) for b in range(2)]
                zv = [sb(f"zv{b}", [P, CH, NV], F16) for b in range(2)]
                hid = [sb(f"h_l2{b}", [P, CH, 16]) for b in range(2)]
                vec = [sb(f"vec{b}", [P, CH, 3]) for b in range(2)]
                ew = [sb(f"ew{b}", [P, CH]) for b in range(2)]
                msg = sb("msg_l2", [P, CH, D])
                prod = [sb(f"prod{b}", [P, NG, 4, 16, M]) for b in range(2)]
                zst = [sb(f"zst{b}", [NS, 4 * P], F16) for b in range(2)]
                zvt = [sb(f"zvt{b}", [NV, 4 * P], F16) for b in range(2)]
                ws = [sb(f"ws{k}", [NS, 3 * KM], BF16) for k in range(2)]
                wv = [sb(f"wv{k}", [NV, 3 * KM], BF16) for k in range(3)]
                ident_h = sb("ident_h", [P, P], F16)
                pv = spread[:, 0:CH * 48].rearrange("p (t m i) -> p t m i", m=2 * M, i=3)
                res_s = sq[:].rearrange("p j f -> p (j f)")[:, 0:Q * 96].rearrange("p (q g t w) -> p q g t w", g=3, t=4, w=M)
                th = sq[:].rearrange("p j f -> p (j f)")[:, Q * 96:Q * 160].rearrange("p (q g t w) -> p q g t w", g=2, t=4, w=M)
                res_v = [agg[:, k * Q * 96:(k + 1) * Q * 96].rearrange("p (q g t w) -> p q g t w", g=3, t=4, w=M) for k in range(2)]
                p_z = ps("p_z", [P, 2, 512], F16)
                p_t = [ps(f"p_t{b}", [P, 3 * 512]) for b in range(2)]
                p_r = ps("p_r", [P, 96])
                loaded2 = [signal(f"loaded2{b}") for b in range(2)]
                s_prep = signal("s_prep")
                p_done = signal("p_done")
                h_split = signal("h_split")
                d_done = signal("d_done")
                z_split = signal("z_split")
                transposed = signal("transposed")
                zt_ready = signal("zt_ready")
                t_made = signal("t_made")
                t_used = signal("t_used")
                red_made = signal("red_made")
                red_out = signal("red_out")
                res_done = signal("res_done")
                th_done = signal("th_done")
                zr = scanned_rows.rearrange("(p t) f -> p t f", p=P)
                sr = start_rows.rearrange("(p t) f -> p t f", p=P)
                w2v = w2.rearrange("k (i u w) -> i u k w", i=7, u=16)

                room = [0]

                def wsb(rows, cols):
                    room[0] += cols
                    return prod[0][0:rows].rearrange("p g t k w -> p (g t k w)")[:, room[0] - cols:room[0]]
                f_s = wsb(NS, 3 * KM)
                f_p = wsb(NS, KM)
                f_v = wsb(NV, 3 * KM)
                f_e = wsb(NV, 3 * KM)
                r_s = wsb(NS, 3 * KM)
                r_v = wsb(NV, 3 * KM)
                b_s = sb("b_s", [NS, 3 * KM], BF16)
                with nc.Block() as block:
                    plan = []
                    for r in (0, 32, 64, 96):
                        plan += [(f_s, r, 1, g, i) for g, i in ((0, 0), (1, 2), (2, 4))]
                        plan += [(f_s, r + 16, 1, g, i) for g, i in ((0, 1), (1, 3))]
                        plan += [(f_p, r + 16, 1, 0, 6)]
                    for r in (0, 64):
                        for c in range(3):
                            plan += [(f_v, r + c, 3, c, 5), (f_e, r + c, 3, c, 6)]

                    @block.sync
                    def _(sp):
                        sp.wait_ge(s_vdone, at(s_vdone, 1))
                        with nc.allow_non_contiguous_dma(reason="weights, in runs of 8"):
                            for t, r, step, g, i in plan:
                                sp.dma_start(t[r:r + 15 * step + 1:step, g * KM:(g + 1) * KM].rearrange("u (k w) -> u k w", w=M),
                                             w2v[i]).then_inc(s_in, 16)

                    @block.gpsimd
                    def _(pool):
                        row_gather(pool, fill[:], table, first_row[:]).then_inc(s_agg, 16)
                        pool.wait_ge(s_agg, at(s_agg, 16))

                    @block.vector
                    def _(v):
                        V = nc.vector
                        for t in (f_s, f_p, f_v):
                            V.memset(t[:], 0.0)
                        for t in zv:
                            V.memset(t[:], 0.0)
                        V.memset(f_e[:], 0.0).then_inc(s_vdone, 1)
                        start = at(s_v, 0)
                        link, count = chain(v, s_v, start)
                        link(V.tensor_copy(ident_h[:], ident[:]))
                        v.wait_ge(s_in, at(s_in, 16 * len(plan)))
                        link(V.tensor_scalar(f_s[:, 0:2 * KM], f_s[:, 0:2 * KM], KAP * PW_S, None, ALU.mult))
                        link(V.tensor_scalar(f_s[:, 2 * KM:], f_s[:, 2 * KM:], KAP * PW_V, None, ALU.mult))
                        link(V.scalar_tensor_tensor(f_s[:, 2 * KM:], f_p[:], KAP * PW_V * math.sqrt(1.5), f_s[:, 2 * KM:], ALU.mult, ALU.add))
                        link(V.tensor_scalar(f_v[:], f_v[:], KAP * PW_V / math.sqrt(3.0), None, ALU.mult))
                        link(V.scalar_tensor_tensor(f_v[:], f_e[:], -KAP * PW_V * math.sqrt(1.5) / 3.0, f_v[:], ALU.mult, ALU.add))
                        link(V.tensor_scalar(f_s[32:64, :], f_s[32:64, :], 1.0 / LOW, None, ALU.mult))
                        link(V.tensor_scalar(f_s[96:128, :], f_s[96:128, :], 1.0 / LOW, None, ALU.mult))
                        link(V.tensor_scalar(f_v[64:NV, :], f_v[64:NV, :], 1.0 / LOW, None, ALU.mult))
                        link(V.tensor_copy(ws[0][:], f_s[:]))
                        link(V.tensor_tensor(r_s[:], f_s[:], ws[0][:], ALU.subtract))
                        link(V.tensor_copy(b_s[:], r_s[:]))
                        link(V.tensor_tensor(r_s[:], r_s[:], b_s[:], ALU.subtract))
                        link(V.tensor_copy(ws[0][64:128, :], b_s[64:128, :]))
                        link(V.tensor_copy(ws[1][:], r_s[:]))
                        link(V.tensor_copy(wv[0][:], f_v[:]))
                        link(V.tensor_tensor(r_v[:], f_v[:], wv[0][:], ALU.subtract))
                        link(V.tensor_copy(wv[1][:], r_v[:]))
                        link(V.tensor_tensor(r_v[:], r_v[:], wv[1][:], ALU.subtract))
                        link(V.tensor_copy(wv[2][:], r_v[:]))
                        close(s_v, count[0])
                close(s_in, 16 * len(plan))
                close(s_vdone, 1)
                close(s_agg, 16)

                PREP, TAIL = 3, 7
                P_AT, D_AT = 9, 10

                with nc.Block() as block:
                    @block.sync
                    def _(sp):
                        def load_rows(c, b):
                            ts = bass.ds(c * CH, CH)
                            sp.dma_start(idx[b][:], src_rows[:, ts]).then_inc(loaded[b], 16)
                            sp.dma_start(z[b][:, :, D:2 * D], sr[:, ts, :]).then_inc(loaded[b], 16)

                        def load_rest(c, b):
                            ts = bass.ds(c * CH, CH)
                            sp.dma_start(hid[b][:], hidden[:, ts, :]).then_inc(loaded2[b], 16)
                            sp.dma_start(vec[b][:], unit[:, ts, :]).then_inc(loaded2[b], 16)
                            sp.dma_start(ew[b][:], edge_w[:, ts]).then_inc(loaded2[b], 16)

                        def store(c, b, times):
                            sp.wait_ge(s_v, at(s_v, 1) + (c + 1) * TAIL)
                            sp.dma_start(zr[:, bass.ds(c * CH, CH), :], msg[:]).then_inc(stored[b], 16)
                            sp.wait_ge(stored[b], at(stored[b], 16) + 16 * times)
                        for b in range(2):
                            load_rows(b, b)
                            load_rest(b, b)
                        with sp.Fori(1, n) as i:
                            for b in range(2):
                                c = 2 * i + b
                                sp.wait_ge(z_split, c - 1)
                                load_rows(c, b)
                                store(c - 2, b, i - 1)
                                load_rest(c, b)
                        for b in range(2):
                            store(2 * n - 2 + b, b, n - 1)

                    @block.gpsimd
                    def _(pool):
                        with pool.Fori(0, n) as i:
                            for b in range(2):
                                pool.wait_ge(loaded[b], at(loaded[b], 32 * (i + 1)))
                                pool.sem_inc(chunks_begun, 1)
                                for t in range(CH):
                                    row_gather(pool, z[b][:, t, 0:D], table, idx[b][:, t:t + 1]).then_inc(gathered[b], 16)

                    @block.tensor
                    def _(pe):
                        def cut(a, e):
                            while a < e:
                                m = min(e, (a // 512 + 1) * 512)
                                yield a, m
                                a = m

                        pe.sem_inc(red_made, 2)
                        with pe.Fori(0, n) as i:
                            for b in range(2):
                                c = 2 * i + b

                                def transposes(q):
                                    pe.wait_ge(zt_ready, c * Q + q + 1)
                                    for t in range(4):
                                        nc.tensor.transpose(p_z[:, 0, t * P:(t + 1) * P], zs[b][:, 4 * q + t, :], ident_h[:])
                                        last = nc.tensor.transpose(p_z[0:NV, 1, t * P:(t + 1) * P], zv[b][:, 4 * q + t, :], ident_h[:])
                                    last.then_inc(transposed, 1)

                                def products(q):
                                    pe.wait_ge(zt_ready, c * Q + q + 2)
                                    for pair in range(2):
                                        pe.wait_ge(t_used, 2 * (c * Q + q) + pair + 1)
                                        for t in range(2):
                                            col = slice((2 * pair + t) * P, (2 * pair + t + 1) * P)
                                            last = None
                                            for lhs, parts, base in (
                                                    (zst[q % 2], ((ws[0], NS), (ws[1], 64)), 0),
                                                    (zvt[q % 2], tuple((w, NV) for w in wv), 3 * KM)):
                                                off = t * NT + base
                                                for k, (w, rows) in enumerate(parts):
                                                    for a, e in cut(off, off + 3 * KM):
                                                        last = nc.tensor.matmul(p_t[pair][:, a:e], lhs[0:rows, col], w[0:rows, a - off:e - off],
                                                                                start=(k == 0), stop=(k == len(parts) - 1))
                                        last.then_inc(t_made, 1)

                                def sums(q):
                                    pe.wait_ge(t_used, 2 * (c * Q + q) + 4)
                                    pe.wait_ge(red_out, c * Q + q + 1)
                                    for k in range(16):
                                        last = nc.tensor.matmul(p_r[:], ident[:],
                                                                prod[q % 2][:, 3:6, :, k, :].rearrange("p g t w -> p (g t) w"),
                                                                start=(k == 0), stop=(k == 15))
                                    last.then_inc(red_made, 1)

                                pe.wait_ge(z_split, c + 1)
                                transposes(0)
                                for q in range(Q):
                                    pe.wait_ge(zt_ready, c * Q + q + 2)
                                    if q + 1 < Q:
                                        transposes(q + 1)
                                    products(q)
                                    if q >= 1:
                                        sums(q - 1)
                                sums(Q - 1)

                    @block.scalar
                    def _(act):
                        A = nc.scalar

                        def high(c, b):
                            act.wait_ge(p_done, c + 1)
                            sc = z[b][:, :, 0:2 * D].rearrange("p t (e f) -> p t e f", e=2)
                            for r in (0, 64):
                                A.activation(zs[b][:, :, r:r + 16].rearrange("p t (e f) -> p t e f", e=2), sc[:, :, :, 0:M], ACT.Copy)
                                A.activation(zs[b][:, :, r + 16:r + 32], z[b][:, :, 2 * D:80], ACT.Copy)
                            A.activation(zv[b][:, :, 0:48].rearrange("p t (e f) -> p t e f", e=2), sc[:, :, :, M:D], ACT.Copy).then_inc(h_split, 1)

                        def low(c, b):
                            act.wait_ge(d_done, c + 1)
                            sc = z[b][:, :, 0:2 * D].rearrange("p t (e f) -> p t e f", e=2)
                            for r in (32, 96):
                                A.activation(zs[b][:, :, r:r + 16].rearrange("p t (e f) -> p t e f", e=2), sc[:, :, :, 0:M], ACT.Copy, scale=LOW)
                                A.activation(zs[b][:, :, r + 16:r + 32], z[b][:, :, 2 * D:80], ACT.Copy, scale=LOW)
                            A.activation(zv[b][:, :, 64:NV].rearrange("p t (e f) -> p t e f", e=2), sc[:, :, :, M:D], ACT.Copy, scale=LOW).then_inc(z_split, 1)

                        def turned(c, q):
                            act.wait_ge(transposed, c * Q + q + 1)
                            if q >= 2:
                                act.wait_ge(t_made, 2 * (c * Q + q - 1))
                            A.activation(zst[q % 2][:], p_z[:, 0, :], ACT.Copy)
                            A.activation(zvt[q % 2][:], p_z[0:NV, 1, :], ACT.Copy).then_inc(zt_ready, 1)

                        def summed(c, b, q):
                            act.wait_ge(red_made, c * Q + q + 3)
                            A.activation(res_v[b][:, q].rearrange("p g t w -> p (g t w)"), p_r[:], ACT.Copy).then_inc(red_out, 1)

                        def one_chunk(c, b, more):
                            turned(c, 0)
                            for q in range(Q):
                                if q + 1 < Q:
                                    turned(c, q + 1)
                                if q >= 1:
                                    summed(c, b, q - 1)
                                if more and q == P_AT + 1:
                                    high(c + 1, 1 - b)
                                if more and q == D_AT + 2:
                                    low(c + 1, 1 - b)
                            summed(c, b, Q - 1)
                            act.wait_ge(res_done, c + 1)
                            A.activation(th.rearrange("p q g t w -> p q (g t w)"),
                                         res_s[:, :, 0:2].rearrange("p q g t w -> p q (g t w)"), ACT.Tanh).then_inc(th_done, 1)

                        act.sem_inc(zt_ready, 1)
                        act.sem_inc(red_out, 1)
                        high(0, 0)
                        low(0, 0)
                        with act.Fori(0, n - 1) as i:
                            for b in range(2):
                                one_chunk(2 * i + b, b, True)
                        one_chunk(2 * n - 2, 0, True)
                        one_chunk(2 * n - 1, 1, False)

                    @block.vector
                    def _(v):
                        V = nc.vector

                        def unit_of(b, m):
                            return vec[b][:].rearrange("p t (a i) -> p t a i", a=1).to_broadcast([P, CH, m, 3])

                        def prepare_z(c, b, times):
                            link, count = chain(v, s_prep, c * PREP)
                            v.wait_ge(loaded[b], at(loaded[b], 32) + 32 * times)
                            v.wait_ge(loaded2[b], 48 + 48 * times)
                            ts = bass.ds(c * CH, CH)
                            link(scans(V, z[b][:, :, D:2 * D], same[:, ts], fill, D))
                            link(V.tensor_copy(fill[:], z[b][:, CH - 1, D:2 * D]))
                            v.wait_ge(gathered[b], 16 * CH + 16 * CH * times)
                            V.tensor_tensor(pv[:, :, 0:M, :], z[b][:, :, M:D].rearrange("p t (m i) -> p t m i", i=3), unit_of(b, M), ALU.mult)
                            link(V.tensor_tensor(pv[:, :, M:2 * M, :], z[b][:, :, D + M:2 * D].rearrange("p t (m i) -> p t m i", i=3), unit_of(b, M), ALU.mult))
                            V.tensor_reduce(z[b][:, :, 2 * D:80], pv, AX.X, ALU.add).then_inc(p_done, 1)

                        def leave(c, b):
                            v.wait_ge(h_split, c + 1)
                            sc = z[b][:, :, 0:2 * D].rearrange("p t (e f) -> p t e f", e=2)
                            V.tensor_tensor(sc[:, :, :, 0:M], sc[:, :, :, 0:M], zs[b][:, :, 0:16].rearrange("p t (e f) -> p t e f", e=2), ALU.subtract)
                            V.tensor_tensor(z[b][:, :, 2 * D:80], z[b][:, :, 2 * D:80], zs[b][:, :, 16:32], ALU.subtract)
                            V.tensor_tensor(sc[:, :, :, M:D], sc[:, :, :, M:D], zv[b][:, :, 0:48].rearrange("p t (e f) -> p t e f", e=2), ALU.subtract).then_inc(d_done, 1)
                            v.wait_ge(d_done, c + 1)

                        def quadruple(c, b, q):
                            v.wait_ge(red_made, c * Q + q + 1)
                            for pair in range(2):
                                v.wait_ge(t_made, 2 * (c * Q + q) + pair + 1)
                                for t in range(2):
                                    h = hid[b][:, 4 * q + 2 * pair + t, :].rearrange("p (a k e) -> p a k e", a=1, e=1).to_broadcast([P, NG, 16, M])
                                    ins = V.tensor_tensor(prod[q % 2][:, :, 2 * pair + t],
                                                          p_t[pair][:, t * NT:(t + 1) * NT].rearrange("p (g k w) -> p g k w", g=NG, k=16), h, ALU.mult)
                                ins.then_inc(t_used, 1)
                            v.wait_ge(t_used, 2 * (c * Q + q) + 4)
                            return V.tensor_reduce(res_s[:, q].rearrange("p g t w -> p (g t) w"),
                                                   prod[q % 2][:, 0:3].rearrange("p g t k w -> p (g t) w k"), AX.X, ALU.add)

                        def messages(c, b, more):
                            link, count = chain(v, s_v, at(s_v, 1) + c * TAIL)
                            if not more:
                                v.wait_ge(stored[1 - b], at(stored[1 - b], 16 * n))
                            v.wait_ge(res_done, c + 1)
                            v.wait_ge(red_out, c * Q + Q + 1)
                            m4 = msg[:].rearrange("p (q t) f -> p q t f", t=4)
                            n4 = vec[b][:].rearrange("p (q t) k -> p q t k", t=4)

                            def o(k):
                                return m4[:, :, :, M + k:D:3]
                            for k in range(3):
                                ins = V.tensor_tensor(o(k), res_s[:, :, 2], n4[:, :, :, k:k + 1].to_broadcast([P, Q, 4, M]), ALU.mult)
                            link(ins)
                            for k in range(3):
                                ins = V.tensor_tensor(o(k), o(k), res_v[b][:, :, k], ALU.add)
                            link(ins)
                            link(V.tensor_scalar(ew[b][:], ew[b][:], GAIN, None, ALU.mult))
                            v.wait_ge(th_done, c + 1)
                            for k in range(3):
                                V.tensor_tensor(o(k), o(k), th[:, :, 1], ALU.mult)
                            link(V.tensor_copy(m4[:, :, :, 0:M], th[:, :, 0]))
                            link(V.tensor_tensor(msg[:], msg[:], ew[b][:].rearrange("p (t a) -> p t a", a=1).to_broadcast([P, CH, D]), ALU.mult))
                            link(scans(V, msg, same[:, bass.ds(c * CH, CH)], tail, D))
                            link(V.tensor_copy(tail[:, 0:D], msg[:, CH - 1, :]))
                            counts[0] = count[0]

                        counts = [0]

                        def one_chunk(c, b, times, more):
                            for q in range(Q):
                                last = quadruple(c, b, q)
                                if q == Q - 1:
                                    last.then_inc(res_done, 1)
                                if more and q == P_AT:
                                    prepare_z(c + 1, 1 - b, times)
                                if more and q == D_AT:
                                    leave(c + 1, 1 - b)
                            messages(c, b, more)

                        V.memset(tail[:], 0.0).then_inc(s_v, 1)
                        v.wait_ge(s_v, at(s_v, 1))
                        v.sem_inc(t_used, 2)
                        prepare_z(0, 0, 0)
                        leave(0, 0)
                        with v.Fori(0, n - 1) as i:
                            one_chunk(2 * i, 0, i, True)
                            one_chunk(2 * i + 1, 1, i + 1, True)
                        one_chunk(2 * n - 2, 0, n - 1, True)
                        one_chunk(2 * n - 1, 1, n, False)
                        assert counts[0] == TAIL, counts
            close(s_v, 1 + 2 * n * TAIL)
            for b in range(2):
                close(loaded[b], 32 * n)
                close(stored[b], 16 * n)

        with ExitStack() as st:
            lo_f = st.enter_context(nc.sbuf_tensor("lo_f", [P, T], BF16))
            hi_f = st.enter_context(nc.sbuf_tensor("hi_f", [P, T], BF16))
            iota_b = st.enter_context(nc.sbuf_tensor("iota_b", [P, P], BF16))
            prepare(lo_f, hi_f, iota_b)
            l0_table()
            l0_pass(lo_f, hi_f, iota_b)
        residual_norm_stage("l0", scanned_rows, D, "plain", scale_table=True)
        with ExitStack() as st:
            x1 = st.enter_context(nc.sbuf_tensor("cheb_x1", [P, NJ, D], F32))
            x2 = st.enter_context(nc.sbuf_tensor("cheb_x2", [P, NJ, D], F32))
            h = st.enter_context(nc.sbuf_tensor("cheb_h", [P, NJ, D], F32))
            for r, x0 in enumerate((x_cur, h)):
                sum_pass(f"cheb{r}a")
                cheb_step_stage(f"cs{r}a", x0, x1, x2, True)
                sum_pass(f"cheb{r}b")
                cheb_step_stage(f"cs{r}b", x0, x1, x2, False)
                cheb_mix_stage(f"mix{r}", [x0, x1, x2], h, gat=(r == 1))
        with ExitStack() as st:
            logit = st.enter_context(nc.sbuf_tensor("logit", [P, T], F32))
            gat_logit_pass(logit)
            with ExitStack() as st2:
                gat_max_stage(logit, st2)
            gat_sum_pass(logit)
        residual_norm_stage("gat", scanned_rows33, D + 1, "start")
        l2_pass()
        residual_norm_stage("l2", scanned_rows, D, "plain")
        sum_pass("l3")
        residual_norm_stage("l3", scanned_rows, D, "plain", last=True)


def kernel(**inputs):
    import numpy as np
    import concourse.bacc as bacc
    from concourse.bass_utils import run_bass_kernel_spmd as run

    a = {k: np.asarray(v) for k, v in inputs.items()}
    n_nodes, n_edges = a["x"].shape[0], a["src"].shape[0]
    NJ, T = shapes(n_nodes, n_edges)

    def by_edge(v, pad):
        full = np.full((P * T,) + v.shape[1:], pad, v.dtype)
        full[:n_edges] = v
        return full.reshape((P, T) + v.shape[1:])

    x = np.zeros((NJ * P, D), a["x"].dtype)
    x[:n_nodes] = a["x"]
    emb = by_edge(a["edge_attr_10"], 0)
    arrays = {
        "x": np.ascontiguousarray(x.reshape(NJ, P, D).transpose(1, 0, 2)),
        "src": by_edge(a["src"], 0),
        "dst": by_edge(a["dst"], n_nodes),
        "emb_t": np.ascontiguousarray(emb.transpose(2, 1, 0)).reshape(10, T * P),
        "attr3": by_edge(a["edge_attr_3"], 1),
        "attr5": by_edge(a["edge_attr_5"], 0),
        "edge_w": by_edge(a["edge_weight"], 0),
        "edge_w1": by_edge(a["edge_weight1"].reshape(-1), 0),
        "l0_w": a["L0_gnn_W"], "lam": a["L1_gnn_lambda_max"], "cheb_w": a["L1_gnn_cheb_W"],
        "cheb_b": a["L1_gnn_cheb_b"], "gat_ws": a["L1_gnn_gat_W_src"], "gat_bs": a["L1_gnn_gat_b_src"],
        "gat_wd": a["L1_gnn_gat_W_dst"], "gat_bd": a["L1_gnn_gat_b_dst"], "gat_attn": a["L1_gnn_gat_attn"],
        "w1": a["L2_gnn_W1"], "w2": a["L2_gnn_W2"],
    }
    nc = bacc.Bacc("TRN2", target_bir_lowering=False, num_devices=1)
    args = [nc.dram_tensor(f"in_{k}", v.shape, mybir.dt.from_np(v.dtype), kind="ExternalInput").ap()
            for k, v in arrays.items()]
    out = nc.dram_tensor("out_x", (P, NJ, D), F32, kind="ExternalOutput").ap()
    gnn_kernel(nc, *args, out)
    r = run(nc, [{f"in_{k}": v for k, v in arrays.items()}], core_ids=[0])
    got = r.results[0]["out_x"]
    return np.ascontiguousarray(got.transpose(1, 0, 2)).reshape(NJ * P, D)[:n_nodes]
```

```python
from contextlib import ExitStack
import math

import concourse.bass as bass
from concourse import mybir

F32 = mybir.dt.float32
BF16 = mybir.dt.bfloat16
I32 = mybir.dt.int32
ALU = mybir.AluOpType
ACT = mybir.ActivationFunctionType
AX = mybir.AxisListType

P = 128
D = 32
M = 8
LOG_P = 7
EPS = 1e-5
BIG = 1e30
DEEP = -200.0


def shapes(n_nodes, n_edges):
    nj = -(-n_nodes // P)
    t = -(-(-(-n_edges // P)) // 784) * 784
    return nj, t


def chain(engine, sem, start):
    count = [0]

    def link(instruction):
        count[0] += 1
        instruction.then_inc(sem, 1)
        engine.wait_ge(sem, start + count[0])

    return link, count


def gnn_kernel(nc, x, src, dst, emb_t, attr3, attr5, edge_w, edge_w1, l0_w, lam, cheb_w, cheb_b,
               gat_ws, gat_bs, gat_wd, gat_bd, gat_attn, w1, w2, out):
    NJ = x.shape[1]
    T = src.shape[1]
    ROWS = P * NJ
    EP = P * T
    C_SUM = 98
    C_MSG = 56
    assert T % (2 * C_SUM) == 0 and T % (2 * C_MSG) == 0
    JB = 14
    BLOCKS = NJ // JB
    assert NJ % JB == 0 and JB * (D + 1) <= 512
    GROUPS = [(4 * g, min(4, NJ - 4 * g)) for g in range(-(-NJ // 4))]

    top = ExitStack()
    with top:
        def keep(name, shape, dt=F32):
            return top.enter_context(nc.sbuf_tensor(name, shape, dt))

        level = {}

        def signal(name):
            sem = top.enter_context(nc.semaphore(name))
            level[id(sem)] = 0
            return sem

        def at(sem, count):
            return level[id(sem)] + count

        def close(sem, count):
            level[id(sem)] += count

        src_rows = nc.dram_tensor("src_rows", [P, T], I32).ap()
        table_l0 = nc.dram_tensor("table_l0", [ROWS, 112], F32).ap()
        table = nc.dram_tensor("table", [ROWS, D], F32).ap()
        table_fd = nc.dram_tensor("table_fd", [ROWS, D], F32).ap()
        scanned_rows = nc.dram_tensor("scanned_rows", [EP, D], F32).ap()
        gat_rows = nc.dram_tensor("gat_rows", [EP, D + 2], F32).ap()
        start_rows = nc.dram_tensor("start_rows", [EP, D], F32).ap()
        hidden = nc.dram_tensor("hidden", [P, T, 16], F32).ap()
        unit = nc.dram_tensor("unit", [P, T, 3], F32).ap()

        x_cur = keep("x_cur", [P, NJ, D])
        same = keep("same", [P, T])
        end_i = keep("end_i", [P, NJ], I32)
        start_i = keep("start_i", [P, NJ], I32)
        nonempty = keep("nonempty", [P, NJ])
        dinv = keep("dinv", [P, NJ])
        cross_lo = keep("cross_lo", [P, P])
        cross_hi = keep("cross_hi", [P, NJ])
        first_f = keep("first_f", [P, 1])
        last_f = keep("last_f", [P, 1])
        first_row = keep("first_row", [P, 1], I32)
        ident = keep("ident", [P, P])
        ones = keep("ones", [P, P])
        iota_f = keep("iota_f", [P, P])
        eps = keep("eps", [P, 1])
        tail = keep("tail", [P, D + 1])
        fill = keep("fill", [P, D])
        lam_c = keep("lam_c", [P, 6])
        agg = keep("agg", [P, NJ * (D + 1)])
        spread = keep("spread", [P, NJ * (D + 1)])
        stat = keep("stat", [P, NJ, 4])
        sq = keep("sq", [P, NJ, D])

        s_in = signal("s_in")
        s_v = signal("s_v")
        s_pool = signal("s_pool")
        s_pe = signal("s_pe")
        s_act = signal("s_act")
        s_vdone = signal("s_vdone")
        s_write = signal("s_write")
        s_agg = signal("s_agg")
        fetched = [signal(f"fetched{k}") for k in range(BLOCKS)]
        s_scatter = signal("s_scatter")
        chunks_begun = signal("chunks_begun")
        s_tp = signal("s_tp")
        s_xt = signal("s_xt")
        s_mm = signal("s_mm")
        s_ev = signal("s_ev")
        free = [signal(f"free{b}") for b in range(2)]
        loaded = [signal(f"loaded{b}") for b in range(2)]
        stored = [signal(f"stored{b}") for b in range(2)]

        def gather_signals(tag):
            return [signal(f"gathered_{tag}{b}") for b in range(2)]

        def row_gather(pool, dest, table_ap, index):
            return pool.indirect_dma_start(out=dest, out_offset=None, in_=table_ap,
                                           in_offset=bass.IndirectOffsetOnAxis(ap=index, axis=0))

        def scans(v, buf, mask, carry, n):
            for f in range(n):
                last = v.tensor_tensor_scan(buf[:, :, f], mask, buf[:, :, f], carry[:, f:f + 1],
                                            ALU.mult, ALU.add)
            return last

        def prepare(lo_f, hi_f, iota_b):
            with ExitStack() as st:
                def sb(name, shape, dt=F32):
                    return st.enter_context(nc.sbuf_tensor(name, shape, dt))
                dst_f = sb("dst_f", [P, T])
                src_i = sb("src_i", [P, T], I32)
                dst_i = sb("dst_i", [P, T], I32)
                work_i = sb("work_i", [P, T], I32)
                iota_i = sb("iota_i", [P, P], I32)
                prev_i = sb("prev_i", [P, 1], I32)
                next_i = sb("next_i", [P, 1], I32)
                pn = sb("pn", [P, 4])
                part_i = sb("part_i", [P, 4], I32)
                cross_i = sb("cross_i", [P, 2], I32)

                with nc.Block() as block:
                    @block.gpsimd
                    def _(pool):
                        nc.gpsimd.iota(iota_i[:], [[1, P]], base=0, channel_multiplier=0).then_inc(s_pool, 1)
                        nc.gpsimd.memset(ones[:], 1.0).then_inc(s_pool, 1)
                        nc.gpsimd.memset(eps[:], EPS).then_inc(s_pool, 1)
                        nc.gpsimd.memset(prev_i[:], -1).then_inc(s_pool, 1)
                        nc.gpsimd.memset(next_i[:], -1).then_inc(s_pool, 1)
                        pool.wait_ge(s_pool, 5)
                        nc.gpsimd.affine_select(out=ident[:], in_=ones[:], compare_op=ALU.is_equal, fill=0.0,
                                                base=0, pattern=[[-1, P]], channel_multiplier=1).then_inc(s_pool, 1)

                    @block.sync
                    def _(sp):
                        sp.dma_start(dst_i[:], dst).then_inc(s_in, 16)
                        sp.dma_start(src_i[:], src).then_inc(s_in, 16)
                        sp.dma_start(x_cur[:], x).then_inc(s_in, 16)
                        sp.dma_start(lam_c[:, 0:1], lam.rearrange("(a b) -> a b", a=1).to_broadcast([P, 1])).then_inc(s_in, 16)
                        sp.wait_ge(s_pool, 5)
                        with nc.allow_non_contiguous_dma(reason="one word of each partition"):
                            sp.dma_start(prev_i[1:P, :], dst[0:P - 1, T - 1:T]).then_inc(s_in, 16)
                            sp.dma_start(next_i[0:P - 1, :], dst[1:P, 0:1]).then_inc(s_in, 16)
                        sp.wait_ge(s_vdone, 1)
                        sp.dma_start(src_rows, work_i[:]).then_inc(s_write, 16)
                        sp.wait_ge(s_write, 16)

                    @block.vector
                    def _(v):
                        start = 0
                        link, count = chain(v, s_v, start)
                        v.wait_ge(s_in, 96)
                        v.wait_ge(s_pool, 6)
                        link(nc.vector.tensor_scalar(work_i[:], src_i[:], P - 1, None, ALU.bitwise_and))
                        link(nc.vector.tensor_scalar(src_i[:], src_i[:], LOG_P, None, ALU.logical_shift_right))
                        ins = nc.vector.scalar_tensor_tensor(work_i[:], work_i[:], float(NJ), src_i[:], ALU.mult, ALU.add)
                        ins.then_inc(s_vdone, 1)
                        v.wait_ge(s_vdone, 1)
                        link(nc.vector.tensor_copy(dst_f[:], dst_i[:]))
                        link(nc.vector.tensor_tensor(same[:, 1:T], dst_f[:, 1:T], dst_f[:, 0:T - 1], ALU.is_equal))
                        link(nc.vector.tensor_copy(pn[:, 0:1], prev_i[:]))
                        link(nc.vector.tensor_copy(pn[:, 1:2], next_i[:]))
                        link(nc.vector.tensor_copy(first_f[:], dst_f[:, 0:1]))
                        link(nc.vector.tensor_copy(last_f[:], dst_f[:, T - 1:T]))
                        link(nc.vector.tensor_tensor(same[:, 0:1], pn[:, 0:1], first_f[:], ALU.is_equal))
                        link(nc.vector.tensor_tensor(pn[:, 2:3], pn[:, 1:2], last_f[:], ALU.is_equal))
                        link(nc.vector.tensor_scalar(part_i[:, 0:1], dst_i[:, 0:1], P - 1, None, ALU.bitwise_and))
                        link(nc.vector.tensor_scalar(part_i[:, 1:2], dst_i[:, 0:1], LOG_P, None, ALU.logical_shift_right))
                        link(nc.vector.scalar_tensor_tensor(first_row[:], part_i[:, 0:1], float(NJ), part_i[:, 1:2], ALU.mult, ALU.add))
                        link(nc.vector.tensor_scalar(cross_i[:, 0:1], dst_i[:, T - 1:T], P - 1, None, ALU.bitwise_and))
                        link(nc.vector.tensor_scalar(cross_i[:, 1:2], dst_i[:, T - 1:T], LOG_P, None, ALU.logical_shift_right))
                        link(nc.vector.tensor_copy(lam_c[:, 4:6], cross_i[:]))
                        link(nc.vector.tensor_copy(iota_f[:], iota_i[:]))
                        link(nc.vector.tensor_copy(iota_b[:], iota_i[:]))
                        link(nc.vector.tensor_scalar(cross_lo[:], iota_f[:], lam_c[:, 4:5], pn[:, 2:3], ALU.is_equal, ALU.mult))
                        link(nc.vector.tensor_scalar(cross_hi[:], iota_f[:, 0:NJ], lam_c[:, 5:6], None, ALU.is_equal))
                        link(nc.vector.tensor_scalar(src_i[:], dst_i[:], P - 1, None, ALU.bitwise_and))
                        link(nc.vector.tensor_copy(lo_f[:], src_i[:]))
                        link(nc.vector.tensor_scalar(src_i[:], dst_i[:], LOG_P, None, ALU.logical_shift_right))
                        link(nc.vector.tensor_copy(hi_f[:], src_i[:]))
                        link(nc.vector.reciprocal(lam_c[:, 1:2], lam_c[:, 0:1]))
                        link(nc.vector.tensor_scalar(lam_c[:, 0:1], lam_c[:, 1:2], -2.0, None, ALU.mult))
                        link(nc.vector.tensor_scalar(lam_c[:, 1:2], lam_c[:, 0:1], -1.0, -1.0, ALU.mult, ALU.add))
                        link(nc.vector.tensor_scalar(lam_c[:, 2:4], lam_c[:, 0:2], 2.0, None, ALU.mult))
                        close(s_v, count[0])
                close(s_in, 96)
                close(s_pool, 6)
                close(s_vdone, 1)
                close(s_write, 16)

        def fetch_sums(pool, dest, rows):
            for j in range(NJ):
                row_gather(pool, dest[:, j, :], rows, end_i[:, j:j + 1]).then_inc(fetched[j // JB], 16)

        def crossing_matmuls(pe, banks, n):
            pe.wait_ge(s_vdone, at(s_vdone, 1))
            for k in range(BLOCKS):
                if k >= 2:
                    pe.wait_ge(s_ev, at(s_ev, k - 1))
                nc.tensor.matmul(banks[k % 2][:, 0:JB * n], cross_lo[:], spread[:, k * JB * n:(k + 1) * JB * n],
                                 start=True, stop=True).then_inc(s_pe, 1)

        def spread_tails(n):
            nc.vector.tensor_tensor(
                spread[:, 0:NJ * n].rearrange("p (j f) -> p j f", f=n),
                cross_hi[:].rearrange("p (j a) -> p j a", a=1).to_broadcast([P, NJ, n]),
                tail[:, 0:n].rearrange("p (a f) -> p a f", a=1).to_broadcast([P, NJ, n]),
                ALU.mult).then_inc(s_vdone, 1)

        def block_of(k):
            return slice(k * JB, (k + 1) * JB)

        def block_sums(v, link, banks, n, k):
            v.wait_ge(fetched[k], at(fetched[k], 16 * JB))
            flat = agg[:, k * JB * n:(k + 1) * JB * n]
            a = flat.rearrange("p (j f) -> p j f", f=n)
            link(nc.vector.tensor_tensor(a, a, by_col(nonempty[:, block_of(k)]), ALU.mult))
            v.wait_ge(s_pe, at(s_pe, k + 1))
            nc.vector.tensor_tensor(flat, flat, banks[k % 2][:, 0:JB * n], ALU.add).then_inc(s_ev, 1)
            v.wait_ge(s_ev, at(s_ev, k + 1))
            return a

        def sums_closed():
            for k in range(BLOCKS):
                close(fetched[k], 16 * JB)
            close(s_pe, BLOCKS)
            close(s_ev, BLOCKS)
            close(s_vdone, 1)

        def by_col(t, n=D):
            m = t.shape[1]
            return t.rearrange("p (j a) -> p j a", a=1).to_broadcast([P, m, n])

        def layer_norm(v, link, js, act_done):
            t, s4, s2 = x_cur[:, js, :], stat[:, js, :], sq[:, js, :]
            link(nc.vector.tensor_reduce(s4[:, :, 0], t, AX.X, ALU.add))
            link(nc.vector.tensor_scalar(s4[:, :, 0], s4[:, :, 0], 1.0 / D, None, ALU.mult))
            link(nc.vector.tensor_tensor(t, t, s4[:, :, 0:1].to_broadcast([P, JB, D]), ALU.subtract))
            link(nc.vector.tensor_tensor(s2, t, t, ALU.mult))
            nc.vector.tensor_reduce(s4[:, :, 1], s2, AX.X, ALU.add).then_inc(s_vdone, 1)
            v.wait_ge(s_act, act_done)
            link(nc.vector.reciprocal(s4[:, :, 3], s4[:, :, 2]))
            link(nc.vector.tensor_tensor(t, t, s4[:, :, 3:4].to_broadcast([P, JB, D]), ALU.mult))

        def norm_root(act, js, ready):
            act.wait_ge(s_vdone, ready)
            nc.scalar.activation(stat[:, js, 2], stat[:, js, 1], ACT.Sqrt, bias=eps[:], scale=1.0 / D).then_inc(s_act, 1)

        def write_blocks(sp, dest, nodes, first, step):
            for k in range(BLOCKS):
                sp.wait_ge(s_vdone, at(s_vdone, first + k * step))
                sp.dma_start(dest[:, block_of(k), :], nodes[:, block_of(k), :]).then_inc(s_write, 16)
            sp.wait_ge(s_write, at(s_write, 16 * BLOCKS))

        def linear_group(pe, g, srcs, w_list, n, pt, xt, po, taken):
            j0, nj = GROUPS[g]
            if g >= 2:
                pe.wait_ge(s_xt, at(s_xt, g - 1))
            for k, s in enumerate(srcs):
                last = nc.tensor.transpose(pt[g % 2][0:nj * D, k * P:(k + 1) * P],
                                           s[:, j0:j0 + nj, :].rearrange("p j f -> p (j f)"), ident[:])
            last.then_inc(s_tp, 1)
            pe.wait_ge(s_xt, at(s_xt, g + 1))
            if g >= 2:
                pe.wait_ge(taken, at(taken, g - 1))
            for k in range(len(srcs)):
                last = nc.tensor.matmul(po[g % 2][:, 0:nj * n], xt[g % 2][0:nj * D, k * P:(k + 1) * P],
                                        w_list[k][0:nj * D, 0:nj * n],
                                        start=(k == 0), stop=(k == len(srcs) - 1))
            last.then_inc(s_mm, 1)

        def linear_pe(pe, srcs, w_list, n, pt, xt, po):
            for g in range(len(GROUPS)):
                linear_group(pe, g, srcs, w_list, n, pt, xt, po, s_ev)

        def linear_act(act, n_srcs, pt, xt):
            for g, (j0, nj) in enumerate(GROUPS):
                act.wait_ge(s_tp, at(s_tp, g + 1))
                if g >= 2:
                    act.wait_ge(s_mm, at(s_mm, g - 1))
                nc.scalar.activation(xt[g % 2][0:nj * D, 0:n_srcs * P], pt[g % 2][0:nj * D, 0:n_srcs * P],
                                     ACT.Copy).then_inc(s_xt, 1)

        def linear_out(v, dest, n, po, bias=None):
            for g, (j0, nj) in enumerate(GROUPS):
                v.wait_ge(s_mm, at(s_mm, g + 1))
                got = po[g % 2][:, 0:nj * n].rearrange("p (j f) -> p j f", f=n)
                if bias is None:
                    nc.vector.tensor_copy(dest[:, j0:j0 + nj, :], got).then_inc(s_ev, 1)
                else:
                    nc.vector.tensor_tensor(dest[:, j0:j0 + nj, :], got,
                                            bias[:, 0:n].rearrange("p (a f) -> p a f", a=1).to_broadcast([P, nj, n]),
                                            ALU.add).then_inc(s_ev, 1)
            v.wait_ge(s_ev, at(s_ev, len(GROUPS)))

        def linear_closed():
            for s in (s_tp, s_xt, s_mm, s_ev):
                close(s, len(GROUPS))

        def replicate(sp, w, n):
            for k in range(1, 4):
                sp.dma_start(w[k * D:(k + 1) * D, k * n:(k + 1) * n], w[0:D, 0:n]).then_inc(s_write, 16)

        def sum_pass(tag):
            CH = C_SUM
            gathered = gather_signals(tag)
            with ExitStack() as st:
                idx = [st.enter_context(nc.sbuf_tensor(f"idx_{tag}{b}", [P, CH], I32)) for b in range(2)]
                rows = [st.enter_context(nc.sbuf_tensor(f"rows_{tag}{b}", [P, CH, D], F32)) for b in range(2)]
                z = scanned_rows.rearrange("(p t) f -> p t f", p=P)
                with nc.Block() as block:
                    @block.sync
                    def _(sp):
                        with sp.Fori(0, T // CH // 2) as i:
                            for b in range(2):
                                sp.wait_ge(free[b], at(free[b], 1 + i))
                                sp.dma_start(idx[b][:], src_rows[:, bass.ds((2 * i + b) * CH, CH)]).then_inc(loaded[b], 16)

                    @block.gpsimd
                    def _(pool):
                        with pool.Fori(0, T // CH // 2) as i:
                            for b in range(2):
                                pool.wait_ge(loaded[b], at(loaded[b], 16 * (i + 1)))
                                pool.sem_inc(chunks_begun, 1)
                                for t in range(CH):
                                    row_gather(pool, rows[b][:, t, :], table, idx[b][:, t:t + 1]).then_inc(gathered[b], 16)

                    @block.vector
                    def _(v):
                        nc.vector.memset(tail[:], 0.0).then_inc(s_v, 1)
                        with v.Fori(0, T // CH // 2) as i:
                            for b in range(2):
                                v.wait_ge(s_v, at(s_v, 1 + 4 * i + 2 * b))
                                v.wait_ge(gathered[b], 16 * CH * (i + 1))
                                scans(nc.vector, rows[b], same[:, bass.ds((2 * i + b) * CH, CH)], tail, D).then_inc(s_v, 1)
                                v.wait_ge(s_v, at(s_v, 2 + 4 * i + 2 * b))
                                nc.vector.tensor_copy(tail[:, 0:D], rows[b][:, CH - 1, :]).then_inc(s_v, 1)

                    @block.scalar
                    def _(act):
                        for b in range(2):
                            act.sem_inc(free[b], 1)
                        with act.Fori(0, T // CH // 2) as i:
                            for b in range(2):
                                act.wait_ge(s_v, at(s_v, 3 + 4 * i + 2 * b))
                                act.dma_start(z[:, bass.ds((2 * i + b) * CH, CH), :], rows[b][:]).then_inc(stored[b], 16)
                                act.wait_ge(stored[b], at(stored[b], 16 * (i + 1)))
                                act.sem_inc(free[b], 1)
            n = T // CH // 2
            close(s_v, 1 + 4 * n)
            for b in range(2):
                close(free[b], 1 + n)
                close(loaded[b], 16 * n)
                close(stored[b], 16 * n)

        def l0_table():
            R3 = 1.0 / math.sqrt(3.0)
            R6 = 1.0 / math.sqrt(6.0)
            with ExitStack() as st:
                wb = st.enter_context(nc.sbuf_tensor("wb_l0", [P, 4 * 112], F32))
                rows = st.enter_context(nc.sbuf_tensor("rows_l0", [P, NJ, 112], F32))
                pt = [st.enter_context(nc.psum_tensor(f"pt{b}", [P, 512], F32)) for b in range(2)]
                po = [st.enter_context(nc.psum_tensor(f"po{b}", [P, 512], F32)) for b in range(2)]
                xt = [st.enter_context(nc.sbuf_tensor(f"xt{b}", [P, P], F32)) for b in range(2)]
                with nc.Block() as block:
                    @block.sync
                    def _(sp):
                        sp.wait_ge(s_vdone, at(s_vdone, 1))
                        with nc.allow_non_contiguous_dma(reason="weights of a few hundred bytes"):
                            n = 0
                            for col, k in ((0, 0), (8, 2)):
                                sp.dma_start(wb[0:M, col:col + M], l0_w[k]).then_inc(s_in, 16)
                                n += 16
                            for col, k in ((16, 1), (40, 3), (64, 4), (88, 5)):
                                for c in range(3):
                                    sp.dma_start(wb[M + c:D:3, col + c:col + 24:3], l0_w[k]).then_inc(s_in, 16)
                                    n += 16
                        assert n == 14 * 16
                        sp.wait_ge(s_vdone, at(s_vdone, 2))
                        replicate(sp, wb, 112)
                        sp.wait_ge(s_vdone, at(s_vdone, 3))
                        sp.dma_start(table_l0.rearrange("(p j) f -> p j f", p=P), rows[:]).then_inc(s_write, 16)
                        sp.wait_ge(s_write, at(s_write, 64))

                    @block.vector
                    def _(v):
                        nc.vector.memset(wb[:], 0.0).then_inc(s_vdone, 1)
                        v.wait_ge(s_in, at(s_in, 14 * 16))
                        start = at(s_v, 0)
                        link, count = chain(v, s_v, start)
                        link(nc.vector.tensor_scalar(wb[0:D, 8:64], wb[0:D, 8:64], R3, None, ALU.mult))
                        nc.vector.tensor_scalar(wb[0:D, 64:88], wb[0:D, 64:88], R6, None, ALU.mult).then_inc(s_vdone, 1)
                        linear_out(v, rows, 112, po)
                        v.sem_inc(s_vdone, 1)
                        close(s_v, count[0])

                    @block.tensor
                    def _(pe):
                        pe.wait_ge(s_write, at(s_write, 48))
                        linear_pe(pe, [x_cur], [wb], 112, pt, xt, po)

                    @block.scalar
                    def _(act):
                        linear_act(act, 1, pt, xt)
            close(s_in, 14 * 16)
            close(s_vdone, 3)
            close(s_write, 64)
            linear_closed()

        def l0_pass(lo_f, hi_f, iota_b):
            CH = C_MSG
            SUBS = 4
            CS = CH // SUBS
            assert CS * SUBS == CH
            gathered = gather_signals("l0")
            A = 1.0 / math.sqrt(10.0)
            B = 1.0 / math.sqrt(30.0)
            with ExitStack() as st:
                def sb(name, shape, dt=F32):
                    return st.enter_context(nc.sbuf_tensor(name, shape, dt))
                idx = [sb(f"idx_l0{b}", [P, CH], I32) for b in range(2)]
                rows = [sb(f"g_l0{b}", [P, CH, 112]) for b in range(2)]
                msg = [sb(f"msg_l0{b}", [P, CH, D]) for b in range(2)]
                a3 = [sb(f"a3_{b}", [P, CH, 3]) for b in range(2)]
                a5 = [sb(f"a5_{b}", [P, CH, 5]) for b in range(2)]
                s0 = [sb(f"s0_{b}", [P, CH]) for b in range(2)]
                bm = sb("bm", [P, CH, 3, 3])
                tmp = sb("tmp", [P, CH, M, 3])
                squares = sb("squares", [P, CH, 3])
                length = sb("length", [P, CH])
                direction = [sb(f"direction{b}", [P, CH, 3]) for b in range(2)]
                lower = sb("lower", [P, P])
                zeros = sb("zeros", [P, CH * D])
                zero_b = sb("zero_b", [P, P], BF16)
                lo1 = [sb(f"lo1_{b}", [P, CS, P], BF16) for b in range(2)]
                hi1 = [sb(f"hi1_{b}", [P, CS, NJ], BF16) for b in range(2)]
                cnt = sb("cnt", [P, NJ])
                cum = sb("cum", [P, 4, NJ])
                w1_s = sb("w1_s", [10, 16])
                emb_s = [sb(f"emb_s{b}", [10, CS * P]) for b in range(2)]
                hid = [sb(f"hid{b}", [P, CH, 16]) for b in range(2)]
                p_cnt = st.enter_context(nc.psum_tensor("p_cnt", [P, 512], F32))
                p_cum = st.enter_context(nc.psum_tensor("p_cum", [P, 2, NJ], F32))
                p_h = [st.enter_context(nc.psum_tensor(f"p_h{b}", [P, 512], F32)) for b in range(2)]
                one_hot = signal("one_hot")
                counted = signal("counted")
                h_in = [signal(f"h_in{b}") for b in range(2)]
                h_made = signal("h_made")
                h_free = signal("h_free")
                h_out = [signal(f"h_out{b}") for b in range(2)]
                zero_out = signal("zero_out")
                w1_in = signal("w1_in")
                len_made = signal("len_made")
                len_root = signal("len_root")
                unit_out = [signal(f"unit_out{b}") for b in range(2)]
                z = scanned_rows.rearrange("(p t) f -> p t f", p=P)
                zero_dest = start_rows.rearrange("(p t) f -> p (t f)", p=P)
                LINKS = 31
                with nc.Block() as block:
                    @block.sync
                    def _(sp):
                        sp.dma_start(w1_s[:], w1).then_inc(w1_in, 16)
                        for b in range(2):
                            sp.sem_inc(stored[b], 16)
                            sp.sem_inc(unit_out[b], 16)
                        sp.wait_ge(s_pool, at(s_pool, 1))
                        with sp.Fori(0, T // CH // 2) as i:
                            for b in range(2):
                                c = 2 * i + b
                                ts = bass.ds(c * CH, CH)
                                sp.wait_ge(stored[b], at(stored[b], 16 * (i + 1)))
                                sp.wait_ge(unit_out[b], 16 * (i + 1))
                                sp.dma_start(idx[b][:], src_rows[:, ts]).then_inc(loaded[b], 16)
                                sp.dma_start(a3[b][:], attr3[:, ts, :]).then_inc(loaded[b], 16)
                                sp.dma_start(a5[b][:], attr5[:, ts, :]).then_inc(loaded[b], 16)
                                sp.dma_start(s0[b][:], edge_w1[:, ts]).then_inc(loaded[b], 16)
                                sp.dma_start(zero_dest[:, bass.ds(c * CH * D, CH * D)], zeros[:]).then_inc(zero_out, 16)
                                for u in range(SUBS):
                                    sp.wait_ge(h_made, c * SUBS + u + 1)
                                    sp.dma_start(emb_s[u % 2][:], emb_t[:, bass.ds((c * CH + u * CS) * P, CS * P)]).then_inc(h_in[u % 2], 16)
                        sp.wait_ge(zero_out, 16 * (T // CH))

                    @block.gpsimd
                    def _(pool):
                        nc.gpsimd.memset(zeros[:], 0.0).then_inc(s_pool, 1)
                        nc.gpsimd.memset(zero_b[:], 0.0)
                        nc.gpsimd.affine_select(out=lower[:], in_=ones[:], compare_op=ALU.is_ge, fill=0.0,
                                                base=0, pattern=[[1, P]], channel_multiplier=-1).then_inc(s_pool, 1)
                        with pool.Fori(0, T // CH // 2) as i:
                            for b in range(2):
                                pool.wait_ge(loaded[b], at(loaded[b], 64 * (i + 1)))
                                pool.sem_inc(chunks_begun, 1)
                                for t in range(CH):
                                    row_gather(pool, rows[b][:, t, :], table_l0, idx[b][:, t:t + 1]).then_inc(gathered[b], 16)

                    @block.vector
                    def _(v):
                        nc.vector.memset(tail[:], 0.0).then_inc(s_v, 1)
                        v.sem_inc(one_hot, 1)
                        with v.Fori(0, T // CH // 2) as i:
                            for b in range(2):
                                c = 2 * i + b
                                for u in range(SUBS):
                                    v.wait_ge(counted, 1 + c * SUBS + u)
                                    for buf, half, n in ((lo1[u % 2], lo_f, P), (hi1[u % 2], hi_f, NJ)):
                                        last = nc.vector.tensor_tensor(
                                            buf[:], iota_b[:, 0:n].rearrange("p (a n) -> p a n", a=1).to_broadcast([P, CS, n]),
                                            half[:, bass.ds(c * CH + u * CS, CS)].rearrange("p (t a) -> p t a", a=1).to_broadcast([P, CS, n]), ALU.is_equal)
                                    last.then_inc(one_hot, 1)
                                start = at(s_v, 1) + (2 * i + b) * LINKS
                                link, count = chain(v, s_v, start)
                                v.wait_ge(s_v, start)
                                v.wait_ge(loaded[b], at(loaded[b], 64 * (i + 1)))
                                V = nc.vector
                                g = rows[b]
                                a1, a3v, a4, a5v = (g[:, :, c:c + 24].rearrange("p t (o k) -> p t o k", k=3) for c in (16, 40, 64, 88))
                                o0 = msg[b][:, :, 0:M]
                                o1 = msg[b][:, :, M:D].rearrange("p t (o k) -> p t o k", k=3)
                                y = a5[b]
                                link(V.tensor_tensor(squares[:], a3[b][:], a3[b][:], ALU.mult))
                                V.tensor_reduce(length[:], squares[:], AX.X, ALU.add).then_inc(len_made, 1)
                                V.tensor_scalar(bm[:, :, 0, 2], y[:, :, 0], A, None, ALU.mult)
                                V.tensor_scalar(bm[:, :, 2, 0], y[:, :, 0], A, None, ALU.mult)
                                V.tensor_scalar(bm[:, :, 0, 1], y[:, :, 1], A, None, ALU.mult)
                                V.tensor_scalar(bm[:, :, 1, 0], y[:, :, 1], A, None, ALU.mult)
                                V.tensor_scalar(bm[:, :, 1, 2], y[:, :, 3], A, None, ALU.mult)
                                V.tensor_scalar(bm[:, :, 2, 1], y[:, :, 3], A, None, ALU.mult)
                                V.tensor_scalar(bm[:, :, 1, 1], y[:, :, 2], 2 * B, None, ALU.mult)
                                V.tensor_scalar(tmp[:, :, 0, 0], y[:, :, 4], -A, None, ALU.mult)
                                link(V.tensor_scalar(tmp[:, :, 1, 0], y[:, :, 4], A, None, ALU.mult))
                                V.scalar_tensor_tensor(bm[:, :, 0, 0], y[:, :, 2], -B, tmp[:, :, 0, 0], ALU.mult, ALU.add)
                                link(V.scalar_tensor_tensor(bm[:, :, 2, 2], y[:, :, 2], -B, tmp[:, :, 1, 0], ALU.mult, ALU.add))
                                v.wait_ge(len_root, c + 1)
                                link(V.reciprocal(length[:], length[:]))
                                V.tensor_tensor(direction[b][:], a3[b][:], length[:].rearrange("p (t a) -> p t a", a=1).to_broadcast([P, CH, 3]), ALU.mult)
                                v.wait_ge(gathered[b], 16 * CH * (i + 1))

                                s_e = s0[b][:].rearrange("p (t a) -> p t a", a=1)
                                v_k = a3[b][:].rearrange("p t (a k) -> p t a k", a=1).to_broadcast([P, CH, M, 3])
                                link(V.tensor_tensor(tmp[:], a3v, v_k, ALU.mult))
                                link(V.tensor_reduce(o0, tmp[:], AX.X, ALU.add))
                                t0 = tmp[:, :, 0:M, 0]
                                link(V.tensor_tensor(t0, g[:, :, 0:M], s_e.to_broadcast([P, CH, M]), ALU.mult))
                                link(V.tensor_tensor(o0, o0, t0, ALU.add))
                                link(V.tensor_tensor(msg[b][:, :, M:D], g[:, :, 16:40], s_e.to_broadcast([P, CH, 24]), ALU.mult))
                                link(V.tensor_tensor(tmp[:], g[:, :, 8:16].rearrange("p t (o a) -> p t o a", a=1).to_broadcast([P, CH, M, 3]), v_k, ALU.mult))
                                link(V.tensor_tensor(o1, o1, tmp[:], ALU.add))
                                for j in range(3):
                                    link(V.tensor_tensor(tmp[:], a5v[:, :, :, j:j + 1].to_broadcast([P, CH, M, 3]),
                                                         bm[:, :, j:j + 1, :].to_broadcast([P, CH, M, 3]), ALU.mult))
                                    link(V.tensor_tensor(o1, o1, tmp[:], ALU.add))
                                for k in range(3):
                                    p1, p2 = (k + 1) % 3, (k + 2) % 3
                                    for n, (iv, ja, op) in enumerate(((p1, p2, ALU.add), (p2, p1, ALU.subtract))):
                                        link(V.tensor_tensor(tmp[:, :, :, n], a4[:, :, :, ja],
                                                             a3[b][:, :, iv:iv + 1].to_broadcast([P, CH, M]), ALU.mult))
                                        link(V.tensor_tensor(o1[:, :, :, k], o1[:, :, :, k], tmp[:, :, :, n], op))
                                link(scans(V, msg[b], same[:, bass.ds((2 * i + b) * CH, CH)], tail, D))
                                ins = V.tensor_copy(tail[:, 0:D], msg[b][:, CH - 1, :])
                                count[0] += 1
                                ins.then_inc(s_v, 1)
                                links[0] = count[0]
                        assert links[0] == LINKS, links
                        link, count = chain(v, s_v, at(s_v, 1) + T // CH * LINKS)
                        v.wait_ge(s_pe, at(s_pe, 1))
                        link(nc.vector.tensor_copy(cnt[:], p_cnt[:, 0:NJ]))
                        link(nc.vector.tensor_scalar(nonempty[:], cnt[:], 1.0, None, ALU.min))
                        nc.vector.tensor_scalar(dinv[:], cnt[:], 1.0, None, ALU.max).then_inc(s_vdone, 1)
                        v.wait_ge(s_pe, at(s_pe, 2))
                        link(nc.vector.tensor_copy(cum[:, 0:2, :], p_cum[:]))
                        link(nc.vector.tensor_tensor_scan(cum[:, 2, :], ones[:, 0:NJ], cum[:, 1, :], 0.0, ALU.mult, ALU.add))
                        link(nc.vector.tensor_tensor(cum[:, 2, :], cum[:, 2, :], cum[:, 1, :], ALU.subtract))
                        link(nc.vector.tensor_tensor(cum[:, 2, :], cum[:, 2, :], cum[:, 0, :], ALU.add))
                        link(nc.vector.tensor_scalar(cum[:, 3, :], cum[:, 2, :], -1.0, 0.0, ALU.add, ALU.max))
                        link(nc.vector.tensor_copy(end_i[:], cum[:, 3, :]))
                        link(nc.vector.tensor_tensor(cum[:, 2, :], cum[:, 2, :], cnt[:], ALU.subtract))
                        link(nc.vector.tensor_scalar(cum[:, 3, :], nonempty[:], -float(EP), float(EP), ALU.mult, ALU.add))
                        link(nc.vector.tensor_tensor(cum[:, 2, :], cum[:, 2, :], cum[:, 3, :], ALU.add))
                        link(nc.vector.tensor_copy(start_i[:], cum[:, 2, :]))
                        v.wait_ge(s_act, at(s_act, 1))
                        link(nc.vector.reciprocal(dinv[:], dinv[:]))
                        final[0] = count[0]

                    @block.tensor
                    def _(pe):
                        pe.wait_ge(s_pool, at(s_pool, 2))
                        pe.wait_ge(w1_in, 16)
                        nc.tensor.matmul(p_cnt[:, 0:NJ], zero_b[:], zero_b[:, 0:NJ], start=True, stop=False).then_inc(counted, 2)
                        pe.sem_inc(h_made, 2)
                        with pe.Fori(0, T // CH // 2) as i:
                            for b in range(2):
                                c = 2 * i + b
                                for u in range(SUBS):
                                    pe.wait_ge(h_in[u % 2], 16 * (c * (SUBS // 2) + u // 2 + 1))
                                    pe.wait_ge(h_free, c * SUBS + u + 1)
                                    for t in range(CS):
                                        last = nc.tensor.matmul(p_h[u % 2][:, 16 * t:16 * t + 16],
                                                                emb_s[u % 2][:, t * P:(t + 1) * P], w1_s[:], start=True, stop=True)
                                    last.then_inc(h_made, 1)
                                for u in range(SUBS):
                                    pe.wait_ge(one_hot, 2 + c * SUBS + u)
                                    for t in range(CS):
                                        last = nc.tensor.matmul(p_cnt[:, 0:NJ], lo1[u % 2][:, t, :], hi1[u % 2][:, t, :], start=False, stop=False)
                                    last.then_inc(counted, 1)
                        nc.tensor.matmul(p_cnt[:, 0:NJ], zero_b[:], zero_b[:, 0:NJ], start=False, stop=True).then_inc(s_pe, 1)
                        pe.wait_ge(s_vdone, at(s_vdone, 1))
                        nc.tensor.matmul(p_cum[:, 0, :], lower[:], cnt[:], start=True, stop=True)
                        nc.tensor.matmul(p_cum[:, 1, :], ones[:], cnt[:], start=True, stop=True).then_inc(s_pe, 1)

                    @block.scalar
                    def _(act):
                        act.sem_inc(h_free, 2)
                        for b in range(2):
                            act.sem_inc(h_out[b], 16)
                        with act.Fori(0, T // CH // 2) as i:
                            for b in range(2):
                                c = 2 * i + b
                                act.wait_ge(h_out[b], 16 * (i + 1))
                                for u in range(SUBS):
                                    act.wait_ge(h_made, c * SUBS + u + 3)
                                    nc.scalar.activation(hid[b][:, u * CS:(u + 1) * CS, :],
                                                         p_h[u % 2][:, 0:16 * CS].rearrange("p (t k) -> p t k", k=16),
                                                         ACT.Relu).then_inc(h_free, 1)
                                act.wait_ge(h_free, (c + 1) * SUBS + 2)
                                act.dma_start(hidden[:, bass.ds(c * CH, CH), :], hid[b][:]).then_inc(h_out[b], 16)
                                act.wait_ge(len_made, c + 1)
                                nc.scalar.activation(length[:], length[:], ACT.Sqrt).then_inc(len_root, 1)
                                act.wait_ge(s_v, at(s_v, 1) + (c + 1) * LINKS)
                                act.dma_start(z[:, bass.ds(c * CH, CH), :], msg[b][:]).then_inc(stored[b], 16)
                                act.dma_start(unit[:, bass.ds(c * CH, CH), :], direction[b][:]).then_inc(unit_out[b], 16)
                        act.wait_ge(s_vdone, at(s_vdone, 1))
                        nc.scalar.activation(dinv[:], dinv[:], ACT.Sqrt).then_inc(s_act, 1)
                        for b in range(2):
                            act.wait_ge(stored[b], at(stored[b], 16 + 16 * (T // CH // 2)))
                            act.wait_ge(unit_out[b], 16 + 16 * (T // CH // 2))
                            act.wait_ge(h_out[b], 16 + 16 * (T // CH // 2))
            n = T // CH // 2
            close(s_v, 1 + 2 * n * LINKS + final[0])
            close(s_pool, 2)
            close(s_pe, 2)
            close(s_act, 1)
            close(s_vdone, 1)
            for b in range(2):
                close(loaded[b], 64 * n)
                close(stored[b], 16 + 16 * n)

        links = [0]
        final = [0]

        def residual_norm_stage(tag, last=False, scale_table=False):
            with ExitStack() as st:
                banks = [st.enter_context(nc.psum_tensor(f"pc_{tag}{b}", [P, 512], F32)) for b in range(2)]
                with nc.Block() as block:
                    @block.gpsimd
                    def _(pool):
                        fetch_sums(pool, agg[:, 0:NJ * D].rearrange("p (j f) -> p j f", f=D), scanned_rows)

                    @block.tensor
                    def _(pe):
                        crossing_matmuls(pe, banks, D)

                    @block.vector
                    def _(v):
                        link, count = chain(v, s_v, at(s_v, 0))
                        spread_tails(D)
                        for k in range(BLOCKS):
                            js = block_of(k)
                            a = block_sums(v, link, banks, D, k)
                            link(nc.vector.tensor_tensor(x_cur[:, js, :], x_cur[:, js, :], a, ALU.add))
                            layer_norm(v, link, js, at(s_act, k + 1))
                            if scale_table:
                                link(nc.vector.tensor_tensor(sq[:, js, :], x_cur[:, js, :], by_col(dinv[:, js]), ALU.mult))
                            v.sem_inc(s_vdone, 1)
                        close(s_v, count[0])

                    @block.scalar
                    def _(act):
                        for k in range(BLOCKS):
                            norm_root(act, block_of(k), at(s_vdone, 2 + 2 * k))

                    @block.sync
                    def _(sp):
                        write_blocks(sp, out if last else table.rearrange("(p j) f -> p j f", p=P),
                                     sq if scale_table else x_cur, 3, 2)
            sums_closed()
            close(s_vdone, 2 * BLOCKS)
            close(s_act, BLOCKS)
            close(s_write, 16 * BLOCKS)

        def scatter_start(pool, nodes, j):
            pool.indirect_dma_start(out=start_rows, out_offset=bass.IndirectOffsetOnAxis(ap=start_i[:, j:j + 1], axis=0),
                                    in_=nodes[:, j, :], in_offset=None, bounds_check=EP - 1,
                                    oob_is_err=False).then_inc(s_scatter, 16)

        def cheb_step_stage(tag, x0, x1):
            with ExitStack() as st:
                banks = [st.enter_context(nc.psum_tensor(f"pc_{tag}{b}", [P, 512], F32)) for b in range(2)]
                with nc.Block() as block:
                    @block.gpsimd
                    def _(pool):
                        fetch_sums(pool, agg[:, 0:NJ * D].rearrange("p (j f) -> p j f", f=D), scanned_rows)

                    @block.tensor
                    def _(pe):
                        crossing_matmuls(pe, banks, D)

                    @block.vector
                    def _(v):
                        V = nc.vector
                        link, count = chain(v, s_v, at(s_v, 0))
                        spread_tails(D)
                        for k in range(BLOCKS):
                            js = block_of(k)
                            a = block_sums(v, link, banks, D, k)
                            link(V.tensor_tensor(a, a, by_col(dinv[:, js]), ALU.mult))
                            link(V.tensor_scalar(a, a, lam_c[:, 0:1], None, ALU.mult))
                            link(V.scalar_tensor_tensor(x1[:, js, :], x0[:, js, :], lam_c[:, 1:2], a, ALU.mult, ALU.add))
                            link(V.tensor_tensor(sq[:, js, :], x1[:, js, :], by_col(dinv[:, js]), ALU.mult))
                            v.sem_inc(s_vdone, 1)
                        close(s_v, count[0])

                    @block.sync
                    def _(sp):
                        write_blocks(sp, table.rearrange("(p j) f -> p j f", p=P), sq, 2, 1)
            sums_closed()
            close(s_vdone, BLOCKS)
            close(s_write, 16 * BLOCKS)

        def cheb_mix_stage(tag, xs, dest, gat=None):
            x0, x1, x2 = xs
            done_by = [[g for g, (j0, nj) in enumerate(GROUPS) if (j0 + nj - 1) // JB == k] for k in range(BLOCKS)]
            with ExitStack() as st:
                def sb(name, shape, dt=F32):
                    return st.enter_context(nc.sbuf_tensor(f"{name}_{tag}", shape, dt))
                wc = [sb(f"wc{k}", [P, 4 * D]) for k in range(3)]
                bias = sb("bias", [P, D])
                wg = sb("wg", [P, 8 * D])
                gbias = sb("gbias", [P, 2 * D])
                both = sb("both", [P, NJ, 2 * D])
                pt = [st.enter_context(nc.psum_tensor(f"pt_{tag}{b}", [P, 512], F32)) for b in range(2)]
                po = [st.enter_context(nc.psum_tensor(f"po_{tag}{b}", [P, 512], F32)) for b in range(2)]
                xt = [sb(f"xt{b}", [P, 3 * P]) for b in range(2)]
                n_in = 4 + (4 if gat else 0)
                fd_out = signal(f"fd_out_{tag}")
                taken = signal(f"taken_{tag}")
                mixed = signal(f"mixed_{tag}")
                w_zero = signal(f"w_zero_{tag}")
                banks = [st.enter_context(nc.psum_tensor(f"pc_{tag}{b}", [P, 512], F32)) for b in range(2)]

                def row(a):
                    return a.rearrange("(a n) -> a n", a=1).to_broadcast([P, D])
                with nc.Block() as block:
                    @block.gpsimd
                    def _(pool):
                        fetch_sums(pool, agg[:, 0:NJ * D].rearrange("p (j f) -> p j f", f=D), scanned_rows)

                    @block.sync
                    def _(sp):
                        sp.wait_ge(w_zero, 1)
                        for k in range(3):
                            sp.dma_start(wc[k][0:D, 0:D], cheb_w[k * D:(k + 1) * D, :]).then_inc(s_in, 16)
                        sp.dma_start(bias[:], row(cheb_b)).then_inc(s_in, 16)
                        if gat:
                            sp.dma_start(wg[0:D, 0:D], gat_ws).then_inc(s_in, 16)
                            sp.dma_start(wg[0:D, D:2 * D], gat_wd).then_inc(s_in, 16)
                            sp.dma_start(gbias[:, 0:D], row(gat_bs)).then_inc(s_in, 16)
                            sp.dma_start(gbias[:, D:2 * D], row(gat_bd)).then_inc(s_in, 16)
                        sp.wait_ge(s_in, at(s_in, 16 * n_in))
                        for k in range(3):
                            replicate(sp, wc[k], D)
                        if gat:
                            replicate(sp, wg, 2 * D)
                        if not gat:
                            for k in range(BLOCKS):
                                sp.wait_ge(mixed, k + 1)
                                a, e = GROUPS[done_by[k][0]][0], sum(GROUPS[done_by[k][-1]])
                                sp.dma_start(table.rearrange("(p j) f -> p j f", p=P)[:, a:e, :], sq[:, a:e, :]).then_inc(s_write, 16)
                            sp.wait_ge(s_write, at(s_write, 16 * (9 + BLOCKS)))

                    @block.tensor
                    def _(pe):
                        def crossing(k):
                            nc.tensor.matmul(banks[k % 2][:, 0:JB * D], cross_lo[:], spread[:, k * JB * D:(k + 1) * JB * D],
                                             start=True, stop=True).then_inc(s_pe, 1)
                        pe.wait_ge(s_vdone, at(s_vdone, 1))
                        crossing(0)
                        crossing(1)
                        pe.wait_ge(s_write, at(s_write, 16 * (12 if gat else 9)))
                        for k in range(BLOCKS):
                            pe.wait_ge(s_vdone, at(s_vdone, 2 + k))
                            if k + 2 < BLOCKS:
                                crossing(k + 2)
                            for g in done_by[k]:
                                linear_group(pe, g, xs, wc, D, pt, xt, po, taken)

                    @block.scalar
                    def _(act):
                        linear_act(act, 3, pt, xt)

                    @block.vector
                    def _(v):
                        V = nc.vector
                        link, count = chain(v, s_v, at(s_v, 0))
                        for w in wc:
                            V.memset(w[:], 0.0)
                        V.memset(wg[:], 0.0).then_inc(w_zero, 1)
                        spread_tails(D)

                        def mix(k):
                            for g in done_by[k]:
                                j0, nj = GROUPS[g]
                                v.wait_ge(s_mm, at(s_mm, g + 1))
                                V.tensor_tensor(dest[:, j0:j0 + nj, :], po[g % 2][:, 0:nj * D].rearrange("p (j f) -> p j f", f=D),
                                                bias[:].rearrange("p (a f) -> p a f", a=1).to_broadcast([P, nj, D]),
                                                ALU.add).then_inc(taken, 1)
                            v.wait_ge(taken, done_by[k][-1] + 1)
                            js = slice(GROUPS[done_by[k][0]][0], sum(GROUPS[done_by[k][-1]]))
                            link(V.scalar_tensor_tensor(dest[:, js, :], dest[:, js, :], 0.01, dest[:, js, :], ALU.mult, ALU.max))
                            V.tensor_tensor(sq[:, js, :], dest[:, js, :], by_col(dinv[:, js]), ALU.mult).then_inc(mixed, 1)
                        for k in range(BLOCKS):
                            js = block_of(k)
                            a = block_sums(v, link, banks, D, k)
                            link(V.tensor_tensor(a, a, by_col(dinv[:, js]), ALU.mult))
                            link(V.tensor_scalar(a, a, lam_c[:, 2:3], None, ALU.mult))
                            link(V.scalar_tensor_tensor(x2[:, js, :], x1[:, js, :], lam_c[:, 3:4], a, ALU.mult, ALU.add))
                            link(V.tensor_tensor(x2[:, js, :], x2[:, js, :], x0[:, js, :], ALU.subtract))
                            v.sem_inc(s_vdone, 1)
                            if k == 0:
                                v.wait_ge(s_in, at(s_in, 16 * n_in))
                            else:
                                mix(k - 1)
                        mix(BLOCKS - 1)
                        close(s_v, count[0])
                sums_closed()
                close(s_in, 16 * n_in)
                close(s_write, 16 * (12 if gat else 9 + BLOCKS))
                close(s_vdone, BLOCKS)
                close(taken, len(GROUPS))
                for s in (s_tp, s_xt, s_mm):
                    close(s, len(GROUPS))
                if gat:
                    with nc.Block() as block:
                        @block.tensor
                        def _(pe):
                            linear_pe(pe, [dest], [wg], 2 * D, pt, xt, po)

                        @block.scalar
                        def _(act):
                            linear_act(act, 1, pt, xt)

                        @block.vector
                        def _(v):
                            linear_out(v, both, 2 * D, po, gbias)

                        @block.gpsimd
                        def _(pool):
                            for g, (j0, nj) in enumerate(GROUPS):
                                pool.wait_ge(s_ev, at(s_ev, g + 1))
                                for j in range(j0, j0 + nj):
                                    scatter_start(pool, both[:, :, D:2 * D], j)
                            pool.wait_ge(fd_out, 16)
                            row_gather(pool, fill[:], table_fd, first_row[:]).then_inc(s_agg, 16)
                            pool.wait_ge(s_scatter, at(s_scatter, 16 * NJ))
                            pool.wait_ge(s_agg, at(s_agg, 16))

                        @block.sync
                        def _(sp):
                            sp.wait_ge(s_ev, at(s_ev, len(GROUPS)))
                            sp.dma_start(table_fd.rearrange("(p j) f -> p j f", p=P), both[:, :, D:2 * D]).then_inc(fd_out, 16)
                            sp.dma_start(table.rearrange("(p j) f -> p j f", p=P), both[:, :, 0:D]).then_inc(s_write, 16)
                            sp.wait_ge(s_write, at(s_write, 16))
                    linear_closed()
                    close(s_agg, 16)
                    close(s_write, 16)
                    close(s_scatter, 16 * NJ)

        def gat_pass(m_last):
            CH = C_MSG
            gathered = gather_signals("gat")
            with ExitStack() as st:
                def sb(name, shape, dt=F32):
                    return st.enter_context(nc.sbuf_tensor(name, shape, dt))
                idx = [sb(f"idx_gat{b}", [P, CH], I32) for b in range(2)]
                rows = [sb(f"g_gat{b}", [P, CH, D]) for b in range(2)]
                fd = [sb(f"fd_gat{b}", [P, CH, D]) for b in range(2)]
                prod = [sb(f"prod_gat{b}", [P, CH, D + 2]) for b in range(2)]
                attn = sb("attn", [P, D])
                pen = sb("pen", [P, CH])
                logit = sb("logit", [P, CH])
                top_f = sb("top_f", [P, CH + 1])
                ex = sb("ex", [P, 2, CH])
                exp_in = signal("exp_in")
                exp_out = signal("exp_out")
                z = gat_rows.rearrange("(p t) f -> p t f", p=P)
                sr = start_rows.rearrange("(p t) f -> p t f", p=P)
                LINKS = 11
                with nc.Block() as block:
                    @block.sync
                    def _(sp):
                        sp.dma_start(attn[:], gat_attn.to_broadcast([P, D])).then_inc(s_in, 16)
                        with sp.Fori(0, T // CH // 2) as i:
                            for b in range(2):
                                ts = bass.ds((2 * i + b) * CH, CH)
                                sp.wait_ge(free[b], at(free[b], 1 + i))
                                sp.dma_start(idx[b][:], src_rows[:, ts]).then_inc(loaded[b], 16)
                                sp.dma_start(fd[b][:], sr[:, ts, :]).then_inc(loaded[b], 16)

                    @block.gpsimd
                    def _(pool):
                        with pool.Fori(0, T // CH // 2) as i:
                            for b in range(2):
                                pool.wait_ge(loaded[b], at(loaded[b], 32 * (i + 1)))
                                pool.sem_inc(chunks_begun, 1)
                                for t in range(CH):
                                    row_gather(pool, rows[b][:, t, :], table, idx[b][:, t:t + 1]).then_inc(gathered[b], 16)

                    @block.vector
                    def _(v):
                        V = nc.vector
                        v.wait_ge(s_in, at(s_in, 16))
                        V.memset(top_f[:, 0:1], -BIG)
                        V.memset(tail[:], 0.0).then_inc(s_v, 1)
                        with v.Fori(0, T // CH // 2) as i:
                            for b in range(2):
                                c = 2 * i + b
                                start = at(s_v, 1) + c * LINKS
                                link, count = chain(v, s_v, start)
                                v.wait_ge(s_v, start)
                                v.wait_ge(loaded[b], at(loaded[b], 32 * (i + 1)))
                                ts = bass.ds(c * CH, CH)
                                V.tensor_scalar(pen[:], same[:, ts], BIG, -BIG, ALU.mult, ALU.add)
                                link(scans(V, fd[b], same[:, ts], fill, D))
                                link(V.tensor_copy(fill[:], fd[b][:, CH - 1, :]))
                                v.wait_ge(gathered[b], 16 * CH * (i + 1))
                                link(V.tensor_tensor(fd[b][:], fd[b][:], rows[b][:], ALU.add))
                                link(V.scalar_tensor_tensor(fd[b][:], fd[b][:], 0.2, fd[b][:], ALU.mult, ALU.max))
                                link(V.tensor_tensor(fd[b][:], fd[b][:], attn[:].rearrange("p (a f) -> p a f", a=1).to_broadcast([P, CH, D]), ALU.mult))
                                link(V.tensor_reduce(logit[:], fd[b][:], AX.X, ALU.add))
                                link(V.tensor_tensor_scan(top_f[:, 1:CH + 1], pen[:], logit[:], top_f[:, 0:1], ALU.add, ALU.max))
                                V.tensor_tensor(ex[:, 1, :], logit[:], top_f[:, 1:CH + 1], ALU.subtract)
                                link(V.tensor_tensor(ex[:, 0, :], top_f[:, 0:CH], top_f[:, 1:CH + 1], ALU.subtract))
                                V.scalar_tensor_tensor(ex[:, 0, :], ex[:, 0, :], DEEP, same[:, ts], ALU.max, ALU.mult).then_inc(exp_in, 1)
                                V.tensor_copy(prod[b][:, :, D + 1:D + 2], top_f[:, 1:CH + 1].rearrange("p (t a) -> p t a", a=1))
                                V.tensor_copy(top_f[:, 0:1], top_f[:, CH:CH + 1])
                                v.wait_ge(exp_out, c + 1)
                                V.tensor_tensor(ex[:, 0, :], ex[:, 0, :], same[:, ts], ALU.mult)
                                w = ex[:, 1, :].rearrange("p (t a) -> p t a", a=1)
                                V.tensor_copy(prod[b][:, :, D:D + 1], w)
                                link(V.tensor_tensor(prod[b][:, :, 0:D], rows[b][:], w.to_broadcast([P, CH, D]), ALU.mult))
                                link(scans(V, prod[b], ex[:, 0, :], tail, D + 1))
                                V.tensor_copy(tail[:], prod[b][:, CH - 1, 0:D + 1]).then_inc(s_v, 1)
                                assert count[0] + 1 == LINKS, count
                        v.wait_ge(s_v, at(s_v, 1) + T // CH * LINKS)
                        V.tensor_copy(m_last[:], top_f[:, 0:1]).then_inc(s_v, 1)

                    @block.scalar
                    def _(act):
                        for b in range(2):
                            act.sem_inc(free[b], 1)
                        with act.Fori(0, T // CH // 2) as i:
                            for b in range(2):
                                c = 2 * i + b
                                act.wait_ge(exp_in, c + 1)
                                nc.scalar.activation(ex[:], ex[:], ACT.Exp).then_inc(exp_out, 1)
                                act.wait_ge(s_v, at(s_v, 1) + (c + 1) * LINKS)
                                act.dma_start(z[:, bass.ds(c * CH, CH), :], prod[b][:]).then_inc(stored[b], 16)
                                act.wait_ge(stored[b], at(stored[b], 16 * (i + 1)))
                                act.sem_inc(free[b], 1)
            n = T // CH // 2
            close(s_in, 16)
            close(s_v, 2 + 2 * n * LINKS)
            for b in range(2):
                close(free[b], 1 + n)
                close(loaded[b], 32 * n)
                close(stored[b], 16 * n)

        def gat_norm_stage(m_last):
            NE, NX = D + 2, D + 3
            with ExitStack() as st:
                def sb(name, shape, dt=F32):
                    return st.enter_context(nc.sbuf_tensor(name, shape, dt))
                ends = sb("ends", [P, NJ, NE])
                over = sb("over", [P, NJ, NX])
                cross = sb("cross", [P, NJ, NX])
                diag = sb("diag", [P, 2, P])
                cand = sb("cand", [P, P])
                mask = sb("mask", [P, P])
                tx = sb("tx", [P, NX])
                d_tail = sb("d_tail", [P, 1])
                u = sb("u", [P, 4, NJ])
                pr = st.enter_context(nc.psum_tensor("pr", [P, 2, P], F32))
                banks = [st.enter_context(nc.psum_tensor(f"pc_gat{b}", [P, 512], F32)) for b in range(2)]
                with nc.Block() as block:
                    @block.gpsimd
                    def _(pool):
                        fetch_sums(pool, ends, gat_rows)
                        for k in range(BLOCKS):
                            pool.wait_ge(s_vdone, at(s_vdone, 6 + 3 * k))
                            for j in range(k * JB, (k + 1) * JB):
                                scatter_start(pool, x_cur, j)
                        pool.wait_ge(s_scatter, at(s_scatter, 16 * NJ))

                    @block.tensor
                    def _(pe):
                        pe.wait_ge(s_vdone, at(s_vdone, 1))
                        nc.tensor.matmul(pr[:].rearrange("p a q -> p (a q)"), ones[:], diag[:].rearrange("p a q -> p (a q)"),
                                         start=True, stop=True).then_inc(s_pe, 1)
                        pe.wait_ge(s_vdone, at(s_vdone, 3))
                        for k in range(BLOCKS):
                            if k >= 2:
                                pe.wait_ge(s_ev, at(s_ev, k - 1))
                            nc.tensor.matmul(banks[k % 2][:, 0:JB * NX], cross_lo[:],
                                             over[:, k * JB:(k + 1) * JB, :].rearrange("p j f -> p (j f)"),
                                             start=True, stop=True).then_inc(s_pe, 1)

                    @block.vector
                    def _(v):
                        V = nc.vector
                        start = at(s_v, 0)
                        link, count = chain(v, s_v, start)
                        V.tensor_scalar(diag[:, 0, :], ident[:], last_f[:], None, ALU.mult)
                        V.tensor_scalar(diag[:, 1, :], ident[:], m_last[:], None, ALU.mult).then_inc(s_vdone, 1)
                        v.wait_ge(s_pe, at(s_pe, 1))
                        link(V.tensor_scalar(mask[:], pr[:, 0, :], last_f[:], None, ALU.is_equal))
                        link(V.tensor_tensor(cand[:], mask[:], pr[:, 1, :], ALU.mult))
                        link(V.tensor_scalar(mask[:], mask[:], BIG, -BIG, ALU.mult, ALU.add))
                        link(V.tensor_tensor(cand[:], cand[:], mask[:], ALU.add))
                        link(V.tensor_reduce(tx[:, D + 1:D + 2], cand[:], AX.X, ALU.max))
                        link(V.tensor_tensor(d_tail[:], m_last[:], tx[:, D + 1:D + 2], ALU.subtract))
                        V.tensor_scalar(d_tail[:], d_tail[:], DEEP, None, ALU.max).then_inc(s_vdone, 1)
                        link(V.memset(tx[:, D + 2:D + 3], 1.0))
                        v.wait_ge(s_act, at(s_act, 1))
                        link(V.tensor_scalar(tx[:, 0:D + 1], tail[:], d_tail[:], None, ALU.mult))
                        V.tensor_tensor(over[:], cross_hi[:].rearrange("p (j a) -> p j a", a=1).to_broadcast([P, NJ, NX]),
                                        tx[:].rearrange("p (a f) -> p a f", a=1).to_broadcast([P, NJ, NX]), ALU.mult).then_inc(s_vdone, 1)
                        for k in range(BLOCKS):
                            v.wait_ge(s_pe, at(s_pe, k + 2))
                            V.tensor_copy(cross[:, k * JB:(k + 1) * JB, :].rearrange("p j f -> p (j f)"),
                                          banks[k % 2][:, 0:JB * NX]).then_inc(s_ev, 1)
                        v.wait_ge(s_ev, at(s_ev, BLOCKS))
                        link(V.tensor_scalar(u[:, 0, :], cross[:, :, D + 2], 1.0, None, ALU.max))
                        link(V.reciprocal(u[:, 0, :], u[:, 0, :]))
                        link(V.tensor_tensor(u[:, 0, :], u[:, 0, :], cross[:, :, D + 1], ALU.mult))
                        link(V.tensor_scalar(u[:, 1, :], cross[:, :, D + 2], 1.0, None, ALU.min))
                        for k in range(BLOCKS):
                            js = block_of(k)
                            own, part, w = ends[:, js, 0:D + 1], cross[:, js, 0:D + 1], u[:, :, js]
                            v.wait_ge(fetched[k], at(fetched[k], 16 * JB))
                            link(V.tensor_tensor(w[:, 0, :], w[:, 0, :], ends[:, js, D + 1], ALU.subtract))
                            link(V.tensor_tensor(w[:, 0, :], w[:, 0, :], w[:, 1, :], ALU.mult))
                            V.tensor_scalar(w[:, 2, :], w[:, 0, :], 0.0, DEEP, ALU.min, ALU.max)
                            link(V.tensor_scalar(w[:, 3, :], w[:, 0, :], -1.0, 0.0, ALU.mult, ALU.min))
                            V.tensor_scalar(w[:, 3, :], w[:, 3, :], DEEP, None, ALU.max).then_inc(s_vdone, 1)
                            link(V.tensor_tensor(own, own, by_col(nonempty[:, js], D + 1), ALU.mult))
                            v.wait_ge(s_act, at(s_act, 2 + 2 * k))
                            V.tensor_tensor(part, part, by_col(w[:, 2, :], D + 1), ALU.mult)
                            link(V.tensor_tensor(own, own, by_col(w[:, 3, :], D + 1), ALU.mult))
                            link(V.tensor_tensor(own, own, part, ALU.add))
                            link(V.tensor_scalar(stat[:, js, 0], nonempty[:, js], -1.0, 1.0, ALU.mult, ALU.add))
                            link(V.tensor_tensor(stat[:, js, 0], stat[:, js, 0], ends[:, js, D], ALU.add))
                            link(V.reciprocal(stat[:, js, 1], stat[:, js, 0]))
                            link(V.tensor_tensor(sq[:, js, :], own[:, :, 0:D], stat[:, js, 1:2].to_broadcast([P, JB, D]), ALU.mult))
                            link(V.scalar_tensor_tensor(sq[:, js, :], sq[:, js, :], 0.01, sq[:, js, :], ALU.mult, ALU.max))
                            link(V.tensor_tensor(x_cur[:, js, :], x_cur[:, js, :], sq[:, js, :], ALU.add))
                            layer_norm(v, link, js, at(s_act, 3 + 2 * k))
                            v.sem_inc(s_vdone, 1)
                        close(s_v, count[0])

                    @block.scalar
                    def _(act):
                        act.wait_ge(s_vdone, at(s_vdone, 2))
                        nc.scalar.activation(d_tail[:], d_tail[:], ACT.Exp).then_inc(s_act, 1)
                        for k in range(BLOCKS):
                            act.wait_ge(s_vdone, at(s_vdone, 4 + 3 * k))
                            nc.scalar.activation(u[:, 2:4, block_of(k)], u[:, 2:4, block_of(k)], ACT.Exp).then_inc(s_act, 1)
                            norm_root(act, block_of(k), at(s_vdone, 5 + 3 * k))

                    @block.sync
                    def _(sp):
                        write_blocks(sp, table.rearrange("(p j) f -> p j f", p=P), x_cur, 6, 3)
            for k in range(BLOCKS):
                close(fetched[k], 16 * JB)
            close(s_pe, 1 + BLOCKS)
            close(s_ev, BLOCKS)
            close(s_vdone, 3 + 3 * BLOCKS)
            close(s_act, 1 + 2 * BLOCKS)
            close(s_write, 16 * BLOCKS)
            close(s_scatter, 16 * NJ)

        def l2_pass():
            CH = C_MSG
            Q = CH // 4
            NG, KM = 6, 16 * M
            NT = NG * KM
            NS, NV = P, 112
            LOW = 2.0 ** 11
            GAIN = 1.593
            PW_S, PW_V = 0.17677669529663687, 0.25
            KAP = math.sqrt(2.0) / math.sqrt(10.0) / 4.0
            n = T // CH // 2
            F16 = mybir.dt.float16
            gathered = gather_signals("l2")
            with ExitStack() as st:
                def sb(name, shape, dt=F32):
                    return st.enter_context(nc.sbuf_tensor(name, shape, dt))

                def ps(name, shape, dt=F32):
                    return st.enter_context(nc.psum_tensor(name, shape, dt))
                idx = [sb(f"idx_l2{b}", [P, CH], I32) for b in range(2)]
                z = [sb(f"z_l2{b}", [P, CH, 80]) for b in range(2)]
                zs = [sb(f"zs{b}", [P, CH, NS], F16) for b in range(2)]
                zv = [sb(f"zv{b}", [P, CH, NV], F16) for b in range(2)]
                hid = [sb(f"h_l2{b}", [P, CH, 16]) for b in range(2)]
                vec = [sb(f"vec{b}", [P, CH, 3]) for b in range(2)]
                ew = [sb(f"ew{b}", [P, CH]) for b in range(2)]
                msg = sb("msg_l2", [P, CH, D])
                prod = [sb(f"prod{b}", [P, NG, 4, 16, M]) for b in range(2)]
                zst = [sb(f"zst{b}", [NS, 4 * P], F16) for b in range(2)]
                zvt = [sb(f"zvt{b}", [NV, 4 * P], F16) for b in range(2)]
                ws = [sb(f"ws{k}", [NS, 3 * KM], BF16) for k in range(2)]
                wv = [sb(f"wv{k}", [NV, 3 * KM], BF16) for k in range(3)]
                ident_h = sb("ident_h", [P, P], F16)
                pv = spread[:, 0:CH * 48].rearrange("p (t m i) -> p t m i", m=2 * M, i=3)
                res_s = sq[:].rearrange("p j f -> p (j f)")[:, 0:Q * 96].rearrange("p (q g t w) -> p q g t w", g=3, t=4, w=M)
                th = sq[:].rearrange("p j f -> p (j f)")[:, Q * 96:Q * 160].rearrange("p (q g t w) -> p q g t w", g=2, t=4, w=M)
                res_v = [agg[:, k * Q * 96:(k + 1) * Q * 96].rearrange("p (q g t w) -> p q g t w", g=3, t=4, w=M) for k in range(2)]
                p_z = ps("p_z", [P, 2, 512], F16)
                p_t = [ps(f"p_t{b}", [P, 3 * 512]) for b in range(2)]
                p_r = ps("p_r", [P, 96])
                loaded2 = [signal(f"loaded2{b}") for b in range(2)]
                s_prep = signal("s_prep")
                p_done = signal("p_done")
                h_split = signal("h_split")
                d_done = signal("d_done")
                z_split = signal("z_split")
                transposed = signal("transposed")
                zt_ready = signal("zt_ready")
                t_made = signal("t_made")
                t_used = signal("t_used")
                red_made = signal("red_made")
                red_out = signal("red_out")
                res_done = signal("res_done")
                th_done = signal("th_done")
                zr = scanned_rows.rearrange("(p t) f -> p t f", p=P)
                sr = start_rows.rearrange("(p t) f -> p t f", p=P)
                w2v = w2.rearrange("k (i u w) -> i u k w", i=7, u=16)

                room = [0]

                def wsb(rows, cols):
                    room[0] += cols
                    return prod[0][0:rows].rearrange("p g t k w -> p (g t k w)")[:, room[0] - cols:room[0]]
                f_s = wsb(NS, 3 * KM)
                f_p = wsb(NS, KM)
                f_v = wsb(NV, 3 * KM)
                f_e = wsb(NV, 3 * KM)
                r_s = wsb(NS, 3 * KM)
                r_v = wsb(NV, 3 * KM)
                b_s = sb("b_s", [NS, 3 * KM], BF16)
                with nc.Block() as block:
                    plan = []
                    for r in (0, 32, 64, 96):
                        plan += [(f_s, r, 1, g, i) for g, i in ((0, 0), (1, 2), (2, 4))]
                        plan += [(f_s, r + 16, 1, g, i) for g, i in ((0, 1), (1, 3))]
                        plan += [(f_p, r + 16, 1, 0, 6)]
                    for r in (0, 64):
                        for c in range(3):
                            plan += [(f_v, r + c, 3, c, 5), (f_e, r + c, 3, c, 6)]

                    @block.sync
                    def _(sp):
                        sp.wait_ge(s_vdone, at(s_vdone, 1))
                        with nc.allow_non_contiguous_dma(reason="weights, in runs of 8"):
                            for t, r, step, g, i in plan:
                                sp.dma_start(t[r:r + 15 * step + 1:step, g * KM:(g + 1) * KM].rearrange("u (k w) -> u k w", w=M),
                                             w2v[i]).then_inc(s_in, 16)

                    @block.gpsimd
                    def _(pool):
                        row_gather(pool, fill[:], table, first_row[:]).then_inc(s_agg, 16)
                        pool.wait_ge(s_agg, at(s_agg, 16))

                    @block.vector
                    def _(v):
                        V = nc.vector
                        for t in (f_s, f_p, f_v):
                            V.memset(t[:], 0.0)
                        for t in zv:
                            V.memset(t[:], 0.0)
                        V.memset(f_e[:], 0.0).then_inc(s_vdone, 1)
                        start = at(s_v, 0)
                        link, count = chain(v, s_v, start)
                        link(V.tensor_copy(ident_h[:], ident[:]))
                        v.wait_ge(s_in, at(s_in, 16 * len(plan)))
                        link(V.tensor_scalar(f_s[:, 0:2 * KM], f_s[:, 0:2 * KM], KAP * PW_S, None, ALU.mult))
                        link(V.tensor_scalar(f_s[:, 2 * KM:], f_s[:, 2 * KM:], KAP * PW_V, None, ALU.mult))
                        link(V.scalar_tensor_tensor(f_s[:, 2 * KM:], f_p[:], KAP * PW_V * math.sqrt(1.5), f_s[:, 2 * KM:], ALU.mult, ALU.add))
                        link(V.tensor_scalar(f_v[:], f_v[:], KAP * PW_V / math.sqrt(3.0), None, ALU.mult))
                        link(V.scalar_tensor_tensor(f_v[:], f_e[:], -KAP * PW_V * math.sqrt(1.5) / 3.0, f_v[:], ALU.mult, ALU.add))
                        link(V.tensor_scalar(f_s[32:64, :], f_s[32:64, :], 1.0 / LOW, None, ALU.mult))
                        link(V.tensor_scalar(f_s[96:128, :], f_s[96:128, :], 1.0 / LOW, None, ALU.mult))
                        link(V.tensor_scalar(f_v[64:NV, :], f_v[64:NV, :], 1.0 / LOW, None, ALU.mult))
                        link(V.tensor_copy(ws[0][:], f_s[:]))
                        link(V.tensor_tensor(r_s[:], f_s[:], ws[0][:], ALU.subtract))
                        link(V.tensor_copy(b_s[:], r_s[:]))
                        link(V.tensor_tensor(r_s[:], r_s[:], b_s[:], ALU.subtract))
                        link(V.tensor_copy(ws[0][64:128, :], b_s[64:128, :]))
                        link(V.tensor_copy(ws[1][:], r_s[:]))
                        link(V.tensor_copy(wv[0][:], f_v[:]))
                        link(V.tensor_tensor(r_v[:], f_v[:], wv[0][:], ALU.subtract))
                        link(V.tensor_copy(wv[1][:], r_v[:]))
                        link(V.tensor_tensor(r_v[:], r_v[:], wv[1][:], ALU.subtract))
                        link(V.tensor_copy(wv[2][:], r_v[:]))
                        close(s_v, count[0])
                close(s_in, 16 * len(plan))
                close(s_vdone, 1)
                close(s_agg, 16)

                PREP = 3
                MADE, TAIL = 4, 6
                F_AT, P_AT, D_AT = 4, 7, 11
                THIRDS = ((0, 11), (11, 22), (22, D))

                with nc.Block() as block:
                    @block.sync
                    def _(sp):
                        def load_rows(c, b):
                            ts = bass.ds(c * CH, CH)
                            sp.dma_start(idx[b][:], src_rows[:, ts]).then_inc(loaded[b], 16)
                            sp.dma_start(z[b][:, :, D:2 * D], sr[:, ts, :]).then_inc(loaded[b], 16)

                        def load_rest(c, b):
                            ts = bass.ds(c * CH, CH)
                            sp.dma_start(hid[b][:], hidden[:, ts, :]).then_inc(loaded2[b], 16)
                            sp.dma_start(vec[b][:], unit[:, ts, :]).then_inc(loaded2[b], 16)
                            sp.dma_start(ew[b][:], edge_w[:, ts]).then_inc(loaded2[b], 16)

                        def store(c, b, times):
                            sp.wait_ge(s_v, at(s_v, 1) + (c + 1) * TAIL)
                            sp.dma_start(zr[:, bass.ds(c * CH, CH), :], msg[:]).then_inc(stored[b], 16)
                            sp.wait_ge(stored[b], at(stored[b], 16) + 16 * times)
                        for b in range(2):
                            load_rows(b, b)
                            load_rest(b, b)
                        with sp.Fori(1, n) as i:
                            for b in range(2):
                                c = 2 * i + b
                                sp.wait_ge(z_split, c - 1)
                                load_rows(c, b)
                                store(c - 2, b, i - 1)
                                load_rest(c, b)
                        for b in range(2):
                            store(2 * n - 2 + b, b, n - 1)

                    @block.gpsimd
                    def _(pool):
                        with pool.Fori(0, n) as i:
                            for b in range(2):
                                pool.wait_ge(loaded[b], at(loaded[b], 32 * (i + 1)))
                                pool.sem_inc(chunks_begun, 1)
                                for t in range(CH):
                                    row_gather(pool, z[b][:, t, 0:D], table, idx[b][:, t:t + 1]).then_inc(gathered[b], 16)

                    @block.tensor
                    def _(pe):
                        def cut(a, e):
                            while a < e:
                                m = min(e, (a // 512 + 1) * 512)
                                yield a, m
                                a = m

                        pe.sem_inc(red_made, 2)
                        with pe.Fori(0, n) as i:
                            for b in range(2):
                                c = 2 * i + b

                                def transposes(q):
                                    pe.wait_ge(zt_ready, c * Q + q + 1)
                                    for t in range(4):
                                        nc.tensor.transpose(p_z[:, 0, t * P:(t + 1) * P], zs[b][:, 4 * q + t, :], ident_h[:])
                                        last = nc.tensor.transpose(p_z[0:NV, 1, t * P:(t + 1) * P], zv[b][:, 4 * q + t, :], ident_h[:])
                                    last.then_inc(transposed, 1)

                                def products(q):
                                    pe.wait_ge(zt_ready, c * Q + q + 2)
                                    for pair in range(2):
                                        pe.wait_ge(t_used, 2 * (c * Q + q) + pair + 1)
                                        for t in range(2):
                                            col = slice((2 * pair + t) * P, (2 * pair + t + 1) * P)
                                            last = None
                                            for lhs, parts, base in (
                                                    (zst[q % 2], ((ws[0], NS), (ws[1], 64)), 0),
                                                    (zvt[q % 2], tuple((w, NV) for w in wv), 3 * KM)):
                                                off = t * NT + base
                                                for k, (w, rows) in enumerate(parts):
                                                    for a, e in cut(off, off + 3 * KM):
                                                        last = nc.tensor.matmul(p_t[pair][:, a:e], lhs[0:rows, col], w[0:rows, a - off:e - off],
                                                                                start=(k == 0), stop=(k == len(parts) - 1))
                                        last.then_inc(t_made, 1)

                                def sums(q):
                                    pe.wait_ge(t_used, 2 * (c * Q + q) + 4)
                                    pe.wait_ge(red_out, c * Q + q + 1)
                                    for k in range(16):
                                        last = nc.tensor.matmul(p_r[:], ident[:],
                                                                prod[q % 2][:, 3:6, :, k, :].rearrange("p g t w -> p (g t) w"),
                                                                start=(k == 0), stop=(k == 15))
                                    last.then_inc(red_made, 1)

                                pe.wait_ge(z_split, c + 1)
                                transposes(0)
                                for q in range(Q):
                                    pe.wait_ge(zt_ready, c * Q + q + 2)
                                    if q + 1 < Q:
                                        transposes(q + 1)
                                    products(q)
                                    if q >= 1:
                                        sums(q - 1)
                                sums(Q - 1)

                    @block.scalar
                    def _(act):
                        A = nc.scalar

                        def high(c, b):
                            act.wait_ge(p_done, c + 1)
                            sc = z[b][:, :, 0:2 * D].rearrange("p t (e f) -> p t e f", e=2)
                            for r in (0, 64):
                                A.activation(zs[b][:, :, r:r + 16].rearrange("p t (e f) -> p t e f", e=2), sc[:, :, :, 0:M], ACT.Copy)
                                A.activation(zs[b][:, :, r + 16:r + 32], z[b][:, :, 2 * D:80], ACT.Copy)
                            A.activation(zv[b][:, :, 0:48].rearrange("p t (e f) -> p t e f", e=2), sc[:, :, :, M:D], ACT.Copy).then_inc(h_split, 1)

                        def low(c, b):
                            act.wait_ge(d_done, c + 1)
                            sc = z[b][:, :, 0:2 * D].rearrange("p t (e f) -> p t e f", e=2)
                            for r in (32, 96):
                                A.activation(zs[b][:, :, r:r + 16].rearrange("p t (e f) -> p t e f", e=2), sc[:, :, :, 0:M], ACT.Copy, scale=LOW)
                                A.activation(zs[b][:, :, r + 16:r + 32], z[b][:, :, 2 * D:80], ACT.Copy, scale=LOW)
                            A.activation(zv[b][:, :, 64:NV].rearrange("p t (e f) -> p t e f", e=2), sc[:, :, :, M:D], ACT.Copy, scale=LOW).then_inc(z_split, 1)

                        def turned(c, q):
                            act.wait_ge(transposed, c * Q + q + 1)
                            if q >= 2:
                                act.wait_ge(t_made, 2 * (c * Q + q - 1))
                            A.activation(zst[q % 2][:], p_z[:, 0, :], ACT.Copy)
                            A.activation(zvt[q % 2][:], p_z[0:NV, 1, :], ACT.Copy).then_inc(zt_ready, 1)

                        def summed(c, b, q):
                            act.wait_ge(red_made, c * Q + q + 3)
                            A.activation(res_v[b][:, q].rearrange("p g t w -> p (g t w)"), p_r[:], ACT.Copy).then_inc(red_out, 1)

                        def one_chunk(c, b, more):
                            turned(c, 0)
                            for q in range(Q):
                                if q + 1 < Q:
                                    turned(c, q + 1)
                                if q >= 1:
                                    summed(c, b, q - 1)
                                if more and q == P_AT + 3:
                                    high(c + 1, 1 - b)
                                if more and q == D_AT + 2:
                                    low(c + 1, 1 - b)
                            summed(c, b, Q - 1)
                            act.wait_ge(res_done, c + 1)
                            A.activation(th.rearrange("p q g t w -> p q (g t w)"),
                                         res_s[:, :, 0:2].rearrange("p q g t w -> p q (g t w)"), ACT.Tanh).then_inc(th_done, 1)

                        act.sem_inc(zt_ready, 1)
                        act.sem_inc(red_out, 1)
                        high(0, 0)
                        low(0, 0)
                        with act.Fori(0, n - 1) as i:
                            for b in range(2):
                                one_chunk(2 * i + b, b, True)
                        one_chunk(2 * n - 2, 0, True)
                        one_chunk(2 * n - 1, 1, False)

                    @block.vector
                    def _(v):
                        V = nc.vector

                        def unit_of(b, m):
                            return vec[b][:].rearrange("p t (a i) -> p t a i", a=1).to_broadcast([P, CH, m, 3])

                        def fill_forward(c, b, times, part):
                            v.wait_ge(loaded[b], at(loaded[b], 32) + 32 * times)
                            v.wait_ge(s_prep, c * PREP)
                            for f in range(*THIRDS[part]):
                                last = V.tensor_tensor_scan(z[b][:, :, D + f], same[:, bass.ds(c * CH, CH)], z[b][:, :, D + f],
                                                            fill[:, f:f + 1], ALU.mult, ALU.add)
                            if part == 2:
                                last.then_inc(s_prep, 1)

                        def p_of_src(c, b, times):
                            v.wait_ge(s_prep, c * PREP + 1)
                            V.tensor_copy(fill[:], z[b][:, CH - 1, D:2 * D]).then_inc(s_prep, 1)
                            v.wait_ge(loaded2[b], 48 + 48 * times)
                            v.wait_ge(gathered[b], 16 * CH + 16 * CH * times)
                            v.wait_ge(p_done, c)
                            V.tensor_tensor(pv[:, :, 0:M, :], z[b][:, :, M:D].rearrange("p t (m i) -> p t m i", i=3), unit_of(b, M), ALU.mult)

                        def p_of_dst(c, b):
                            V.tensor_tensor(pv[:, :, M:2 * M, :], z[b][:, :, D + M:2 * D].rearrange("p t (m i) -> p t m i", i=3), unit_of(b, M), ALU.mult).then_inc(s_prep, 1)

                        def sum_p(c, b):
                            v.wait_ge(s_prep, c * PREP + 3)
                            V.tensor_reduce(z[b][:, :, 2 * D:80], pv, AX.X, ALU.add).then_inc(p_done, 1)

                        def leave_scalars(c, b):
                            v.wait_ge(h_split, c + 1)
                            sc = z[b][:, :, 0:2 * D].rearrange("p t (e f) -> p t e f", e=2)
                            V.tensor_tensor(sc[:, :, :, 0:M], sc[:, :, :, 0:M], zs[b][:, :, 0:16].rearrange("p t (e f) -> p t e f", e=2), ALU.subtract)
                            V.tensor_tensor(z[b][:, :, 2 * D:80], z[b][:, :, 2 * D:80], zs[b][:, :, 16:32], ALU.subtract)

                        def leave_vectors(c, b):
                            sc = z[b][:, :, 0:2 * D].rearrange("p t (e f) -> p t e f", e=2)
                            V.tensor_tensor(sc[:, :, :, M:D], sc[:, :, :, M:D], zv[b][:, :, 0:48].rearrange("p t (e f) -> p t e f", e=2), ALU.subtract).then_inc(d_done, 1)

                        def quadruple(c, b, q):
                            v.wait_ge(red_made, c * Q + q + 1)
                            for pair in range(2):
                                v.wait_ge(t_made, 2 * (c * Q + q) + pair + 1)
                                for t in range(2):
                                    h = hid[b][:, 4 * q + 2 * pair + t, :].rearrange("p (a k e) -> p a k e", a=1, e=1).to_broadcast([P, NG, 16, M])
                                    ins = V.tensor_tensor(prod[q % 2][:, :, 2 * pair + t],
                                                          p_t[pair][:, t * NT:(t + 1) * NT].rearrange("p (g k w) -> p g k w", g=NG, k=16), h, ALU.mult)
                                ins.then_inc(t_used, 1)
                            v.wait_ge(t_used, 2 * (c * Q + q) + 4)
                            return V.tensor_reduce(res_s[:, q].rearrange("p g t w -> p (g t) w"),
                                                   prod[q % 2][:, 0:3].rearrange("p g t k w -> p (g t) w k"), AX.X, ALU.add)

                        def messages(c, b, more):
                            link, count = chain(v, s_v, at(s_v, 1) + c * TAIL)
                            if not more:
                                v.wait_ge(stored[1 - b], at(stored[1 - b], 16 * n))
                            v.wait_ge(res_done, c + 1)
                            m4 = msg[:].rearrange("p (q t) f -> p q t f", t=4)
                            n4 = vec[b][:].rearrange("p (q t) k -> p q t k", t=4)
                            e4 = ew[b][:].rearrange("p (q t a) -> p q t a", t=4, a=1).to_broadcast([P, Q, 4, M])

                            def o(k):
                                return m4[:, :, :, M + k:D:3]
                            for k in range(3):
                                ins = V.tensor_tensor(o(k), res_s[:, :, 2], n4[:, :, :, k:k + 1].to_broadcast([P, Q, 4, M]), ALU.mult)
                            link(ins)
                            v.wait_ge(th_done, c + 1)
                            V.scalar_tensor_tensor(m4[:, :, :, 0:M], th[:, :, 0], GAIN, e4, ALU.mult, ALU.mult)
                            link(V.scalar_tensor_tensor(th[:, :, 1], th[:, :, 1], GAIN, e4, ALU.mult, ALU.mult))
                            v.wait_ge(red_out, c * Q + Q + 1)
                            for k in range(3):
                                ins = V.tensor_tensor(o(k), o(k), res_v[b][:, :, k], ALU.add)
                            link(ins)
                            for k in range(3):
                                ins = V.tensor_tensor(o(k), o(k), th[:, :, 1], ALU.mult)
                            link(ins)
                            assert count[0] == MADE

                        def message_sums(c, part):
                            for f in range(part * M, (part + 1) * M):
                                last = V.tensor_tensor_scan(msg[:, :, f], same[:, bass.ds(c * CH, CH)], msg[:, :, f],
                                                            tail[:, f:f + 1], ALU.mult, ALU.add)
                            if part == 3:
                                link, count = chain(v, s_v, at(s_v, 1) + c * TAIL + MADE)
                                link(last)
                                link(V.tensor_copy(tail[:, 0:D], msg[:, CH - 1, :]))
                                assert count[0] == TAIL - MADE

                        def one_chunk(c, b, times, before=True, more=True):
                            for q in range(Q):
                                last = quadruple(c, b, q)
                                if q == Q - 1:
                                    last.then_inc(res_done, 1)
                                if before and q < 4:
                                    message_sums(c - 1, q)
                                if more and F_AT <= q < F_AT + 3:
                                    fill_forward(c + 1, 1 - b, times, q - F_AT)
                                if more and q == P_AT:
                                    p_of_src(c + 1, 1 - b, times)
                                if more and q == P_AT + 1:
                                    p_of_dst(c + 1, 1 - b)
                                if more and q == P_AT + 2:
                                    sum_p(c + 1, 1 - b)
                                if more and q == D_AT:
                                    leave_scalars(c + 1, 1 - b)
                                if more and q == D_AT + 1:
                                    leave_vectors(c + 1, 1 - b)
                            messages(c, b, more)

                        V.memset(tail[:], 0.0).then_inc(s_v, 1)
                        v.wait_ge(s_v, at(s_v, 1))
                        v.sem_inc(t_used, 2)
                        v.wait_ge(loaded[0], at(loaded[0], 32))
                        scans(V, z[0][:, :, D:2 * D], same[:, 0:CH], fill, D).then_inc(s_prep, 1)
                        v.wait_ge(s_prep, 1)
                        V.tensor_copy(fill[:], z[0][:, CH - 1, D:2 * D]).then_inc(s_prep, 1)
                        v.wait_ge(loaded2[0], 48)
                        v.wait_ge(gathered[0], 16 * CH)
                        V.tensor_tensor(pv[:, :, 0:M, :], z[0][:, :, M:D].rearrange("p t (m i) -> p t m i", i=3), unit_of(0, M), ALU.mult)
                        p_of_dst(0, 0)
                        sum_p(0, 0)
                        leave_scalars(0, 0)
                        leave_vectors(0, 0)
                        one_chunk(0, 0, 0, before=False)
                        with v.Fori(0, n - 1) as i:
                            one_chunk(2 * i + 1, 1, i + 1)
                            one_chunk(2 * i + 2, 0, i + 1)
                        one_chunk(2 * n - 1, 1, n, more=False)
                        for part in range(4):
                            message_sums(2 * n - 1, part)
            close(s_v, 1 + 2 * n * TAIL)
            for b in range(2):
                close(loaded[b], 32 * n)
                close(stored[b], 16 * n)

        with ExitStack() as st:
            lo_f = st.enter_context(nc.sbuf_tensor("lo_f", [P, T], BF16))
            hi_f = st.enter_context(nc.sbuf_tensor("hi_f", [P, T], BF16))
            iota_b = st.enter_context(nc.sbuf_tensor("iota_b", [P, P], BF16))
            prepare(lo_f, hi_f, iota_b)
            l0_table()
            l0_pass(lo_f, hi_f, iota_b)
        residual_norm_stage("l0", scale_table=True)
        with ExitStack() as st:
            x1 = st.enter_context(nc.sbuf_tensor("cheb_x1", [P, NJ, D], F32))
            x2 = st.enter_context(nc.sbuf_tensor("cheb_x2", [P, NJ, D], F32))
            h = st.enter_context(nc.sbuf_tensor("cheb_h", [P, NJ, D], F32))
            for r, x0 in enumerate((x_cur, h)):
                sum_pass(f"cheb{r}a")
                cheb_step_stage(f"cs{r}a", x0, x1)
                sum_pass(f"cheb{r}b")
                cheb_mix_stage(f"mix{r}", [x0, x1, x2], h, gat=(r == 1))
        with ExitStack() as st:
            m_last = st.enter_context(nc.sbuf_tensor("m_last", [P, 1], F32))
            gat_pass(m_last)
            gat_norm_stage(m_last)
        l2_pass()
        residual_norm_stage("l2")
        sum_pass("l3")
        residual_norm_stage("l3", last=True)


def kernel(**inputs):
    import numpy as np
    import concourse.bacc as bacc
    from concourse.bass_utils import run_bass_kernel_spmd as run

    a = {k: np.asarray(v) for k, v in inputs.items()}
    n_nodes, n_edges = a["x"].shape[0], a["src"].shape[0]
    NJ, T = shapes(n_nodes, n_edges)

    def by_edge(v, pad):
        full = np.full((P * T,) + v.shape[1:], pad, v.dtype)
        full[:n_edges] = v
        return full.reshape((P, T) + v.shape[1:])

    x = np.zeros((NJ * P, D), a["x"].dtype)
    x[:n_nodes] = a["x"]
    emb = by_edge(a["edge_attr_10"], 0)
    arrays = {
        "x": np.ascontiguousarray(x.reshape(NJ, P, D).transpose(1, 0, 2)),
        "src": by_edge(a["src"], 0),
        "dst": by_edge(a["dst"], n_nodes),
        "emb_t": np.ascontiguousarray(emb.transpose(2, 1, 0)).reshape(10, T * P),
        "attr3": by_edge(a["edge_attr_3"], 1),
        "attr5": by_edge(a["edge_attr_5"], 0),
        "edge_w": by_edge(a["edge_weight"], 0),
        "edge_w1": by_edge(a["edge_weight1"].reshape(-1), 0),
        "l0_w": a["L0_gnn_W"], "lam": a["L1_gnn_lambda_max"], "cheb_w": a["L1_gnn_cheb_W"],
        "cheb_b": a["L1_gnn_cheb_b"], "gat_ws": a["L1_gnn_gat_W_src"], "gat_bs": a["L1_gnn_gat_b_src"],
        "gat_wd": a["L1_gnn_gat_W_dst"], "gat_bd": a["L1_gnn_gat_b_dst"], "gat_attn": a["L1_gnn_gat_attn"],
        "w1": a["L2_gnn_W1"], "w2": a["L2_gnn_W2"],
    }
    nc = bacc.Bacc("TRN2", target_bir_lowering=False, num_devices=1)
    args = [nc.dram_tensor(f"in_{k}", v.shape, mybir.dt.from_np(v.dtype), kind="ExternalInput").ap()
            for k, v in arrays.items()]
    out = nc.dram_tensor("out_x", (P, NJ, D), F32, kind="ExternalOutput").ap()
    gnn_kernel(nc, *args, out)
    r = run(nc, [{f"in_{k}": v for k, v in arrays.items()}], core_ids=[0])
    got = r.results[0]["out_x"]
    return np.ascontiguousarray(got.transpose(1, 0, 2)).reshape(NJ * P, D)[:n_nodes]
```
